# Optimizing a Trainium2 kernel written in Bass

```python
import numpy as np
import jax
import jax.numpy as jnp

def _softmax(x, axis=-1):
    return jax.nn.softmax(x, axis=axis)

def _gelu(x):
    return jax.nn.gelu(x, approximate=True)

def _silu(x):
    return jax.nn.silu(x)

def _sigmoid(x):
    return jax.nn.sigmoid(x)

def _layernorm(x, axis=-1, eps=1e-05):
    m = jnp.mean(x, axis=axis, keepdims=True)
    v = jnp.var(x, axis=axis, keepdims=True)
    return (x - m) / jnp.sqrt(v + eps)

def _scatter_add(tgt, idx, src, axis=0):
    return tgt.at[idx].add(src)

def _segment_sum(src, seg, n):
    return jax.ops.segment_sum(src, seg, n)
kernel_name = 'mk_decoder_postln_d2_seqx_r4_5fcf18'

def setup_inputs(seed: int=0):
    np.random.seed(seed)
    _w = jnp.asarray

    def _rec_inputs():
        import jax
        import jax.numpy as jnp
        _rk = jax.random.key(seed)
        x = -0.0002928 + 1 * jax.random.normal(jax.random.fold_in(_rk, 1), (8, 256, 256), jnp.float32)
        _lenS = 256 - jax.random.randint(jax.random.fold_in(_rk, 7), (8,), 0, max(1, 256 // 4) + 1, jnp.int32)
        _lenS2 = 256 - jax.random.randint(jax.random.fold_in(_rk, 8), (8,), 0, max(1, 256 // 4) + 1, jnp.int32)
        _ctx_1024P = jax.random.normal(jax.random.fold_in(_rk, 11), (8, 16, 256), jnp.float32)
        _ctx_1024c = jax.random.dirichlet(jax.random.fold_in(_rk, 511), 0.3 * jnp.ones((16,), jnp.float32), (8, 256))
        _ctx_1024t = jnp.einsum('bsk,bkd->bsd', _ctx_1024c, _ctx_1024P)
        _ctx_1024t = _ctx_1024t * jax.lax.rsqrt(jnp.mean(jnp.square(_ctx_1024t)) + 1e-12) * 0.953939
        ctx_1024 = -1.39393e-06 + 0.999914 * (_ctx_1024t + 0.3 * jax.random.normal(jax.random.fold_in(_rk, 611), (8, 256, 256), jnp.float32))
        itok_SxS2_0_2016 = jax.random.randint(jax.random.fold_in(_rk, 12), (256, 256), 0, 2017, jnp.int32)
        return (x, ctx_1024, itok_SxS2_0_2016)
    x, ctx_1024, itok_SxS2_0_2016 = _rec_inputs()

    def _L0_attn_setup():
        import jax, jax.numpy as jnp
        import numpy as np
        MODEL_DIM = 256
        NUM_HEADS = 16
        HEAD_DIM = MODEL_DIM // NUM_HEADS
        WINDOW_SIZE = 64
        BATCH = 1
        SEQ_LEN = 1024

        def local_causal_bias(seq_len, window_size, dtype):
            i = jnp.arange(seq_len)[:, None]
            j = jnp.arange(seq_len)[None, :]
            allowed = (j <= i) & (j > i - window_size)
            neg_inf = jnp.array(-jnp.inf, dtype=dtype)
            return jnp.where(allowed, jnp.array(0.0, dtype=dtype), neg_inf)
        key = jax.random.key(seed)
        k_h, k_q, k_k, k_v, k_o = jax.random.split(key, 5)
        s = 1.0 / np.sqrt(MODEL_DIM)
        hidden = jax.random.normal(k_h, (BATCH, SEQ_LEN, MODEL_DIM), dtype=jnp.float32)
        Wq = jax.random.normal(k_q, (MODEL_DIM, MODEL_DIM), dtype=jnp.float32) * s
        Wk = jax.random.normal(k_k, (MODEL_DIM, MODEL_DIM), dtype=jnp.float32) * s
        Wv = jax.random.normal(k_v, (MODEL_DIM, MODEL_DIM), dtype=jnp.float32) * s
        Wo = jax.random.normal(k_o, (MODEL_DIM, MODEL_DIM), dtype=jnp.float32) * s
        return {'hidden': hidden, 'Wq': Wq, 'Wk': Wk, 'Wv': Wv, 'Wo': Wo}
    _L0_attn_all = _L0_attn_setup()
    _L0_attn_in = {k: v for k, v in _L0_attn_all.items() if k in ('Wq', 'Wk', 'Wv', 'Wo')}
    del _L0_attn_all

    def _L0_xattn_setup():
        import jax, jax.numpy as jnp
        import numpy as np
        E = 256
        H = 16
        D = E // H
        B, L, S = (2, 512, 512)
        key = jax.random.key(seed)
        ks = jax.random.split(key, 10)
        scale = 1.0 / np.sqrt(E)
        return {'x': jax.random.normal(ks[0], (B, L, E), jnp.float32), 'context': jax.random.normal(ks[1], (B, S, E), jnp.float32), 'Wq': jax.random.normal(ks[2], (E, E), jnp.float32) * scale, 'bq': jnp.zeros((E,), jnp.float32), 'Wk': jax.random.normal(ks[3], (E, E), jnp.float32) * scale, 'bk': jnp.zeros((E,), jnp.float32), 'Wv': jax.random.normal(ks[4], (E, E), jnp.float32) * scale, 'bv': jnp.zeros((E,), jnp.float32), 'Wp': jax.random.normal(ks[5], (E, E), jnp.float32) * scale, 'bp': jnp.zeros((E,), jnp.float32)}
    _L0_xattn_all = _L0_xattn_setup()
    _L0_xattn_in = {k: v for k, v in _L0_xattn_all.items() if k in ('Wq', 'bq', 'Wk', 'bk', 'Wv', 'bv', 'Wp', 'bp')}
    del _L0_xattn_all

    def _L0_ffn_setup():
        import jax, jax.numpy as jnp
        import numpy as np
        D_MODEL = 256
        D_HIDDEN = 1024
        NUM_EXPERTS = 8
        B, T = (2, 512)
        key = jax.random.key(seed)
        ks = jax.random.split(key, 8)
        s = 0.02
        x = jax.random.normal(ks[0], (B, T, D_MODEL), dtype=jnp.float32)
        Wg = jax.random.normal(ks[1], (D_MODEL, NUM_EXPERTS), dtype=jnp.float32) * s
        bg = jnp.zeros((NUM_EXPERTS,), dtype=jnp.float32)
        W1 = jax.random.normal(ks[2], (NUM_EXPERTS, D_MODEL, D_HIDDEN), dtype=jnp.float32) * s
        b1 = jnp.zeros((NUM_EXPERTS, D_HIDDEN), dtype=jnp.float32)
        W2 = jax.random.normal(ks[3], (NUM_EXPERTS, D_HIDDEN, D_MODEL), dtype=jnp.float32) * s
        b2 = jnp.zeros((NUM_EXPERTS, D_MODEL), dtype=jnp.float32)
        return {'x': x, 'Wg': Wg, 'bg': bg, 'W1': W1, 'b1': b1, 'W2': W2, 'b2': b2}
    _L0_ffn_all = _L0_ffn_setup()
    _L0_ffn_in = {k: v for k, v in _L0_ffn_all.items() if k in ('Wg', 'bg', 'W1', 'b1', 'W2', 'b2')}
    del _L0_ffn_all

    def _L1_attn_setup():
        import jax, jax.numpy as jnp
        import numpy as np
        import math
        HEAD_SIZE = 128

        def rotate_every_two(x):
            x1 = x[..., ::2]
            x2 = x[..., 1::2]
            return jnp.stack((-x2, x1), axis=-1).reshape(x.shape)

        def rope_table(seq_len, dtype=jnp.float32):
            pos = jnp.arange(seq_len, dtype=jnp.float32)
            inv = 10000.0 ** (jnp.arange(0, HEAD_SIZE, 2, dtype=jnp.float32) / HEAD_SIZE)
            radians = pos[:, None] / inv
            sincos = jnp.stack((jnp.sin(radians), jnp.cos(radians)), axis=-1).reshape(seq_len, -1)
            t = jnp.repeat(sincos, 2, axis=-1)
            return t.astype(dtype)
        key = jax.random.key(seed)
        ks = jax.random.split(key, 7)
        B, S, H = (2, 1024, 256)
        sd = 1.0 / math.sqrt(H)
        return {'hidden_states': jax.random.normal(ks[0], (B, S, H), dtype=jnp.float32), 'Wq': jax.random.normal(ks[1], (H, H), dtype=jnp.float32) * sd, 'bq': jax.random.normal(ks[2], (H,), dtype=jnp.float32) * sd, 'Wk': jax.random.normal(ks[3], (H, H), dtype=jnp.float32) * sd, 'bk': jax.random.normal(ks[4], (H,), dtype=jnp.float32) * sd, 'Wv': jax.random.normal(ks[5], (H, H), dtype=jnp.float32) * sd, 'bv': jax.random.normal(ks[6], (H,), dtype=jnp.float32) * sd}
    _L1_attn_all = _L1_attn_setup()
    _L1_attn_in = {k: v for k, v in _L1_attn_all.items() if k in ('Wq', 'bq', 'Wk', 'bk', 'Wv', 'bv')}
    del _L1_attn_all

    def _L1_xattn_setup():
        import jax, jax.numpy as jnp
        import numpy as np
        B, S, DIM, NH = (64, 64, 256, 8)
        DH = DIM // NH
        EPS = 1e-06
        LN_EPS = 1e-05

        def _make_hops(n):
            hops = np.zeros((n, n), dtype=np.int64)
            cur = 1
            for i in range(n):
                for j in range(i + 1, n):
                    hops[i, j] = cur
                    hops[j, i] = cur
                    cur += 1
            return (hops, cur)

        def _mlstm_forward(q, k, v, igate_w, igate_b, fgate_w, fgate_b, rpe, ln_w, ln_b, hops):
            Bq, Sq, _ = q.shape
            pos_emb = rpe[hops]
            gate_in = jnp.concatenate([q, k, v], axis=-1)
            ig = gate_in @ igate_w.T + igate_b
            fg = gate_in @ fgate_w.T + fgate_b
            ig = jnp.transpose(ig, (0, 2, 1))
            fg = jnp.transpose(fg, (0, 2, 1))
            qh = q.reshape(Bq, Sq, NH, DH).transpose(0, 2, 1, 3)
            kh = k.reshape(Bq, Sq, NH, DH).transpose(0, 2, 1, 3)
            vh = v.reshape(Bq, Sq, NH, DH).transpose(0, 2, 1, 3)
            log_f = jax.nn.log_sigmoid(fg)
            csum = jnp.cumsum(log_f, axis=-1)
            csum = jnp.concatenate([jnp.zeros((Bq, NH, 1), csum.dtype), csum], axis=-1)
            lfm = csum[:, :, :, None] - csum[:, :, None, :]
            ltr = jnp.tril(jnp.ones((Sq, Sq), dtype=bool))
            log_fg_matrix = jnp.where(ltr, lfm[:, :, 1:, 1:], -jnp.inf)
            log_D = log_fg_matrix + ig[:, :, None, :]
            max_log_D = jnp.max(log_D, axis=-1, keepdims=True)
            D = jnp.exp(log_D - max_log_D)
            k_scaled = kh / np.sqrt(DH).astype(np.float32)
            pe = pos_emb.reshape(Sq, Sq, NH, DH)
            k_hop = jnp.einsum('bhvc,vmhc->bhvm', qh, pe)
            qk = jnp.einsum('bhsd,bhtd->bhst', qh, k_scaled)
            C = (qk + k_hop) * D
            normalizer = jnp.maximum(jnp.abs(jnp.sum(C, axis=-1, keepdims=True)), jnp.exp(-max_log_D))
            Cn = C / (normalizer + EPS)
            h = Cn @ vh
            mu = jnp.mean(h, axis=-1, keepdims=True)
            var = jnp.mean(jnp.square(h - mu), axis=-1, keepdims=True)
            hn = (h - mu) / jnp.sqrt(var + LN_EPS)
            w = (1.0 + ln_w).reshape(NH, DH)
            b = ln_b.reshape(NH, DH)
            hn = hn * w[None, :, None, :] + b[None, :, None, :]
            return hn.transpose(0, 2, 1, 3).reshape(Bq, Sq, DIM)
        key = jax.random.key(seed)
        ks = jax.random.split(key, 8)
        hops_np, curnum = _make_hops(S)
        return {'q': jax.random.normal(ks[0], (B, S, DIM), dtype=jnp.float32), 'k': jax.random.normal(ks[1], (B, S, DIM), dtype=jnp.float32), 'v': jax.random.normal(ks[2], (B, S, DIM), dtype=jnp.float32), 'igate_w': jax.random.normal(ks[3], (NH, 3 * DIM), dtype=jnp.float32) * 0.02, 'igate_b': jax.random.normal(ks[4], (NH,), dtype=jnp.float32) * 0.1, 'fgate_w': jax.random.normal(ks[5], (NH, 3 * DIM), dtype=jnp.float32) * 0.02, 'fgate_b': jnp.linspace(3.0, 6.0, NH, dtype=jnp.float32), 'rpe': jax.random.normal(ks[6], (curnum, DIM), dtype=jnp.float32) * 0.02, 'ln_w': jax.random.normal(ks[7], (DIM,), dtype=jnp.float32) * 0.1, 'ln_b': jnp.zeros((DIM,), dtype=jnp.float32), 'hops': jnp.asarray(hops_np)}
    _L1_xattn_all = _L1_xattn_setup()
    _L1_xattn_in = {k: v for k, v in _L1_xattn_all.items() if k in ('igate_w', 'igate_b', 'fgate_w', 'fgate_b', 'rpe', 'ln_w', 'ln_b')}
    del _L1_xattn_all

    def _L1_ffn_setup():
        import jax, jax.numpy as jnp
        import numpy as np
        B, S, D, E, H, K = (4, 512, 256, 8, 128, 2)
        key = jax.random.key(seed)
        ks = jax.random.split(key, 11)
        sc = 0.02
        return {'x': jax.random.normal(ks[0], (B, S, D), dtype=jnp.float32), 'gate_W': jax.random.normal(ks[1], (D, E), dtype=jnp.float32) * sc, 'W1': jax.random.normal(ks[2], (E, D, H), dtype=jnp.float32) * sc, 'b1': jnp.zeros((E, H), dtype=jnp.float32), 'W2': jax.random.normal(ks[3], (E, H, D), dtype=jnp.float32) * sc, 'b2': jnp.zeros((E, D), dtype=jnp.float32), 'Ws1': jax.random.normal(ks[4], (D, H), dtype=jnp.float32) * sc, 'bs1': jnp.zeros((H,), dtype=jnp.float32), 'Ws2': jax.random.normal(ks[5], (H, D), dtype=jnp.float32) * sc, 'bs2': jnp.zeros((D,), dtype=jnp.float32), 'route_scale': jnp.ones((), dtype=jnp.float32)}
    _L1_ffn_all = _L1_ffn_setup()
    _L1_ffn_in = {k: v for k, v in _L1_ffn_all.items() if k in ('gate_W', 'W1', 'b1', 'W2', 'b2', 'Ws1', 'bs1', 'Ws2', 'bs2', 'route_scale')}
    del _L1_ffn_all
    return {'x': x, 'ctx_1024': ctx_1024, 'itok_SxS2_0_2016': itok_SxS2_0_2016, 'L0_attn_Wq': _L0_attn_in['Wq'], 'L0_attn_Wk': _L0_attn_in['Wk'], 'L0_attn_Wv': _L0_attn_in['Wv'], 'L0_attn_Wo': _L0_attn_in['Wo'], 'L0_xattn_Wq': _L0_xattn_in['Wq'], 'L0_xattn_bq': _L0_xattn_in['bq'], 'L0_xattn_Wk': _L0_xattn_in['Wk'], 'L0_xattn_bk': _L0_xattn_in['bk'], 'L0_xattn_Wv': _L0_xattn_in['Wv'], 'L0_xattn_bv': _L0_xattn_in['bv'], 'L0_xattn_Wp': _L0_xattn_in['Wp'], 'L0_xattn_bp': _L0_xattn_in['bp'], 'L0_ffn_Wg': _L0_ffn_in['Wg'], 'L0_ffn_bg': _L0_ffn_in['bg'], 'L0_ffn_W1': _L0_ffn_in['W1'], 'L0_ffn_b1': _L0_ffn_in['b1'], 'L0_ffn_W2': _L0_ffn_in['W2'], 'L0_ffn_b2': _L0_ffn_in['b2'], 'L1_attn_Wq': _L1_attn_in['Wq'], 'L1_attn_bq': _L1_attn_in['bq'], 'L1_attn_Wk': _L1_attn_in['Wk'], 'L1_attn_bk': _L1_attn_in['bk'], 'L1_attn_Wv': _L1_attn_in['Wv'], 'L1_attn_bv': _L1_attn_in['bv'], 'L1_xattn_igate_w': _L1_xattn_in['igate_w'], 'L1_xattn_igate_b': _L1_xattn_in['igate_b'], 'L1_xattn_fgate_w': _L1_xattn_in['fgate_w'], 'L1_xattn_fgate_b': _L1_xattn_in['fgate_b'], 'L1_xattn_rpe': _L1_xattn_in['rpe'], 'L1_xattn_ln_w': _L1_xattn_in['ln_w'], 'L1_xattn_ln_b': _L1_xattn_in['ln_b'], 'L1_ffn_gate_W': _L1_ffn_in['gate_W'], 'L1_ffn_W1': _L1_ffn_in['W1'], 'L1_ffn_b1': _L1_ffn_in['b1'], 'L1_ffn_W2': _L1_ffn_in['W2'], 'L1_ffn_b2': _L1_ffn_in['b2'], 'L1_ffn_Ws1': _L1_ffn_in['Ws1'], 'L1_ffn_bs1': _L1_ffn_in['bs1'], 'L1_ffn_Ws2': _L1_ffn_in['Ws2'], 'L1_ffn_bs2': _L1_ffn_in['bs2'], 'L1_ffn_route_scale': _L1_ffn_in['route_scale']}

def reference(x, ctx_1024, itok_SxS2_0_2016, L0_attn_Wq, L0_attn_Wk, L0_attn_Wv, L0_attn_Wo, L0_xattn_Wq, L0_xattn_bq, L0_xattn_Wk, L0_xattn_bk, L0_xattn_Wv, L0_xattn_bv, L0_xattn_Wp, L0_xattn_bp, L0_ffn_Wg, L0_ffn_bg, L0_ffn_W1, L0_ffn_b1, L0_ffn_W2, L0_ffn_b2, L1_attn_Wq, L1_attn_bq, L1_attn_Wk, L1_attn_bk, L1_attn_Wv, L1_attn_bv, L1_xattn_igate_w, L1_xattn_igate_b, L1_xattn_fgate_w, L1_xattn_fgate_b, L1_xattn_rpe, L1_xattn_ln_w, L1_xattn_ln_b, L1_ffn_gate_W, L1_ffn_W1, L1_ffn_b1, L1_ffn_W2, L1_ffn_b2, L1_ffn_Ws1, L1_ffn_bs1, L1_ffn_Ws2, L1_ffn_bs2, L1_ffn_route_scale):
    import jax
    import jax.numpy as jnp

    def _L0_attn_ref(hidden, Wq, Wk, Wv, Wo):
        import jax, jax.numpy as jnp
        import numpy as np
        MODEL_DIM = 256
        NUM_HEADS = 16
        HEAD_DIM = MODEL_DIM // NUM_HEADS
        WINDOW_SIZE = 64
        BATCH = 1
        SEQ_LEN = 1024

        def local_causal_bias(seq_len, window_size, dtype):
            i = jnp.arange(seq_len)[:, None]
            j = jnp.arange(seq_len)[None, :]
            allowed = (j <= i) & (j > i - window_size)
            neg_inf = jnp.array(-jnp.inf, dtype=dtype)
            return jnp.where(allowed, jnp.array(0.0, dtype=dtype), neg_inf)
        B, S, D = hidden.shape

        def proj(x, W):
            y = jnp.einsum('bsd,ed->bse', x, W)
            return y.reshape(B, S, NUM_HEADS, HEAD_DIM).transpose(0, 2, 1, 3)
        q = proj(hidden, Wq)
        k = proj(hidden, Wk)
        v = proj(hidden, Wv)
        scale = 1.0 / np.sqrt(HEAD_DIM)
        bias = local_causal_bias(S, WINDOW_SIZE, hidden.dtype)
        scores = jnp.einsum('bhqd,bhkd->bhqk', q, k) * scale + bias
        attn = jax.nn.softmax(scores, axis=-1)
        out = jnp.einsum('bhqk,bhkd->bhqd', attn, v)
        out = out.transpose(0, 2, 1, 3).reshape(B, S, D)
        return jnp.einsum('bsd,ed->bse', out, Wo)

    def _L0_xattn_ref(x, context, Wq, bq, Wk, bk, Wv, bv, Wp, bp):
        import jax, jax.numpy as jnp
        import numpy as np
        E = 256
        H = 16
        D = E // H
        B, L, S = (2, 512, 512)
        b, l, _ = x.shape
        s = context.shape[1]
        q = (x @ Wq + bq).reshape(b, l, H, D).transpose(0, 2, 1, 3)
        k = (context @ Wk + bk).reshape(b, s, H, D).transpose(0, 2, 1, 3)
        v = (context @ Wv + bv).reshape(b, s, H, D).transpose(0, 2, 1, 3)
        attn = jnp.einsum('bhld,bhsd->bhls', q, k) / jnp.sqrt(jnp.float32(D))
        attn = jax.nn.softmax(attn, axis=-1)
        out = jnp.einsum('bhls,bhsd->bhld', attn, v)
        out = out.transpose(0, 2, 1, 3).reshape(b, l, E)
        return out @ Wp + bp

    def _L0_ffn_ref(x, Wg, bg, W1, b1, W2, b2):
        import jax, jax.numpy as jnp
        import numpy as np
        D_MODEL = 256
        D_HIDDEN = 1024
        NUM_EXPERTS = 8
        B, T = (2, 512)
        gate_logits = jnp.einsum('btd,de->bte', x, Wg) + bg
        gate_scores = jax.nn.softmax(gate_logits, axis=-1)
        top1_idx = jnp.argmax(gate_scores, axis=-1)
        top1_mask = jax.nn.one_hot(top1_idx, NUM_EXPERTS, dtype=x.dtype)
        top1_weight = jnp.sum(gate_scores * top1_mask, axis=-1, keepdims=True)
        h = jax.nn.silu(jnp.einsum('btd,edh->bteh', x, W1) + b1)
        o = jnp.einsum('bteh,ehd->bted', h, W2) + b2
        y = jnp.sum(o * top1_mask[..., None], axis=2) * top1_weight
        return y

    def _L1_attn_ref(hidden_states, Wq, bq, Wk, bk, Wv, bv):
        import jax, jax.numpy as jnp
        import numpy as np
        import math
        HEAD_SIZE = 128

        def rotate_every_two(x):
            x1 = x[..., ::2]
            x2 = x[..., 1::2]
            return jnp.stack((-x2, x1), axis=-1).reshape(x.shape)

        def rope_table(seq_len, dtype=jnp.float32):
            pos = jnp.arange(seq_len, dtype=jnp.float32)
            inv = 10000.0 ** (jnp.arange(0, HEAD_SIZE, 2, dtype=jnp.float32) / HEAD_SIZE)
            radians = pos[:, None] / inv
            sincos = jnp.stack((jnp.sin(radians), jnp.cos(radians)), axis=-1).reshape(seq_len, -1)
            t = jnp.repeat(sincos, 2, axis=-1)
            return t.astype(dtype)
        B, S, H = hidden_states.shape
        t = rope_table(S, hidden_states.dtype)
        q = hidden_states @ Wq.T + bq
        k = hidden_states @ Wk.T + bk
        v = hidden_states @ Wv.T + bv
        q = q * t + rotate_every_two(q) * t
        k = k * t + rotate_every_two(k) * t
        scale = math.sqrt(HEAD_SIZE)
        scores = jnp.einsum('bsh,bth->bst', q, k) / scale
        probs = jax.nn.softmax(scores, axis=-1)
        out = jnp.einsum('bst,bth->bsh', probs, v)
        return out

    def _L1_xattn_ref(q, k, v, igate_w, igate_b, fgate_w, fgate_b, rpe, ln_w, ln_b, hops):
        import jax, jax.numpy as jnp
        import numpy as np
        B, S, DIM, NH = (64, 64, 256, 8)
        DH = DIM // NH
        EPS = 1e-06
        LN_EPS = 1e-05

        def _make_hops(n):
            hops = np.zeros((n, n), dtype=np.int64)
            cur = 1
            for i in range(n):
                for j in range(i + 1, n):
                    hops[i, j] = cur
                    hops[j, i] = cur
                    cur += 1
            return (hops, cur)

        def _mlstm_forward(q, k, v, igate_w, igate_b, fgate_w, fgate_b, rpe, ln_w, ln_b, hops):
            Bq, Sq, _ = q.shape
            pos_emb = rpe[hops]
            gate_in = jnp.concatenate([q, k, v], axis=-1)
            ig = gate_in @ igate_w.T + igate_b
            fg = gate_in @ fgate_w.T + fgate_b
            ig = jnp.transpose(ig, (0, 2, 1))
            fg = jnp.transpose(fg, (0, 2, 1))
            qh = q.reshape(Bq, Sq, NH, DH).transpose(0, 2, 1, 3)
            kh = k.reshape(Bq, Sq, NH, DH).transpose(0, 2, 1, 3)
            vh = v.reshape(Bq, Sq, NH, DH).transpose(0, 2, 1, 3)
            log_f = jax.nn.log_sigmoid(fg)
            csum = jnp.cumsum(log_f, axis=-1)
            csum = jnp.concatenate([jnp.zeros((Bq, NH, 1), csum.dtype), csum], axis=-1)
            lfm = csum[:, :, :, None] - csum[:, :, None, :]
            ltr = jnp.tril(jnp.ones((Sq, Sq), dtype=bool))
            log_fg_matrix = jnp.where(ltr, lfm[:, :, 1:, 1:], -jnp.inf)
            log_D = log_fg_matrix + ig[:, :, None, :]
            max_log_D = jnp.max(log_D, axis=-1, keepdims=True)
            D = jnp.exp(log_D - max_log_D)
            k_scaled = kh / np.sqrt(DH).astype(np.float32)
            pe = pos_emb.reshape(Sq, Sq, NH, DH)
            k_hop = jnp.einsum('bhvc,vmhc->bhvm', qh, pe)
            qk = jnp.einsum('bhsd,bhtd->bhst', qh, k_scaled)
            C = (qk + k_hop) * D
            normalizer = jnp.maximum(jnp.abs(jnp.sum(C, axis=-1, keepdims=True)), jnp.exp(-max_log_D))
            Cn = C / (normalizer + EPS)
            h = Cn @ vh
            mu = jnp.mean(h, axis=-1, keepdims=True)
            var = jnp.mean(jnp.square(h - mu), axis=-1, keepdims=True)
            hn = (h - mu) / jnp.sqrt(var + LN_EPS)
            w = (1.0 + ln_w).reshape(NH, DH)
            b = ln_b.reshape(NH, DH)
            hn = hn * w[None, :, None, :] + b[None, :, None, :]
            return hn.transpose(0, 2, 1, 3).reshape(Bq, Sq, DIM)
        return _mlstm_forward(q, k, v, igate_w, igate_b, fgate_w, fgate_b, rpe, ln_w, ln_b, hops)

    def _L1_ffn_ref(x, gate_W, W1, b1, W2, b2, Ws1, bs1, Ws2, bs2, route_scale):
        import jax, jax.numpy as jnp
        import numpy as np
        B, S, D, E, H, K = (4, 512, 256, 8, 128, 2)
        scores = jax.nn.sigmoid(x @ gate_W) * route_scale
        topk_scores, topk_idx = jax.lax.top_k(scores, K)
        topk_w = topk_scores / topk_scores.sum(-1, keepdims=True)
        onehot = jax.nn.one_hot(topk_idx, E, dtype=x.dtype)
        gate_full = jnp.einsum('bsk,bske->bse', topk_w, onehot)
        h = jax.nn.gelu(jnp.einsum('bsd,edh->bseh', x, W1) + b1, approximate=False)
        y = jnp.einsum('bseh,ehd->bsed', h, W2) + b2
        expert_out = jnp.einsum('bse,bsed->bsd', gate_full, y)
        shared = jax.nn.gelu(x @ Ws1 + bs1, approximate=False) @ Ws2 + bs2
        return expert_out + shared
    x = _layernorm(x + _L0_attn_ref(x, L0_attn_Wq, L0_attn_Wk, L0_attn_Wv, L0_attn_Wo), axis=-1)
    x = _layernorm(x + _L0_xattn_ref(x, ctx_1024, L0_xattn_Wq, L0_xattn_bq, L0_xattn_Wk, L0_xattn_bk, L0_xattn_Wv, L0_xattn_bv, L0_xattn_Wp, L0_xattn_bp), axis=-1)
    x = _layernorm(x + _L0_ffn_ref(x, L0_ffn_Wg, L0_ffn_bg, L0_ffn_W1, L0_ffn_b1, L0_ffn_W2, L0_ffn_b2), axis=-1)
    x = _layernorm(x + _L1_attn_ref(x, L1_attn_Wq, L1_attn_bq, L1_attn_Wk, L1_attn_bk, L1_attn_Wv, L1_attn_bv), axis=-1)
    x = _layernorm(x + _L1_xattn_ref(x, ctx_1024, ctx_1024, L1_xattn_igate_w, L1_xattn_igate_b, L1_xattn_fgate_w, L1_xattn_fgate_b, L1_xattn_rpe, L1_xattn_ln_w, L1_xattn_ln_b, itok_SxS2_0_2016), axis=-1)
    x = _layernorm(x + _L1_ffn_ref(x, L1_ffn_gate_W, L1_ffn_W1, L1_ffn_b1, L1_ffn_W2, L1_ffn_b2, L1_ffn_Ws1, L1_ffn_bs1, L1_ffn_Ws2, L1_ffn_bs2, L1_ffn_route_scale), axis=-1)
    return x

_drawn_inputs = setup_inputs


def setup_inputs(seed=0):
    import zlib

    import numpy as np

    out = dict(_drawn_inputs(seed))
    spreads = {'L0_xattn_bq': (0.0, 0.1),
     'L0_xattn_bk': (0.0, 2.0),
     'L0_xattn_bv': (0.0, 0.1),
     'L0_xattn_bp': (0.0, 0.1),
     'L0_ffn_bg': (0.0, 0.453),
     'L0_ffn_b1': (0.0, 0.729),
     'L0_ffn_b2': (0.0, 0.332),
     'L1_xattn_ln_b': (0.0, 0.1),
     'L1_ffn_b1': (0.0, 0.8),
     'L1_ffn_b2': (0.0, 0.1),
     'L1_ffn_bs1': (0.0, 0.68),
     'L1_ffn_bs2': (0.0, 0.1)}
    factors = {'L1_attn_bq': 3.658, 'L1_attn_bk': 5.555, 'L1_xattn_igate_b': 64.0}
    for name, (base, spread) in spreads.items():
        noise = np.random.default_rng([zlib.crc32(name.encode()), seed]).standard_normal(out[name].shape)
        drawn = base * np.exp(spread * noise) if base else spread * noise
        out[name] = jnp.asarray(drawn.astype(out[name].dtype))
    for name, factor in factors.items():
        out[name] = (out[name] * factor).astype(out[name].dtype)
    return out
```

```python
from contextlib import ExitStack

import numpy as np

import concourse.bass as bass
from concourse import mybir

ALU = mybir.AluOpType
ACT = mybir.ActivationFunctionType
AX = mybir.AxisListType
F32 = mybir.dt.float32
BF16 = mybir.dt.bfloat16
I32 = mybir.dt.int32
U32 = mybir.dt.uint32

P = 128
B = 8
S = 256
D = 256
KT = D // P
QT = S // P
NH = 16
HD = D // NH
WINDOW = 64
LN_EPS = 1e-5
NEG = -1.0e30

WQ0, WK0, WV0, WO0, XQ, XK, XV, XP, WQ1, WK1, WV1 = range(11)
C_BQ, C_BK, C_B1Q, C_B1K, C_MASK = range(5)
R_BV, R_BP, R_B1V, R_LNW, R_LNB, R_BS2 = range(6)


class Count:

    def __init__(self, engine, sem, per_pass, base):
        self.engine, self.sem, self.per_pass, self.base, self.n = engine, sem, per_pass, base, 0

    def link(self, ins):
        ins.then_inc(self.sem, 1)
        self.n += 1
        self.engine.wait_ge(self.sem, self.base + self.n)

    def end(self):
        assert self.n == self.per_pass, self.n


def phase_semaphores(nc, ctx, prefix):
    made = []

    def sem(name):
        made.append(nc.alloc_semaphore(prefix + name))
        return made[-1]

    def clear():
        nc.clear_and_free_semaphores(made)
        nc.all_engine_barrier(sem_only=True)

    ctx.callback(clear)
    return sem


def units():
    out = []
    for g in range(4):
        out.append(dict(layer=0, qt=0, g=g, heads=[(t, par) for t in range(2) for par in range(2)], k0=0, nk=128))
    for t in range(2):
        for g in range(4):
            out.append(dict(layer=0, qt=1, g=g, heads=[(t, 0), (t, 1)], k0=64, nk=192))
    for qt in range(QT):
        for t in range(2):
            for g in range(4):
                out.append(dict(layer=1, qt=qt, g=g, heads=[(t, 0), (t, 1)], k0=0, nk=256))
    return out


UNITS = units()
NU = len(UNITS)
NU0 = 12
LAST_OF = {0: NU0 - 1, 1: NU - 1}
ON_ACT = [u for u in range(NU) if u % 4 == 3]
STEPS = 11


def head_of(t, g, par):
    return 8 * t + 2 * g + par


def layer0_attention(nc, dram, pool_share):
    with ExitStack() as ctx:
        def sb(name, shape, dt=F32):
            return ctx.enter_context(nc.sbuf_tensor("a_" + name, shape, dt))

        sem = phase_semaphores(nc, ctx, "a_")

        w = sb("w", [P, 8, KT, D])
        cols = sb("cols", [P, 5, 2])
        rows = sb("rows", [P, 2, D])
        ident = sb("ident", [P, P])
        identb = sb("identb", [P, P], BF16)
        mask0 = sb("mask0", [P, 4, 128], BF16)
        mask1 = sb("mask1", [P, 2, 192], BF16)
        maskf = sb("maskf", [P, 4 * 128 + 2 * 192])
        eps = sb("eps", [P, 1])
        xT = sb("xT", [P, KT, S])
        cT = sb("cT", [P, KT, S])
        xin = sb("xin", [P, QT, D])
        kT = [sb(f"kT{i}", [P, 2, S]) for i in range(2)]
        qT = [[sb(f"qT{i}{j}", [P, 2, S]) for j in range(2)] for i in range(2)]
        v = [sb(f"v{i}", [P, QT, D]) for i in range(2)]
        probs = [sb(f"probs{i}", [P, 512]) for i in range(2)]
        probs_w = [sb(f"probs_w{i}", [P, 2, 256]) for i in range(2)]
        probsT = [sb(f"probsT{i}", [P, 4, P]) for i in range(2)]
        negmax = sb("negmax", [P, 4, 4])
        rsum = sb("rsum", [P, QT, NH])
        rinv = sb("rinv", [P, QT, NH])
        o = sb("o", [P, QT, D])
        oT = sb("oT", [P, KT, S])
        y = sb("y", [P, QT, D])
        x1 = sb("x1", [P, QT, D])
        x1T = sb("x1T", [P, KT, S])
        x2 = sb("x2", [P, QT, D])
        st = sb("st", [P, QT, 6])
        mv = sb("mv", [P, QT, 2])
        lnv = sb("lnv", [P, QT])
        rstd = sb("rstd", [P, QT])
        sc = [ctx.enter_context(nc.psum_tensor(f"a_sc{i}", [P, 512], F32)) for i in range(4)]
        pt = [ctx.enter_context(nc.psum_tensor(f"a_pt{i}", [P, 512], F32)) for i in range(2)]
        op = ctx.enter_context(nc.psum_tensor("a_op", [P, 512], F32))
        mi = ctx.enter_context(nc.psum_tensor("a_mi", [P, 2, 256], F32))

        zeros = sb("zeros", [P, TILES * D // 4])
        s_zeroed = sem("zeroed")
        s_const = sem("const")
        s_maskb = sem("maskb")
        s_zero = sem("zero")
        s_xT = sem("xT")
        s_xin = sem("xin")
        s_cT = sem("cT")
        s_step = sem("step")
        s_copied = sem("copied")
        s_scores = sem("scores")
        s_max = sem("max")
        s_exp = sem("exp")
        s_turned = sem("turned")
        s_evac_dve = sem("evac_dve")
        s_evac_act = sem("evac_act")
        s_pv = sem("pv")
        s_onorm = sem("onorm")
        s_stats = sem("stats")
        s_rstd = sem("rstd")
        s_x1 = sem("x1")
        s_x2 = sem("x2")
        s_x2_out = sem("x2_out")
        s_x2_free = sem("x2_free")
        s_dve = sem("dve")
        s_act = sem("act")
        block = ctx.enter_context(nc.Block())

        n_act, n_dve = len(ON_ACT), NU - len(ON_ACT)

        def wait_evac(eng, b, u):
            if u in ON_ACT:
                eng.wait_ge(s_evac_act, b * n_act + ON_ACT.index(u) + 1)
            else:
                before = len([x for x in range(u) if x not in ON_ACT])
                eng.wait_ge(s_evac_dve, b * n_dve + before + 1)

        @block.sync
        def _(sp):
            sp.dma_start(ident[:], dram["ident"]).then_inc(s_const, 16)
            sp.dma_start(w[:, 0:4], dram["w"][:, 0:4]).then_inc(s_const, 16)
            sp.dma_start(cols[:], dram["cols"]).then_inc(s_const, 16)
            sp.dma_start(xT[:], dram["xT"][0]).then_inc(s_xT, 16)
            sp.dma_start(maskf[:], dram["masks"]).then_inc(s_const, 16)
            sp.dma_start(xin[:], dram["x"][0].rearrange("(t p) d -> p t d", p=P)).then_inc(s_xin, 16)
            sp.dma_start(w[:, 4:8], dram["w"][:, 4:8]).then_inc(s_const, 16)
            sp.dma_start(rows[:], dram["rows"][:, 0:2]).then_inc(s_const, 16)
            sp.dma_start(cT[:], dram["cT"][0]).then_inc(s_cT, 16)
            sp.wait_ge(s_zero, 1)
            for i in range(4):
                sp.dma_start(dram["xs"].rearrange("(p r) d -> p (r d)", p=P)[:, i * zeros.shape[1]:(i + 1) * zeros.shape[1]],
                             zeros[:]).then_inc(s_zeroed, 16)

            def store(b):
                sp.wait_ge(s_x2, b + 1)
                sp.dma_start(dram["x2"][bass.ds(b, 1)].rearrange("b (t p) d -> p (b t) d", p=P),
                             x2[:]).then_inc(s_x2_out, 16)

            with sp.Fori(0, B - 1) as b:
                sp.wait_ge(s_step, b * STEPS + 3)
                sp.dma_start(xT[:], dram["xT"][bass.ds(b + 1, 1)].rearrange("b p k s -> p (b k) s"))\
                    .then_inc(s_xT, 16)
                sp.wait_ge(s_copied, b * STEPS + 6)
                sp.dma_start(xin[:], dram["x"][bass.ds(b + 1, 1)].rearrange("b (t p) d -> p (b t) d", p=P))\
                    .then_inc(s_xin, 16)
                sp.wait_ge(s_step, b * STEPS + 7)
                sp.dma_start(cT[:], dram["cT"][bass.ds(b + 1, 1)].rearrange("b p k s -> p (b k) s"))\
                    .then_inc(s_cT, 16)
                store(b)
                sp.wait_ge(s_x2_out, 16 * b + 16)
                sp.sem_inc(s_x2_free, 1)
            store(B - 1)
            sp.wait_ge(s_x2_out, 16 * B)
            sp.wait_ge(s_zeroed, 64)

        @block.gpsimd
        def _(pool):
            pool.memset(zeros[:], 0.0).then_inc(s_zero, 1)
            for i in range(2):
                pool.memset(probs_w[i][:, :, 0:64], 0.0).then_inc(s_zero, 1)
            pool_share(pool)

        @block.scalar
        def _(act):
            act.preload_act_table_set("natural_log_exp_and_others")
            act.wait_ge(s_zero, 3)

            def exps(b, u):
                un = UNITS[u]
                act.wait_ge(s_max, b * NU + u + 1)
                if u >= 2:
                    act.wait_ge(s_turned, b * NU + u - 1)
                for j, (t, par) in enumerate(un["heads"]):
                    h = head_of(t, un["g"], par)
                    if un["layer"] == 0 and un["qt"] == 1:
                        dst = probs_w[u % 2][:, j, 64:256]
                    else:
                        dst = probs[u % 2][:, j * un["nk"]:(j + 1) * un["nk"]]
                    ins = act.activation(dst, sc[u % 4][:, j * un["nk"]:(j + 1) * un["nk"]], ACT.Exp,
                                         bias=negmax[:, u % 4, j:j + 1],
                                         accum_out=rsum[:, un["qt"], h:h + 1])
                ins.then_inc(s_exp, 1)

            def evac(b, u):
                act.wait_ge(s_turned, b * NU + u + 1)
                if u >= 2:
                    act.wait_ge(s_pv, b * NU + u - 1)
                act.copy(probsT[u % 2][:], pt[u % 2][:]).then_inc(s_evac_act, 1)

            def layer(b, us):
                for u in list(us) + [None]:
                    if u is not None:
                        exps(b, u)
                    before = us[-1] if u is None else u - 1
                    if before in ON_ACT and before >= us[0]:
                        evac(b, before)

            def step(b, n):
                act.wait_ge(s_step, b * STEPS + n + 1)

            def rsqrt(b, n):
                act.wait_ge(s_stats, 2 * b + n + 1)
                act.activation(lnv[:], mv[:, :, 1], ACT.Ln, bias=eps[:]).then_inc(s_act, 1)
                act.wait_ge(s_act, 2 * b + n + 1)
                act.activation(rstd[:], lnv[:], ACT.Exp, scale=-0.5).then_inc(s_rstd, 1)

            with act.Fori(0, B) as b:
                step(b, 0)
                act.copy(kT[0][:], mi[:]).then_inc(s_copied, 1)
                step(b, 2)
                act.copy(v[0][:], mi[:]).then_inc(s_copied, 1)
                layer(b, range(NU0))
                step(b, 3)
                act.copy(oT[:], mi[:]).then_inc(s_copied, 1)
                step(b, 5)
                act.activation(kT[1][:, 0], mi[:, 0], ACT.Identity, bias=cols[:, C_BK, 0:1])
                act.activation(kT[1][:, 1], mi[:, 1], ACT.Identity, bias=cols[:, C_BK, 1:2])\
                    .then_inc(s_copied, 1)
                rsqrt(b, 0)
                step(b, 7)
                act.copy(x1T[:], mi[:]).then_inc(s_copied, 1)
                layer(b, range(NU0, NU))
                step(b, 9)
                act.copy(oT[:], mi[:]).then_inc(s_copied, 1)
                rsqrt(b, 1)

        @block.tensor
        def _(pe):
            pe.wait_ge(s_const, 16 * 6)
            pe.wait_ge(s_maskb, 4)

            def free(b, n):
                pe.wait_ge(s_copied, b * STEPS + n + 1)

            def project_T(b, n, wi, src):
                free(b, n)
                for et in range(2):
                    for k in range(KT):
                        ins = pe.matmul(mi[:, et], w[:, wi, k, et * P:(et + 1) * P], src[:, k, :],
                                        start=(k == 0), stop=(k == KT - 1))
                ins.then_inc(s_step, 1)

            def project(b, n, wi, srcT):
                free(b, n)
                for qt in range(QT):
                    for k in range(KT):
                        ins = pe.matmul(mi[:, qt], srcT[:, k, qt * P:(qt + 1) * P], w[:, wi, k, :],
                                        start=(k == 0), stop=(k == KT - 1))
                ins.then_inc(s_step, 1)

            def turn(b, n, src):
                free(b, n)
                for k in range(KT):
                    for qt in range(QT):
                        ins = pe.transpose(mi[:, k, qt * P:(qt + 1) * P], src[:, qt, k * P:(k + 1) * P], ident[:])
                ins.then_inc(s_step, 1)

            def scores(b, u):
                un = UNITS[u]
                L, g, nk, qt = un["layer"], un["g"], un["nk"], un["qt"]
                bank = sc[u % 4]
                if u >= 4:
                    pe.wait_ge(s_exp, b * NU + u - 3)
                if L == 0:
                    mask = mask0 if qt == 0 else mask1
                    width = len(un["heads"]) * nk
                    pe.matmul(bank[:, 0:width], identb[:], mask[:].rearrange("p h k -> p (h k)"),
                              start=True, stop=True, skip_group_check=True)
                for j, (t, par) in enumerate(un["heads"]):
                    ins = pe.matmul(bank[:, j * nk:(j + 1) * nk],
                                    qT[L][par][32 * g:32 * g + 32, t, qt * P:(qt + 1) * P],
                                    kT[L][32 * g:32 * g + 32, t, un["k0"]:un["k0"] + nk],
                                    start=(L == 1), stop=True,
                                    skip_group_check=True)
                ins.then_inc(s_scores, 1)

            def transposes(b, u):
                un = UNITS[u]
                pe.wait_ge(s_exp, b * NU + u + 1)
                if u >= 2:
                    wait_evac(pe, b, u - 2)
                if un["layer"] == 0 and un["qt"] == 1:
                    src = probs_w[u % 2][:].rearrange("p h k -> p (h k)")
                else:
                    src = probs[u % 2][:]
                for c in range(4):
                    ins = pe.transpose(pt[u % 2][:, c * P:(c + 1) * P], src[:, c * P:(c + 1) * P], ident[:])
                ins.then_inc(s_turned, 1)

            def pv(b, u):
                un = UNITS[u]
                wait_evac(pe, b, u)
                nc_ = 1 if un["nk"] == 128 else 2
                for j, (t, par) in enumerate(un["heads"]):
                    h = head_of(t, un["g"], par)
                    at = un["qt"] * D + h * HD
                    for c in range(nc_):
                        ins = pe.matmul(op[:, at:at + HD], probsT[u % 2][:, j * nc_ + c, :],
                                        v[un["layer"]][:, c, h * HD:(h + 1) * HD],
                                        start=(c == 0), stop=(c == nc_ - 1), skip_group_check=True)
                ins.then_inc(s_pv, 1)

            def layer(b, us):
                n = len(us)
                for i in range(3):
                    scores(b, us[i])
                for i in range(n + 2):
                    if i + 3 < n:
                        scores(b, us[i + 3])
                    if i < n:
                        transposes(b, us[i])
                    if i >= 2:
                        pv(b, us[i - 2])

            with pe.Fori(0, B) as b:
                pe.wait_ge(s_xT, 16 * b + 16)
                project_T(b, 0, WK0, xT)
                project_T(b, 1, WQ0, xT)
                project(b, 2, WV0, xT)
                free(b, 3)
                layer(b, range(NU0))
                pe.wait_ge(s_onorm, 2 * b + 1)
                turn(b, 3, o)
                free(b, 4)
                project(b, 4, WO0, oT)
                pe.wait_ge(s_cT, 16 * b + 16)
                project_T(b, 5, XK, cT)
                project(b, 6, XV, cT)
                pe.wait_ge(s_x1, b + 1)
                turn(b, 7, x1)
                free(b, 8)
                project_T(b, 8, XQ, x1T)
                free(b, 9)
                layer(b, range(NU0, NU))
                pe.wait_ge(s_onorm, 2 * b + 2)
                turn(b, 9, o)
                free(b, 10)
                project(b, 10, XP, oT)

        @block.vector
        def _(dve):
            dve.memset(eps[:], LN_EPS).then_inc(s_maskb, 1)
            dve.sem_inc(s_copied, 1)
            dve.sem_inc(s_x2_free, 1)
            dve.wait_ge(s_const, 16 * 6)
            dve.tensor_copy(mask0[:].rearrange("p h k -> p (h k)"), maskf[:, 0:512]).then_inc(s_maskb, 1)
            dve.tensor_copy(mask1[:].rearrange("p h k -> p (h k)"), maskf[:, 512:896]).then_inc(s_maskb, 1)
            dve.tensor_copy(identb[:], ident[:]).then_inc(s_maskb, 1)

            def row_max(b, u):
                un = UNITS[u]
                n = len(un["heads"])
                dve.wait_ge(s_scores, b * NU + u + 1)
                dve.tensor_reduce(negmax[:, u % 4, 0:n],
                                  sc[u % 4][:, 0:n * un["nk"]].rearrange("p (h k) -> p h k", h=n),
                                  AX.X, ALU.max, negate=True).then_inc(s_max, 1)

            def evac(b, u):
                dve.wait_ge(s_turned, b * NU + u + 1)
                if u >= 2:
                    dve.wait_ge(s_pv, b * NU + u - 1)
                dve.tensor_copy(probsT[u % 2][:].rearrange("p h k -> p (h k)"), pt[u % 2][:])\
                    .then_inc(s_evac_dve, 1)

            def layer(b, us):
                n = len(us)
                for i in range(n + 2):
                    if i < n:
                        row_max(b, us[i])
                    if i >= 2 and us[i - 2] not in ON_ACT:
                        evac(b, us[i - 2])

            def normalise(b, L, chain):
                dve.wait_ge(s_exp, b * NU + LAST_OF[L] + 1)
                chain.link(dve.reciprocal(rinv[:], rsum[:]))
                dve.wait_ge(s_pv, b * NU + LAST_OF[L] + 1)
                dve.tensor_tensor(o[:].rearrange("p t (h d) -> p (t h) d", d=HD),
                                  op[:].rearrange("p (h d) -> p h d", d=HD),
                                  rinv[:].rearrange("p t h -> p (t h)").unsqueeze(2).broadcast_to([P, QT * NH, HD]),
                                  ALU.mult).then_inc(s_onorm, 1)

            def statistics(b, n, chain):
                dve.bn_stats(st[:, 0], y[:, 0])
                chain.link(dve.bn_stats(st[:, 1], y[:, 1]))
                dve.nop(nofuse=True)
                dve.bn_aggr(mv[:, 0], st[:, 0])
                dve.bn_aggr(mv[:, 1], st[:, 1]).then_inc(s_stats, 1)

            def scaled(b, n, dst, done):
                dve.wait_ge(s_rstd, 2 * b + n + 1)
                dve.wait_ge(s_stats, 2 * b + n + 1)
                for qt in range(QT):
                    ins = dve.tensor_scalar(dst[:, qt], y[:, qt], mv[:, qt, 0:1], rstd[:, qt:qt + 1],
                                            ALU.subtract, ALU.mult)
                ins.then_inc(done, 1)

            with dve.Fori(0, B) as b:
                chain = Count(dve, s_dve, 5, b * 5)
                dve.wait_ge(s_step, b * STEPS + 2)
                dve.tensor_scalar(qT[0][0][:], mi[:], cols[:, C_MASK, 0:1], None, ALU.mult)
                dve.tensor_scalar(qT[0][1][:], mi[:], cols[:, C_MASK, 1:2], None, ALU.mult).then_inc(s_copied, 1)
                layer(b, range(NU0))
                normalise(b, 0, chain)
                dve.wait_ge(s_step, b * STEPS + 5)
                dve.wait_ge(s_xin, 16 * b + 16)
                dve.tensor_tensor(y[:], mi[:], xin[:], ALU.add).then_inc(s_copied, 1)
                dve.wait_ge(s_copied, b * STEPS + 6)
                statistics(b, 0, chain)
                dve.wait_ge(s_step, b * STEPS + 7)
                dve.tensor_tensor(v[1][:], mi[:], rows[:, 0].unsqueeze(1).broadcast_to([P, QT, D]), ALU.add)\
                    .then_inc(s_copied, 1)
                scaled(b, 0, x1, s_x1)
                dve.wait_ge(s_step, b * STEPS + 9)
                for et in range(2):
                    for par in range(2):
                        ins = dve.tensor_scalar(qT[1][par][:, et], mi[:, et], cols[:, C_BQ, et:et + 1],
                                                cols[:, C_MASK, par:par + 1], ALU.add, ALU.mult)
                ins.then_inc(s_copied, 1)
                layer(b, range(NU0, NU))
                normalise(b, 1, chain)
                chain.link(dve.tensor_tensor(x1[:], x1[:], rows[:, 1].unsqueeze(1).broadcast_to([P, QT, D]), ALU.add))
                dve.wait_ge(s_step, b * STEPS + 11)
                dve.tensor_tensor(y[:], mi[:], x1[:], ALU.add).then_inc(s_copied, 1)
                dve.wait_ge(s_copied, b * STEPS + 12)
                statistics(b, 1, chain)
                dve.wait_ge(s_x2_free, b + 1)
                scaled(b, 1, x2, s_x2)
                chain.end()


GROUP = 4
UNITS_R = P + 2 * P
GROUPS = UNITS_R // GROUP


class TableRows:

    def __init__(self, nc, ctx, dram):
        self.nc, self.dram = nc, dram
        self.idx = ctx.enter_context(nc.sbuf_tensor("r_idx", [P, UNITS_R], I32))
        self.cur = [ctx.enter_context(nc.sbuf_tensor(f"r_cur{i}", [P, GROUP], I32)) for i in range(2)]
        self.buf = [ctx.enter_context(nc.sbuf_tensor(f"r_buf{i}", [P, GROUP, D], F32)) for i in range(2)]
        self.s_idx = ctx.enter_context(nc.semaphore("r_idx_loaded"))
        self.s_cur = [ctx.enter_context(nc.semaphore(f"r_cur_ready{i}")) for i in range(2)]
        self.s_got = [ctx.enter_context(nc.semaphore(f"r_got{i}")) for i in range(2)]
        self.s_sent = [ctx.enter_context(nc.semaphore(f"r_sent{i}")) for i in range(2)]

    def start(self, pool):
        pool.dma_start(self.idx[:], self.dram["hopsT"]).then_inc(self.s_idx, 16)
        pool.wait_ge(self.s_idx, 16)

    def group(self, pool, g, i, first=False):
        turn = g // 2
        if not first:
            pool.wait_ge(self.s_sent[i], turn * 16)
        pool.tensor_copy(self.cur[i][:], self.idx[:, bass.ds(g * GROUP, GROUP)]).then_inc(self.s_cur[i], 1)
        pool.wait_ge(self.s_cur[i], turn + 1)
        pool.nop(nofuse=True)
        for j in range(GROUP):
            pool.indirect_dma_start(
                out=self.buf[i][:, j, :], out_offset=None, in_=self.dram["rpe"],
                in_offset=bass.IndirectOffsetOnAxis(ap=self.cur[i][:, j:j + 1], axis=0))\
                .then_inc(self.s_got[i], 16)

    def send(self, pool, g, i):
        pool.wait_ge(self.s_got[i], (g // 2 + 1) * 16 * GROUP)
        pool.dma_start(self.dram["pos_rows"][bass.ds(g, 1)].rearrange("g p n -> p (g n)"),
                       self.buf[i][:].rearrange("p j d -> p (j d)")).then_inc(self.s_sent[i], 16)

    def share(self, first, last):
        def run(pool):
            lo = first
            if first == 0:
                self.start(pool)
                self.group(pool, 0, 0, True)
                self.group(pool, 1, 1, True)
                self.send(pool, 0, 0)
                self.send(pool, 1, 1)
                lo = 1
            with pool.Fori(lo, last) as t:
                self.group(pool, 2 * t, 0)
                self.group(pool, 2 * t + 1, 1)
                self.send(pool, 2 * t, 0)
                self.send(pool, 2 * t + 1, 1)
        return run


NE = 8
HID = 1024
HT = HID // P
TT = B * QT
TILES = TT + NE - 1
NEG_BIG = 1.0e30


def first_max_onehot(dve, link, lg, mx, t8, low, onehot, iota8m):
    shape = [P, TT, NE]
    link(dve.tensor_reduce(mx, lg, AX.X, ALU.max))
    link(dve.tensor_tensor(t8, lg, mx.unsqueeze(2).broadcast_to(shape), ALU.is_equal))
    link(dve.tensor_tensor(t8, t8, iota8m, ALU.mult))
    link(dve.tensor_reduce(low, t8, AX.X, ALU.min))
    link(dve.tensor_tensor(onehot, iota8m, low.unsqueeze(2).broadcast_to(shape), ALU.is_equal))


def moe_route(nc, dram, x2, pos, te, wtop, pool_share):
    with ExitStack() as ctx:
        def sb(name, shape, dt=F32):
            return ctx.enter_context(nc.sbuf_tensor("b_" + name, shape, dt))

        sem = phase_semaphores(nc, ctx, "b_")

        ident = sb("ident", [P, P])
        before = sb("before", [P, P])
        ones = sb("ones", [P, P])
        wg = sb("wg", [P, KT, NE])
        consts = sb("consts", [P, 3 * TT * NE + NE * TILES])
        iota8m = consts[:, 0:TT * NE].rearrange("p (t e) -> p t e", e=NE)
        bg = consts[:, TT * NE:2 * TT * NE].rearrange("p (t e) -> p t e", e=NE)
        steps = consts[:, 2 * TT * NE:3 * TT * NE].rearrange("p (e j) -> p e j", e=NE)
        tile_no = consts[:, 3 * TT * NE:].rearrange("p (i e) -> p i e", e=NE)
        xT = [sb(f"xT{i}", [P, KT, 4, P]) for i in range(2)]
        lg = sb("lg", [P, TT, NE])
        mx = sb("mx", [P, TT])
        t8 = sb("t8", [P, TT, NE])
        low = sb("low", [P, TT])
        onehot = sb("onehot", [P, TT, NE])
        ex = sb("ex", [P, TT, NE])
        z = sb("z", [P, TT])
        run = [sb(f"run{i}", [P, TT, NE]) for i in range(2)]
        tot = sb("tot", [P, TT, NE])
        need = sb("need", [P, NE])
        cum = [sb(f"cum{i}", [P, NE]) for i in range(2)]
        base = sb("base", [P, NE])
        posf = sb("posf", [P, TT])
        tmpi = sb("tmpi", [P, TILES, NE])
        tef = sb("tef", [P, TILES])
        pt = [ctx.enter_context(nc.psum_tensor(f"b_pt{i}", [P, 4, P], F32)) for i in range(4)]
        pl = ctx.enter_context(nc.psum_tensor("b_pl", [P, TT, NE], F32))
        pr = ctx.enter_context(nc.psum_tensor("b_pr", [P, TT, NE], F32))
        pc = ctx.enter_context(nc.psum_tensor("b_pc", [P, TT, NE], F32))

        s_in = sem("in")
        s_x = sem("x")
        s_turned = sem("turned")
        s_xT = [sem("xT_act"), sem("xT_dve")]
        s_logits = sem("logits")
        s_cent = sem("centred")
        s_ex = sem("ex")
        s_onehot = sem("onehot")
        s_ranks = sem("ranks")
        s_pos = sem("pos")
        s_te = sem("te")
        s_rows = sem("rows")
        s_dve = sem("dve")
        block = ctx.enter_context(nc.Block())

        @block.sync
        def _(sp):
            sp.dma_start(x2[:], dram["x2"].rearrange("b (t p) d -> p (b t) d", p=P)).then_inc(s_x, 16)
            sp.dma_start(ident[:], dram["ident"]).then_inc(s_in, 16)
            sp.dma_start(wg[:], dram["wg"]).then_inc(s_in, 16)
            sp.dma_start(before[:], dram["before"]).then_inc(s_in, 16)
            sp.dma_start(consts[:], dram["route"]).then_inc(s_in, 16)

        @block.tensor
        def _(pe):
            pe.wait_ge(s_in, 64)
            pe.wait_ge(s_x, 16)
            for q in range(4):
                if q >= 2:
                    pe.wait_ge(s_xT[0], q - 1)
                    pe.wait_ge(s_xT[1], q - 1)
                for k in range(KT):
                    for j in range(4):
                        ins = pe.transpose(pt[2 * (q % 2) + k][:, j], x2[:, 4 * q + j, k * P:(k + 1) * P], ident[:])
                ins.then_inc(s_turned, 1)
                pe.wait_ge(s_xT[0], q + 1)
                pe.wait_ge(s_xT[1], q + 1)
                for j in range(4):
                    for k in range(KT):
                        ins = pe.matmul(pl[:, 4 * q + j], xT[q % 2][:, k, j], wg[:, k], start=(k == 0),
                                        stop=(k == KT - 1), skip_group_check=True)
            ins.then_inc(s_logits, 1)
            pe.wait_ge(s_onehot, 1)
            pe.matmul(pr[:], before[:], onehot[:], start=True, stop=True)
            pe.matmul(pc[:], ones[:], onehot[:], start=True, stop=True).then_inc(s_ranks, 1)

        @block.scalar
        def _(act):
            for q in range(4):
                act.wait_ge(s_turned, q + 1)
                if q >= 2:
                    act.wait_ge(s_turned, q + 1)
                act.copy(xT[q % 2][:, 0], pt[2 * (q % 2)][:]).then_inc(s_xT[0], 1)
            act.wait_ge(s_cent, 1)
            act.activation(ex[:], ex[:], ACT.Exp).then_inc(s_ex, 1)

        @block.vector
        def _(dve):
            n = [0]

            def link(ins):
                ins.then_inc(s_dve, 1)
                n[0] += 1
                dve.wait_ge(s_dve, n[0])

            dve.memset(ones[:], 1.0)
            for q in range(4):
                dve.wait_ge(s_turned, q + 1)
                dve.tensor_copy(xT[q % 2][:, 1], pt[2 * (q % 2) + 1][:]).then_inc(s_xT[1], 1)
            dve.wait_ge(s_in, 64)
            dve.wait_ge(s_logits, 1)
            link(dve.tensor_tensor(lg[:], pl[:], bg, ALU.add))
            first_max_onehot(dve, link, lg[:], mx[:], t8[:], low[:], onehot[:], iota8m)
            dve.tensor_tensor(ex[:], lg[:], mx[:].unsqueeze(2).broadcast_to([P, TT, NE]), ALU.subtract)\
                .then_inc(s_cent, 1)
            dve.sem_inc(s_onehot, 1)
            dve.wait_ge(s_ex, 1)
            link(dve.tensor_reduce(z[:], ex[:], AX.X, ALU.add))
            dve.reciprocal(wtop, z[:])
            dve.wait_ge(s_ranks, 1)
            link(dve.tensor_copy(tot[:], pc[:]))
            src = tot
            for i, d in enumerate((1, 2, 4, 8)):
                dst = run[i % 2]
                dve.tensor_copy(dst[:, 0:d], src[:, 0:d])
                link(dve.tensor_tensor(dst[:, d:TT], src[:, d:TT], src[:, 0:TT - d], ALU.add))
                src = dst
            link(dve.tensor_tensor(t8[:].rearrange("p t e -> p (t e)").rearrange("p (e j) -> p e j", e=NE),
                                   src[:, TT - 1].unsqueeze(2).broadcast_to([P, NE, TT]), steps, ALU.is_gt))
            link(dve.tensor_reduce(need[:], t8[:].rearrange("p t e -> p (t e)").rearrange("p (e j) -> p e j", e=NE),
                                   AX.X, ALU.add))
            c = need
            for i, d in enumerate((1, 2, 4)):
                dst = cum[i % 2]
                dve.tensor_copy(dst[:, 0:d], c[:, 0:d])
                link(dve.tensor_tensor(dst[:, d:NE], c[:, d:NE], c[:, 0:NE - d], ALU.add))
                c = dst
            link(dve.tensor_tensor(tmpi[:], c[:].unsqueeze(1).broadcast_to([P, TILES, NE]), tile_no, ALU.is_le))
            link(dve.tensor_reduce(tef[:], tmpi[:], AX.X, ALU.add))
            link(dve.tensor_scalar(te, tef[:], float(NE - 1), None, ALU.min))
            link(dve.tensor_tensor(base[:], c[:], need[:], ALU.subtract))
            link(dve.tensor_scalar(base[:], base[:], float(P), None, ALU.mult))
            link(dve.tensor_tensor(t8[:], src[:], tot[:], ALU.subtract))
            link(dve.tensor_tensor(t8[:], t8[:], pr[:], ALU.add))
            link(dve.tensor_tensor(t8[:], t8[:], base[:].unsqueeze(1).broadcast_to([P, TT, NE]), ALU.add))
            link(dve.tensor_tensor(t8[:], t8[:], onehot[:], ALU.mult))
            link(dve.tensor_reduce(posf[:], t8[:], AX.X, ALU.add))
            dve.tensor_copy(pos, posf[:]).then_inc(s_pos, 1)

        @block.gpsimd
        def _(pool):
            pool.wait_ge(s_pos, 1)
            pool.wait_ge(s_x, 16)
            for t in range(TT):
                pool.indirect_dma_start(
                    out=dram["xs"], out_offset=bass.IndirectOffsetOnAxis(ap=pos[:, t:t + 1], axis=0),
                    in_=x2[:, t, :], in_offset=None).then_inc(s_rows, 16)
            pool.wait_ge(s_rows, 16 * TT)
            pool_share(pool)


def moe_experts(nc, dram, te, pool_share):
    with ExitStack() as ctx:
        def sb(name, shape, dt=F32):
            return ctx.enter_context(nc.sbuf_tensor("e_" + name, shape, dt))

        sem = phase_semaphores(nc, ctx, "e_")

        ident = sb("ident", [P, P])
        w1 = [sb(f"w1{i}", [P, KT, HID]) for i in range(2)]
        w2 = [sb(f"w2{i}", [P, HT, D]) for i in range(2)]
        b1 = [sb(f"b1{i}", [P, HT]) for i in range(2)]
        b2 = [sb(f"b2{i}", [P, D]) for i in range(2)]
        xs = [sb(f"xs{i}", [P, D]) for i in range(2)]
        xsT = [sb(f"xsT{i}", [P, KT, P]) for i in range(2)]
        h = [sb(f"h{i}", [P, HT, P]) for i in range(2)]
        ys = [sb(f"ys{i}", [P, D]) for i in range(2)]
        pt = ctx.enter_context(nc.psum_tensor("e_pt", [P, KT, P], F32))
        ph = [ctx.enter_context(nc.psum_tensor(f"e_ph{i}", [P, HT, P], F32)) for i in range(2)]
        po = [ctx.enter_context(nc.psum_tensor(f"e_po{i}", [P, D], F32)) for i in range(2)]

        s_in = sem("in")
        s_w1 = [sem(f"w1_{i}") for i in range(2)]
        s_b1 = [sem(f"b1_{i}") for i in range(2)]
        s_w2 = [sem(f"w2_{i}") for i in range(2)]
        s_turned = sem("turned")
        s_xsT = sem("xsT")
        s_half = sem("half")
        s_hid = sem("hid")
        s_silu = sem("silu")
        s_out = sem("out")
        s_ys = sem("ys")
        s_sent = [sem(f"sent{i}") for i in range(2)]
        block = ctx.enter_context(nc.Block())

        @block.sync
        def _(sp):
            sp.dma_start(ident[:], dram["ident"]).then_inc(s_in, 16)

            def load(i, p, first):
                e = sp.value_load(te[0:1, bass.ds(i, 1)], min_val=0, max_val=NE - 1)
                if not first:
                    sp.wait_ge(s_hid, i - 1)
                    sp.wait_ge(s_turned, i - 1)
                sp.dma_start(w1[p][:], dram["w1"][bass.ds(e, 1)].rearrange("e p k h -> p (e k) h")).then_inc(s_w1[p], 16)
                sp.dma_start(xs[p][:], dram["xs"][bass.ds(i * P, P), :]).then_inc(s_w1[p], 16)
                if not first:
                    sp.wait_ge(s_silu, i - 1)
                sp.dma_start(b1[p][:], dram["b1"][bass.ds(e, 1)].rearrange("e p h -> p (e h)")).then_inc(s_b1[p], 16)
                if not first:
                    sp.wait_ge(s_ys, i - 1)
                sp.dma_start(w2[p][:], dram["w2"][bass.ds(e, 1)].rearrange("e p k h -> p (e k) h")).then_inc(s_w2[p], 16)
                sp.dma_start(b2[p][:], dram["b2"][bass.ds(e, 1), :].broadcast_to([P, D])).then_inc(s_w2[p], 16)

            def store(i, p):
                sp.wait_ge(s_ys, i + 1)
                sp.dma_start(dram["ys"][bass.ds(i * P, P), :], ys[p][:]).then_inc(s_sent[p], 16)

            load(0, 0, True)
            load(1, 1, True)
            with sp.Fori(0, TILES - 3, 2) as i:
                load(i + 2, 0, False)
                store(i, 0)
                load(i + 3, 1, False)
                store(i + 1, 1)
            load(TILES - 1, 0, False)
            for i in range(TILES - 3, TILES):
                store(i, i % 2)
            sp.wait_ge(s_sent[0], 16 * (TILES // 2 + 1))
            sp.wait_ge(s_sent[1], 16 * (TILES // 2))

        @block.gpsimd
        def _(pool):
            pool_share(pool)

        @block.tensor
        def _(pe):
            pe.wait_ge(s_in, 16)

            def hidden(i, p, turn):
                pe.wait_ge(s_w1[p], turn * 32 + 32)
                for k in range(KT):
                    ins = pe.transpose(pt[:, k], xs[p][:, k * P:(k + 1) * P], ident[:])
                ins.then_inc(s_turned, 1)
                pe.wait_ge(s_xsT, i + 1)
                for c in range(HT):
                    for k in range(KT):
                        ins = pe.matmul(ph[p][:, c], w1[p][:, k, c * P:(c + 1) * P], xsT[p][:, k],
                                        start=(k == 0), stop=(k == KT - 1), skip_group_check=True)
                    if c == HT // 2 - 1:
                        ins.then_inc(s_half, 1)
                ins.then_inc(s_hid, 1)

            def outer(i, p, turn):
                pe.wait_ge(s_silu, i + 1)
                pe.wait_ge(s_w2[p], turn * 32 + 32)
                for c in range(HT):
                    ins = pe.matmul(po[p][:], h[p][:, c], w2[p][:, c], start=(c == 0), stop=(c == HT - 1))
                ins.then_inc(s_out, 1)

            hidden(0, 0, 0)
            with pe.Fori(0, TILES // 2) as t:
                hidden(2 * t + 1, 1, t)
                outer(2 * t, 0, t)
                hidden(2 * t + 2, 0, t + 1)
                outer(2 * t + 1, 1, t)
            outer(TILES - 1, 0, TILES // 2)

        @block.scalar
        def _(act):
            def silu(i, p, turn):
                act.wait_ge(s_b1[p], turn * 16 + 16)
                for c in range(HT):
                    if c == 0:
                        act.wait_ge(s_half, i + 1)
                    if c == HT // 2:
                        act.wait_ge(s_hid, i + 1)
                    ins = act.activation(h[p][:, c], ph[p][:, c], ACT.Silu, bias=b1[p][:, c:c + 1])
                ins.then_inc(s_silu, 1)

            silu(0, 0, 0)
            with act.Fori(0, TILES // 2) as t:
                silu(2 * t + 1, 1, t)
                silu(2 * t + 2, 0, t + 1)

        @block.vector
        def _(dve):
            def turned(i, p):
                dve.wait_ge(s_turned, i + 1)
                dve.tensor_copy(xsT[p][:], pt[:]).then_inc(s_xsT, 1)

            def finish(i, p, turn, first):
                dve.wait_ge(s_out, i + 1)
                if not first:
                    dve.wait_ge(s_sent[p], turn * 16)
                dve.tensor_tensor(ys[p][:], po[p][:], b2[p][:], ALU.add).then_inc(s_ys, 1)

            turned(0, 0)
            turned(1, 1)
            finish(0, 0, 0, True)
            turned(2, 0)
            finish(1, 1, 0, True)
            with dve.Fori(1, TILES // 2) as t:
                turned(2 * t + 1, 1)
                finish(2 * t, 0, t, False)
                turned(2 * t + 2, 0)
                finish(2 * t + 1, 1, t, False)
            finish(TILES - 1, 0, TILES // 2, False)


def moe_combine(nc, dram, x2, pos, wtop, pool_share):
    with ExitStack() as ctx:
        def sb(name, shape, dt=F32):
            return ctx.enter_context(nc.sbuf_tensor("m_" + name, shape, dt))

        sem = phase_semaphores(nc, ctx, "m_")

        y = sb("y", [P, TT, D])
        st = sb("st", [P, TT, 6])
        mv = sb("mv", [P, TT, 2])
        lnv = sb("lnv", [P, TT])
        rstd = sb("rstd", [P, TT])
        eps = sb("eps", [P, 1])
        s_y = [sem(f"y{t}") for t in range(TT)]
        s_eps = sem("eps")
        s_dve = sem("dve")
        s_mv = sem("mv")
        s_lnv = sem("lnv")
        s_rstd = sem("rstd")
        s_x3 = sem("x3")
        s_sent = sem("sent")
        block = ctx.enter_context(nc.Block())

        @block.gpsimd
        def _(pool):
            for t in range(TT):
                pool.indirect_dma_start(
                    out=y[:, t, :], out_offset=None, in_=dram["ys"],
                    in_offset=bass.IndirectOffsetOnAxis(ap=pos[:, t:t + 1], axis=0)).then_inc(s_y[t], 16)
            pool_share(pool)

        @block.vector
        def _(dve):
            dve.memset(eps[:], LN_EPS).then_inc(s_eps, 1)
            for t in range(TT):
                dve.wait_ge(s_y[t], 16)
                dve.scalar_tensor_tensor(y[:, t], y[:, t], wtop[:, t:t + 1], x2[:, t], ALU.mult, ALU.add)\
                    .then_inc(s_dve, 1)
                dve.wait_ge(s_dve, 2 * t + 1)
                dve.bn_stats(st[:, t], y[:, t]).then_inc(s_dve, 1)
                dve.wait_ge(s_dve, 2 * t + 2)
                dve.bn_aggr(mv[:, t], st[:, t]).then_inc(s_mv, 1)
            dve.wait_ge(s_mv, TT)
            dve.wait_ge(s_rstd, 1)
            for t in range(TT):
                dve.tensor_scalar(y[:, t], y[:, t], mv[:, t, 0:1], rstd[:, t:t + 1],
                                  ALU.subtract, ALU.mult).then_inc(s_x3, 1)

        @block.scalar
        def _(act):
            act.wait_ge(s_eps, 1)
            act.wait_ge(s_mv, TT)
            act.activation(lnv[:], mv[:, :, 1], ACT.Ln, bias=eps[:]).then_inc(s_lnv, 1)
            act.wait_ge(s_lnv, 1)
            act.activation(rstd[:], lnv[:], ACT.Exp, scale=-0.5).then_inc(s_rstd, 1)

        @block.sync
        def _(sp):
            for q in range(4):
                sp.wait_ge(s_x3, 4 * q + 4)
                sp.dma_start(dram["x3"][2 * q:2 * q + 2].rearrange("b (t p) d -> p (b t) d", p=P),
                             y[:, 4 * q:4 * q + 4]).then_inc(s_sent, 16)
            sp.wait_ge(s_sent, 64)


def layer1_attention(nc, dram, pool_share):
    with ExitStack() as ctx:
        def sb(name, shape, dt=F32):
            return ctx.enter_context(nc.sbuf_tensor("c_" + name, shape, dt))

        def two(name, shape, dt=F32):
            return [sb(f"{name}{i}", shape, dt) for i in range(2)]

        sem = phase_semaphores(nc, ctx, "c_")

        def sems(name):
            return [sem(f"{name}{i}") for i in range(2)]

        ident = sb("ident", [P, P])
        w = sb("w", [P, 3, KT, D])
        wr = sb("wr", [P, 2, KT, D])
        cols = sb("cols", [P, 5, 2])
        br = sb("br", [P, 2, 2])
        bv = sb("bv", [P, D])
        rope = sb("rope", [P, KT, S])
        ropeq = sb("ropeq", [P, KT, S])
        gw = sb("gw", [P, 6, 16])
        gwc = sb("gwc", [P, KT, 16])
        gb = sb("gb", [16, 1])
        eps = sb("eps", [P, 1])
        x = two("x", [P, QT, D])
        xT = two("xT", [P, KT, S])
        cT = two("cT", [P, KT, S])
        qT = two("qT", [P, KT, S])
        kT = two("kT", [P, KT, S])
        v = two("v", [P, QT, D])
        negmax = two("negmax", [P, QT])
        rsum = two("rsum", [P, QT])
        rinv = two("rinv", [P, QT])
        probs = two("probs", [P, QT, S])
        probsT = two("probsT", [P, 4, P])
        y = two("y", [P, QT, D])
        st = two("st", [P, QT, 6])
        mv = two("mv", [P, QT, 2])
        lnv = two("lnv", [P, QT])
        rstd = two("rstd", [P, QT])
        x4 = two("x4", [P, QT, D])
        x4T = two("x4T", [P, KT, S])
        gates = two("gates", [16, S])
        pm = [ctx.enter_context(nc.psum_tensor(f"c_pm{i}", [P, 2, 256], F32)) for i in range(2)]
        ps = [ctx.enter_context(nc.psum_tensor(f"c_ps{i}", [P, 2, 256], F32)) for i in range(2)]
        pt = [ctx.enter_context(nc.psum_tensor(f"c_pt{i}", [P, 4, P], F32)) for i in range(2)]
        po = [ctx.enter_context(nc.psum_tensor(f"c_po{i}", [P, 2, 256], F32)) for i in range(2)]

        s_in = sem("in")
        s_w = sem("w")
        s_x = sems("x")
        s_cT = sems("cT")
        s_step = sems("step")
        s_copied = sems("copied")
        s_scores = sems("scores")
        s_max = sems("max")
        s_exp = sems("exp")
        s_turned = sems("turned")
        s_evac = sems("evac")
        s_pv = sems("pv")
        s_stats = sems("stats")
        s_lnv = sems("lnv")
        s_rstd = sems("rstd")
        s_x4 = sems("x4")
        s_free = sems("free")
        s_sent = sems("sent")
        s_sent_g = sems("sent_g")
        s_dve = sem("dve")
        block = ctx.enter_context(nc.Block())
        STEPS1 = 6
        PASSES = B // 2

        @block.sync
        def _(sp):
            sp.dma_start(ident[:], dram["ident"]).then_inc(s_in, 16)
            sp.dma_start(w[:], dram["w"][:, WQ1:WQ1 + 3]).then_inc(s_in, 16)
            sp.dma_start(cols[:], dram["cols1"]).then_inc(s_in, 16)
            sp.dma_start(bv[:], dram["rows"][:, R_B1V]).then_inc(s_in, 16)
            sp.dma_start(rope[:], dram["rope"][:, 0]).then_inc(s_in, 16)
            sp.dma_start(ropeq[:], dram["rope"][:, 1]).then_inc(s_in, 16)
            sp.dma_start(gw[:], dram["gw"]).then_inc(s_in, 16)
            sp.dma_start(gb[:], dram["gb"]).then_inc(s_in, 16)

            def load_x(b, p):
                sp.dma_start(x[p][:], dram["x3"][bass.ds(b, 1)].rearrange("b (t p) d -> p (b t) d", p=P))\
                    .then_inc(s_x[p], 16)

            def load_c(b, p):
                sp.dma_start(cT[p][:], dram["cT"][bass.ds(b, 1)].rearrange("b p k s -> p (b k) s"))\
                    .then_inc(s_cT[p], 16)

            def store(t, p):
                b = 2 * t + p
                sp.wait_ge(s_x4[p], t + 1)
                sp.dma_start(dram["x4"][bass.ds(b, 1)].rearrange("b (t p) d -> p (b t) d", p=P), x4[p][:])\
                    .then_inc(s_sent[p], 16)
                sp.wait_ge(s_copied[p], t * STEPS1 + 6)
                sp.dma_start(dram["x4T"][bass.ds(b, 1)].rearrange("b p k s -> p (b k) s"), x4T[p][:])\
                    .then_inc(s_sent[p], 16)
                sp.wait_ge(s_copied[p], t * STEPS1 + 7)
                for g, name in enumerate(("gate_i", "gate_f")):
                    sp.dma_start(dram[name][bass.ds(b, 1)].rearrange("b h s -> (b h) s"),
                                 gates[p][8 * g:8 * g + 8, :]).then_inc(s_sent_g[p], 16)

            for p in range(2):
                load_x(p, p)
                load_c(p, p)
            with sp.Fori(0, PASSES - 1) as t:
                for p in range(2):
                    sp.wait_ge(s_stats[p], t + 1)
                    load_x(2 * t + 2 + p, p)
                for p in range(2):
                    store(t, p)
                    sp.wait_ge(s_step[p], t * STEPS1 + 6)
                    load_c(2 * t + 2 + p, p)
                for p in range(2):
                    sp.wait_ge(s_sent[p], 32 * t + 32)
                    sp.wait_ge(s_sent_g[p], 32 * t + 32)
                    sp.sem_inc(s_free[p], 1)
            for p in range(2):
                store(PASSES - 1, p)
            for p in range(2):
                sp.wait_ge(s_sent[p], 32 * PASSES)
                sp.wait_ge(s_sent_g[p], 32 * PASSES)

        @block.gpsimd
        def _(pool):
            pool_share(pool)

        @block.tensor
        def _(pe):
            pe.wait_ge(s_in, 16 * 8)
            pe.wait_ge(s_w, 6)

            def free(t, p, n):
                pe.wait_ge(s_copied[p], t * STEPS1 + n + 1)

            def turn(t, p, n, src):
                free(t, p, n)
                for k in range(KT):
                    for qt in range(QT):
                        ins = pe.transpose(pm[p][:, k, qt * P:(qt + 1) * P], src[p][:, qt, k * P:(k + 1) * P], ident[:])
                ins.then_inc(s_step[p], 1)

            def project_T(t, p, n, wi):
                free(t, p, n)
                for et in range(2):
                    for k in range(KT):
                        ins = pe.matmul(pm[p][:, et], wr[:, wi, k, et * P:(et + 1) * P], xT[p][:, k, :],
                                        start=(k == 0), stop=(k == KT - 1))
                ins.then_inc(s_step[p], 1)

            with pe.Fori(0, PASSES) as t:
                for p in range(2):
                    pe.wait_ge(s_x[p], 16 * t + 16)
                    turn(t, p, 0, x)
                for p in range(2):
                    project_T(t, p, 1, 1)
                for p in range(2):
                    project_T(t, p, 2, 0)
                for p in range(2):
                    free(t, p, 3)
                    for qt in range(QT):
                        for k in range(KT):
                            ins = pe.matmul(pm[p][:, qt], xT[p][:, k, qt * P:(qt + 1) * P], w[:, 2, k, :],
                                            start=(k == 0), stop=(k == KT - 1))
                    ins.then_inc(s_step[p], 1)
                for p in range(2):
                    for qt in range(QT):
                        for k in range(KT):
                            ins = pe.matmul(ps[p][:, qt], qT[p][:, k, qt * P:(qt + 1) * P], kT[p][:, k, :],
                                            start=(k == 0), stop=(k == KT - 1))
                    ins.then_inc(s_scores[p], 1)
                for p in range(2):
                    pe.wait_ge(s_exp[p], t + 1)
                    for qt in range(QT):
                        for c in range(2):
                            ins = pe.transpose(pt[p][:, 2 * qt + c], probs[p][:, qt, c * P:(c + 1) * P], ident[:])
                    ins.then_inc(s_turned[p], 1)
                for p in range(2):
                    free(t, p, 4)
                    pe.wait_ge(s_evac[p], t + 1)
                    for qt in range(QT):
                        for c in range(2):
                            ins = pe.matmul(po[p][:, qt], probsT[p][:, 2 * qt + c], v[p][:, c, :],
                                            start=(c == 0), stop=(c == 1))
                    ins.then_inc(s_pv[p], 1)
                for p in range(2):
                    pe.wait_ge(s_x4[p], t + 1)
                    turn(t, p, 4, x4)
                for p in range(2):
                    free(t, p, 5)
                    pe.wait_ge(s_cT[p], 16 * t + 16)
                    for k in range(KT):
                        pe.matmul(pm[p][0:16, 0], gw[:, k, :], x4T[p][:, k, :], start=(k == 0), stop=False)
                    for k in range(KT):
                        ins = pe.matmul(pm[p][0:16, 0], gwc[:, k, :], cT[p][:, k, :], start=False, stop=(k == KT - 1))
                    ins.then_inc(s_step[p], 1)

        @block.scalar
        def _(act):
            act.wait_ge(s_in, 16 * 8)
            with act.Fori(0, PASSES) as t:
                for p in range(2):
                    act.wait_ge(s_step[p], t * STEPS1 + 1)
                    act.copy(xT[p][:], pm[p][:]).then_inc(s_copied[p], 1)
                for p in range(2):
                    act.wait_ge(s_step[p], t * STEPS1 + 4)
                    act.copy(v[p][:], pm[p][:]).then_inc(s_copied[p], 1)
                for p in range(2):
                    act.wait_ge(s_max[p], t + 1)
                    for qt in range(QT):
                        ins = act.activation(probs[p][:, qt], ps[p][:, qt], ACT.Exp, bias=negmax[p][:, qt:qt + 1],
                                             accum_out=rsum[p][:, qt:qt + 1])
                    ins.then_inc(s_exp[p], 1)
                for p in range(2):
                    act.wait_ge(s_turned[p], t + 1)
                    act.copy(probsT[p][:], pt[p][:]).then_inc(s_evac[p], 1)
                for p in range(2):
                    act.wait_ge(s_stats[p], t + 1)
                    act.activation(lnv[p][:], mv[p][:, :, 1], ACT.Ln, bias=eps[:]).then_inc(s_lnv[p], 1)
                    act.wait_ge(s_lnv[p], t + 1)
                    act.activation(rstd[p][:], lnv[p][:], ACT.Exp, scale=-0.5).then_inc(s_rstd[p], 1)
                for p in range(2):
                    act.wait_ge(s_free[p], t + 1)
                    act.wait_ge(s_step[p], t * STEPS1 + 5)
                    act.copy(x4T[p][:], pm[p][:]).then_inc(s_copied[p], 1)
                for p in range(2):
                    act.wait_ge(s_step[p], t * STEPS1 + 6)
                    act.activation(gates[p][:], pm[p][0:16, 0], ACT.Identity, bias=gb[:]).then_inc(s_copied[p], 1)

        @block.vector
        def _(dve):
            dve.memset(eps[:], LN_EPS).then_inc(s_w, 1)
            for p in range(2):
                dve.sem_inc(s_copied[p], 1)
                dve.sem_inc(s_free[p], 1)
            dve.wait_ge(s_in, 16 * 8)
            src = w[:, 0:2].rearrange("p w k (i two) -> p (w k i) two", two=2)
            dst = wr[:].rearrange("p w k (i two) -> p (w k i) two", two=2)
            dve.tensor_tensor(dst[:, :, 0], src[:, :, 0], src[:, :, 1], ALU.subtract).then_inc(s_w, 1)
            dve.tensor_tensor(dst[:, :, 1], src[:, :, 1], src[:, :, 0], ALU.add).then_inc(s_w, 1)
            for i in range(2):
                dve.scalar_tensor_tensor(br[:, i], cols[:, 2 + i], cols[:, 4, 0:1], cols[:, i], ALU.mult, ALU.add)\
                    .then_inc(s_w, 1)
            dve.tensor_tensor(gwc[:], gw[:, 2:4], gw[:, 4:6], ALU.add).then_inc(s_w, 1)
            dve.wait_ge(s_w, 6)
            with dve.Fori(0, PASSES) as t:
                chain = Count(dve, s_dve, 6, t * 6)
                for p in range(2):
                    dve.wait_ge(s_step[p], t * STEPS1 + 2)
                    for et in range(2):
                        ins = dve.scalar_tensor_tensor(kT[p][:, et], pm[p][:, et], br[:, 1, et:et + 1], rope[:, et],
                                                       ALU.add, ALU.mult)
                    ins.then_inc(s_copied[p], 1)
                for p in range(2):
                    dve.wait_ge(s_step[p], t * STEPS1 + 3)
                    for et in range(2):
                        ins = dve.scalar_tensor_tensor(qT[p][:, et], pm[p][:, et], br[:, 0, et:et + 1], ropeq[:, et],
                                                       ALU.add, ALU.mult)
                    ins.then_inc(s_copied[p], 1)
                for p in range(2):
                    dve.wait_ge(s_scores[p], t + 1)
                    dve.tensor_reduce(negmax[p][:], ps[p][:], AX.X, ALU.max, negate=True).then_inc(s_max[p], 1)
                for p in range(2):
                    dve.wait_ge(s_x[p], 16 * t + 16)
                    dve.tensor_tensor(y[p][:], x[p][:], bv[:].unsqueeze(1).broadcast_to([P, QT, D]), ALU.add)
                    dve.wait_ge(s_exp[p], t + 1)
                    chain.link(dve.reciprocal(rinv[p][:], rsum[p][:]))
                for p in range(2):
                    dve.wait_ge(s_pv[p], t + 1)
                    for qt in range(QT):
                        ins = dve.scalar_tensor_tensor(y[p][:, qt], po[p][:, qt], rinv[p][:, qt:qt + 1], y[p][:, qt],
                                                       ALU.mult, ALU.add)
                    chain.link(ins)
                    dve.bn_stats(st[p][:, 0], y[p][:, 0])
                    chain.link(dve.bn_stats(st[p][:, 1], y[p][:, 1]))
                    dve.nop(nofuse=True)
                    dve.bn_aggr(mv[p][:, 0], st[p][:, 0])
                    dve.bn_aggr(mv[p][:, 1], st[p][:, 1]).then_inc(s_stats[p], 1)
                for p in range(2):
                    dve.wait_ge(s_free[p], t + 1)
                    dve.wait_ge(s_rstd[p], t + 1)
                    dve.wait_ge(s_stats[p], t + 1)
                    for qt in range(QT):
                        ins = dve.tensor_scalar(x4[p][:, qt], y[p][:, qt], mv[p][:, qt, 0:1], rstd[p][:, qt:qt + 1],
                                                ALU.subtract, ALU.mult)
                    ins.then_inc(s_x4[p], 1)
                chain.end()


H1 = 8
HW = D // H1
BH = B * H1
SCALE1 = float(1.0 / np.sqrt(np.float32(HW)))


def mlstm_gates(nc, dram, aT, eT, pool_share):
    with ExitStack() as ctx:
        def sb(name, shape, dt=F32):
            return ctx.enter_context(nc.sbuf_tensor("g_" + name, shape, dt))

        sem = phase_semaphores(nc, ctx, "g_")

        ident = sb("ident", [P, P])
        gi = sb("gi", [BH, S])
        gf = sb("gf", [BH, S])
        ab = sb("ab", [BH, S])
        ex = sb("ex", [BH, S])
        l1 = sb("l1", [BH, S])
        ls = sb("ls", [BH, S])
        ones = sb("ones", [BH, S])
        one = sb("one", [BH, 1])
        cs = sb("cs", [BH, S])
        a = sb("a", [BH, S])
        m = sb("m", [BH, S])
        en = sb("en", [BH, S])
        pt = ctx.enter_context(nc.psum_tensor("g_pt", [P, 2, 2, BH], F32))
        s_in = sem("in")
        s_ones = sem("ones")
        s_abs = sem("abs")
        s_ex = sem("ex")
        s_l1 = sem("l1")
        s_a = sem("a")
        s_m = sem("m")
        s_mld = sem("mld")
        s_en = sem("en")
        s_turned = sem("turned")
        s_done = sem("done")
        s_sent = sem("sent")
        s_dve = sem("dve")
        block = ctx.enter_context(nc.Block())

        @block.sync
        def _(sp):
            sp.dma_start(gf[:], dram["gate_f"].rearrange("b h s -> (b h) s")).then_inc(s_in, 16)
            sp.dma_start(gi[:], dram["gate_i"].rearrange("b h s -> (b h) s")).then_inc(s_in, 16)
            sp.dma_start(ident[:], dram["ident"]).then_inc(s_in, 16)
            sp.wait_ge(s_m, 1)
            sp.dma_start(dram["runmax"], m[:]).then_inc(s_sent, 16)
            sp.wait_ge(s_sent, 16)

        @block.gpsimd
        def _(pool):
            pool_share(pool)

        @block.scalar
        def _(act):
            act.wait_ge(s_abs, 1)
            act.activation(ex[:], ab[:], ACT.Exp, scale=-1.0).then_inc(s_ex, 1)
            act.wait_ge(s_ex, 1)
            act.activation(l1[:], ex[:], ACT.Ln, bias=one[:]).then_inc(s_l1, 1)
            act.wait_ge(s_mld, 1)
            act.activation(en[:], ab[:], ACT.Exp, scale=-1.0).then_inc(s_en, 1)

        @block.vector
        def _(dve):
            n = [0]

            def link(ins):
                ins.then_inc(s_dve, 1)
                n[0] += 1
                dve.wait_ge(s_dve, n[0])

            dve.memset(ones[:], 1.0)
            link(dve.memset(one[:], 1.0))
            dve.wait_ge(s_in, 48)
            dve.scalar_tensor_tensor(ab[:], gf[:], -1.0, gf[:], ALU.mult, ALU.max).then_inc(s_abs, 1)
            link(dve.tensor_scalar(ls[:], gf[:], 0.0, None, ALU.min))
            dve.wait_ge(s_l1, 1)
            link(dve.tensor_tensor(ls[:], ls[:], l1[:], ALU.subtract))
            link(dve.tensor_tensor_scan(cs[:], ones[:], ls[:], 0.0, ALU.mult, ALU.add))
            dve.tensor_tensor(a[:], gi[:], cs[:], ALU.subtract).then_inc(s_a, 1)
            dve.wait_ge(s_a, 1)
            dve.tensor_tensor_scan(m[:], a[:], a[:], -3.0e38, ALU.max, ALU.max).then_inc(s_m, 1)
            dve.wait_ge(s_m, 1)
            dve.wait_ge(s_ex, 1)
            dve.tensor_tensor(ab[:], cs[:], m[:], ALU.add).then_inc(s_mld, 1)
            dve.wait_ge(s_turned, 1)
            dve.tensor_copy(aT[:], pt[:, 0])
            dve.tensor_copy(eT[:], pt[:, 1]).then_inc(s_done, 1)

        @block.tensor
        def _(pe):
            pe.wait_ge(s_in, 48)
            pe.wait_ge(s_a, 1)
            pe.wait_ge(s_en, 1)
            for i, src in enumerate((a, en)):
                for t in range(2):
                    ins = pe.transpose(pt[:, i, t], src[:, t * P:(t + 1) * P], ident[0:BH, 0:BH])
            ins.then_inc(s_turned, 1)


def query_blocks(nc, dram, vt, qblk, pool_share):
    with ExitStack() as ctx:
        xq = ctx.enter_context(nc.sbuf_tensor(f"q{vt}_xq", [P, B, KT, P], F32))
        sem = phase_semaphores(nc, ctx, f"q{vt}_")
        s_xq = sem("xq_in")
        s_zero = sem("zero")
        block = ctx.enter_context(nc.Block())

        @block.sync
        def _(sp):
            for b in range(B):
                sp.dma_start(xq[:, b], dram["x4T"][b, :, :, vt * P:(vt + 1) * P]).then_inc(s_xq, 16)

        def fill(eng, copy, hp):
            src = xq[32 * hp:32 * hp + 32].rearrange("p b k v -> p (k v) b")
            dst = qblk[32 * hp:32 * hp + 32].rearrange("p k v n -> p (k v) n")[:, :, 8 * hp:8 * hp + 8]
            copy(dst, src)

        @block.gpsimd
        def _(pool):
            if vt == 0:
                pool.memset(qblk[:, 1], 0.0).then_inc(s_zero, 1)
            pool_share(pool)

        @block.vector
        def _(dve):
            if vt == 0:
                dve.memset(qblk[:, 0], 0.0).then_inc(s_zero, 1)
                dve.wait_ge(s_zero, 2)
            dve.wait_ge(s_xq, 16 * B)
            for hp in range(2):
                fill(dve, dve.tensor_copy, hp)

        @block.scalar
        def _(act):
            if vt == 0:
                act.wait_ge(s_zero, 2)
            act.wait_ge(s_xq, 16 * B)
            for hp in range(2, 4):
                fill(act, act.copy, hp)


def hop_scores(nc, dram, vt, qblk, kh, pool_share):
    first = 0 if vt == 0 else P // GROUP
    groups = P * (vt + 1) // GROUP
    ring = 4
    passes = groups // ring
    with ExitStack() as ctx:
        sem = phase_semaphores(nc, ctx, f"h{vt}_")

        ident = ctx.enter_context(nc.sbuf_tensor(f"h{vt}_ident", [P, P], F32))
        rows = [ctx.enter_context(nc.sbuf_tensor(f"h{vt}_rows{i}", [P, GROUP, D], F32)) for i in range(ring)]
        rT = [ctx.enter_context(nc.sbuf_tensor(f"h{vt}_rT{i}", [P, KT, GROUP, P], F32)) for i in range(2)]
        pt = [[ctx.enter_context(nc.psum_tensor(f"h{vt}_pt{i}{k}", [P, GROUP, P], F32)) for k in range(KT)]
              for i in range(2)]
        po = [ctx.enter_context(nc.psum_tensor(f"h{vt}_po{i}", [P, GROUP, BH], F32)) for i in range(2)]
        s_in = sem("in")
        s_rows = [sem(f"rows{i}") for i in range(ring)]
        s_turned = sem("turned")
        s_rT = [sem("rT_act"), sem("rT_dve")]
        s_prod = sem("prod")
        s_kh = [sem("kh_act"), sem("kh_dve")]
        block = ctx.enter_context(nc.Block())

        @block.sync
        def _(sp):
            sp.dma_start(ident[:], dram["ident"]).then_inc(s_in, 16)

            def load(n, i):
                sp.dma_start(rows[i][:].rearrange("p j d -> p (j d)"),
                             dram["pos_rows"][bass.ds(first + n, 1)].rearrange("g p n -> p (g n)"))\
                    .then_inc(s_rows[i], 16)

            for i in range(ring):
                load(i, i)
            with sp.Fori(0, passes - 1) as t:
                for i in range(ring):
                    sp.wait_ge(s_turned, 4 * t + i + 1)
                    load(4 * t + ring + i, i)

        @block.gpsimd
        def _(pool):
            pool_share(pool)

        @block.tensor
        def _(pe):
            pe.wait_ge(s_in, 16)

            def turn(t, i):
                pe.wait_ge(s_rows[i], 16 * t + 16)
                for k in range(KT):
                    for j in range(GROUP):
                        ins = pe.transpose(pt[i % 2][k][:, j], rows[i][:, j, k * P:(k + 1) * P], ident[:])
                ins.then_inc(s_turned, 1)

            def product(t, i):
                n = 4 * t + i
                pe.wait_ge(s_rT[0], n + 1)
                pe.wait_ge(s_rT[1], n + 1)
                pe.wait_ge(s_kh[i % 2], 2 * t + i // 2 + 1)
                for j in range(GROUP):
                    v = n * GROUP + j if vt == 0 else n * 2 + j // 2
                    for k in range(KT):
                        ins = pe.matmul(po[i % 2][:, j, k * 32:(k + 1) * 32], rT[i % 2][:, k, j],
                                        qblk[:, k, bass.ds(v, 1), :].rearrange("p v n -> p (v n)"),
                                        start=True, stop=True, skip_group_check=True)
                ins.then_inc(s_prod, 1)

            turn(0, 0)
            with pe.Fori(0, passes - 1) as t:
                for i in range(ring):
                    if i < ring - 1:
                        turn(t, i + 1)
                    else:
                        turn(t + 1, 0)
                    product(t, i)
            for i in range(ring):
                if i < ring - 1:
                    turn(passes - 1, i + 1)
                product(passes - 1, i)

        def evacuate(eng, copy, which):
            eng.sem_inc(s_kh[which], 1)
            if which == 0:
                eng.sem_inc(s_prod, 2)

            def scores_of(t, i):
                n = 4 * t + i
                eng.wait_ge(s_prod, n + 3)
                if vt == 0:
                    dst = kh[:, bass.ds(n * GROUP, GROUP), 0]
                else:
                    dst = kh[:, bass.ds(n * 2, 2)].rearrange("p v t n -> p (v t) n")
                copy(dst, po[i % 2][:]).then_inc(s_kh[which], 1)

            def rows_of(t, i):
                n = 4 * t + i
                eng.wait_ge(s_prod, n + 1)
                eng.wait_ge(s_turned, n + 1)
                copy(rT[i % 2][:, which], pt[i % 2][which][:]).then_inc(s_rT[which], 1)

            for i in range(ring):
                rows_of(0, i)
                if i >= 1 and (i - 1) % 2 == which:
                    scores_of(0, i - 1)
            with eng.Fori(1, passes) as t:
                for i in range(ring):
                    rows_of(t, i)
                    if (i - 1) % 2 == which:
                        if i == 0:
                            scores_of(t - 1, ring - 1)
                        else:
                            scores_of(t, i - 1)
            if which == 1:
                scores_of(passes - 1, ring - 1)

        @block.scalar
        def _(act):
            evacuate(act, act.copy, 0)

        @block.vector
        def _(dve):
            evacuate(dve, dve.tensor_copy, 1)


def mlstm_heads(nc, dram, vt, qblk, kh, aT, eT, pool_share):
    mts = range(vt + 1)
    nm = len(mts)
    with ExitStack() as ctx:
        def sb(name, shape, dt=F32):
            return ctx.enter_context(nc.sbuf_tensor(f"l{vt}_" + name, shape, dt))

        def two(name, shape, dt=F32):
            return [sb(f"{name}{i}", shape, dt) for i in range(2)]

        sem = phase_semaphores(nc, ctx, f"l{vt}_")

        def sems(name):
            return [sem(f"{name}{i}") for i in range(2)]

        lnw = sb("lnw", [P, D])
        lnb = sb("lnb", [P, D])
        eps = sb("eps", [P, 1])
        cT = two("cT", [P, KT, S])
        va = two("va", [P, 2, H1 * (HW + 1)])
        x4 = two("x4", [P, D])
        mb = two("mb", [P, H1, P])
        dm = two("dm", [P, nm, H1, P])
        cm = two("cm", [P, nm, H1, P])
        den = sb("den", [P, H1])
        rn = sb("rn", [P, H1])
        hh = sb("hh", [P, H1, HW])
        sq = sb("sq", [P, H1, HW])
        mu = sb("mu", [P, H1])
        var = sb("var", [P, H1])
        lnv8 = sb("lnv8", [P, H1])
        r8 = sb("r8", [P, H1])
        y = sb("y", [P, D])
        st = sb("st", [P, 6])
        mv = sb("mv", [P, 2])
        lnv = sb("lnv", [P, 1])
        rstd = sb("rstd", [P, 1])
        x5 = two("x5", [P, D])
        pq = [ctx.enter_context(nc.psum_tensor(f"l{vt}_pq{m}", [P, H1, P], F32)) for m in mts]
        pv = [ctx.enter_context(nc.psum_tensor(f"l{vt}_pv{i}", [P, H1, HW + 1], F32)) for i in range(2)]

        s_in = sem("in")
        s_w = sem("w")
        s_q = sems("q")
        s_va = sems("va")
        s_x4 = sems("x4")
        s_mb = sems("mb")
        s_pool = sem("pool")
        s_arg = sem("arg")
        s_dm = sem("dm")
        s_dm_free = sem("dm_free")
        s_qk = sem("qk")
        s_qk_read = sem("qk_read")
        s_c = sem("c")
        s_pv = sem("pv")
        s_var = sem("var")
        s_ln8 = sem("ln8")
        s_r8 = sem("r8")
        s_xb = sem("xb")
        s_y = sem("y")
        s_mv = sem("mv")
        s_lnv = sem("lnv")
        s_rstd = sem("rstd")
        s_x5 = sem("x5")
        s_free = sems("free")
        s_sent = sems("sent")
        s_dve = sem("dve")
        block = ctx.enter_context(nc.Block())
        PASSES = B // 2

        @block.sync
        def _(sp):
            sp.dma_start(lnw[:], dram["rows"][:, R_LNW]).then_inc(s_in, 16)
            sp.dma_start(lnb[:], dram["rows"][:, R_LNB]).then_inc(s_in, 16)

            def load(b, p, first):
                if not first:
                    sp.wait_ge(s_qk, b - 1)
                one = bass.ds(b, 1)
                sp.dma_start(cT[p][:], dram["cT"][one].rearrange("b p k s -> p (b k) s")).then_inc(s_q[p], 16)
                if not first:
                    sp.wait_ge(s_arg, b - 1)
                sp.dma_start(mb[p][:], dram["runmax"].rearrange("(b h) s -> b h s", h=H1)[
                    one, :, vt * P:(vt + 1) * P].broadcast_to([P, H1, P])).then_inc(s_mb[p], 16)
                if not first:
                    sp.wait_ge(s_pv, b - 1)
                sp.dma_start(va[p][:], dram["ctx_ones"][one].rearrange("b p m n -> p (b m) n")).then_inc(s_va[p], 16)
                if not first:
                    sp.wait_ge(s_y, b - 1)
                sp.dma_start(x4[p][:], dram["x4"][one, vt * P:(vt + 1) * P].rearrange("b p d -> p (b d)"))\
                    .then_inc(s_x4[p], 16)

            def store(b, p):
                sp.wait_ge(s_x5, b + 1)
                sp.dma_start(dram["x5"][bass.ds(b, 1), vt * P:(vt + 1) * P].rearrange("b p d -> p (b d)"), x5[p][:])\
                    .then_inc(s_sent[p], 16)

            load(0, 0, True)
            load(1, 1, True)
            with sp.Fori(0, PASSES - 1) as t:
                for p in range(2):
                    load(2 * t + 2 + p, p, False)
                    store(2 * t + p, p)
                for p in range(2):
                    sp.wait_ge(s_sent[p], 16 * t + 16)
                    sp.sem_inc(s_free[p], 1)
            for p in range(2):
                store(B - 2 + p, p)
            for p in range(2):
                sp.wait_ge(s_sent[p], 16 * PASSES)

        @block.gpsimd
        def _(pool):
            pool.wait_ge(s_w, 2)

            def args(t, p):
                b = 2 * t + p
                pool.wait_ge(s_mb[p], 16 * t + 16)
                pool.wait_ge(s_dm_free, b + 1)
                pool.nop(nofuse=True)
                pool.nop(nofuse=True)
                for m in mts:
                    ins = pool.tensor_tensor(
                        dm[p][:, m], aT[:, m, bass.ds(H1 * b, H1)].unsqueeze(2).broadcast_to([P, H1, P]), mb[p][:],
                        ALU.subtract)
                ins.then_inc(s_pool, 1)
                pool.wait_ge(s_pool, b + 1)
                pool.nop(nofuse=True)
                pool.affine_select(out=dm[p][:, vt], in_=dm[p][:, vt], compare_op=ALU.is_ge, fill=NEG, base=0,
                                   pattern=[[0, H1], [1, P]], channel_multiplier=-1).then_inc(s_arg, 1)
                pool.wait_ge(s_x4[p], 16 * t + 16)
                pool.tensor_tensor(x4[p][:], x4[p][:], lnb[:], ALU.add).then_inc(s_xb, 1)

            with pool.Fori(0, PASSES) as t:
                args(t, 0)
                args(t, 1)

        @block.tensor
        def _(pe):
            def qk(t, p):
                b = 2 * t + p
                pe.wait_ge(s_q[p], 16 * t + 16)
                pe.wait_ge(s_qk_read, b + 1)
                for m in mts:
                    for k in range(KT):
                        q = qblk[:, k].rearrange("p v (h b) -> p h v b", b=B)[:, :, :, bass.ds(b, 1)]\
                            .rearrange("p h v b -> p h (v b)")
                        ins = pe.matmul(pq[m][:, 4 * k:4 * k + 4], cT[p][:, k, m * P:(m + 1) * P], q,
                                        start=True, stop=True, skip_group_check=True)
                ins.then_inc(s_qk, 1)

            def values(t, p):
                b = 2 * t + p
                pe.wait_ge(s_va[p], 16 * t + 16)
                pe.wait_ge(s_c, b + 1)
                for h in range(H1):
                    for m in mts:
                        ins = pe.matmul(pv[p][:, h], cm[p][:, m, h], va[p][:, m, h * (HW + 1):(h + 1) * (HW + 1)],
                                        start=(m == 0), stop=(m == nm - 1), skip_group_check=True)
                ins.then_inc(s_pv, 1)

            qk(0, 0)
            with pe.Fori(0, PASSES - 1) as t:
                qk(t, 1)
                values(t, 0)
                qk(t + 1, 0)
                values(t, 1)
            qk(PASSES - 1, 1)
            values(PASSES - 1, 0)
            values(PASSES - 1, 1)

        @block.scalar
        def _(act):
            act.wait_ge(s_w, 2)

            def decay(t, p):
                b = 2 * t + p
                act.wait_ge(s_arg, b + 1)
                act.activation(dm[p][:], dm[p][:], ACT.Exp).then_inc(s_dm, 1)

            def roots(t, p):
                b = 2 * t + p
                act.wait_ge(s_var, b + 1)
                act.activation(lnv8[:], var[:], ACT.Ln, bias=eps[:], scale=1.0 / HW).then_inc(s_ln8, 1)
                act.wait_ge(s_ln8, b + 1)
                act.activation(r8[:], lnv8[:], ACT.Exp, scale=-0.5).then_inc(s_r8, 1)
                act.wait_ge(s_mv, b + 1)
                act.activation(lnv[:], mv[:, 1:2], ACT.Ln, bias=eps[:]).then_inc(s_lnv, 1)
                act.wait_ge(s_lnv, b + 1)
                act.activation(rstd[:], lnv[:], ACT.Exp, scale=-0.5).then_inc(s_rstd, 1)

            decay(0, 0)
            with act.Fori(0, PASSES - 1) as t:
                decay(t, 1)
                roots(t, 0)
                decay(t + 1, 0)
                roots(t, 1)
            decay(PASSES - 1, 1)
            roots(PASSES - 1, 0)
            roots(PASSES - 1, 1)

        @block.vector
        def _(dve):
            dve.memset(eps[:], LN_EPS).then_inc(s_w, 1)
            dve.sem_inc(s_qk_read, 1)
            dve.sem_inc(s_dm_free, 2)
            for p in range(2):
                dve.sem_inc(s_free[p], 1)
            dve.wait_ge(s_in, 32)
            dve.tensor_scalar(lnw[:], lnw[:], 1.0, None, ALU.add).then_inc(s_w, 1)
            dve.wait_ge(s_w, 2)
            def front(t, p):
                b = 2 * t + p
                dve.wait_ge(s_qk, b + 1)
                for m in mts:
                    hop = kh[:, :, m, :].rearrange("p v (h b) -> p h v b", b=B)[:, :, :, bass.ds(b, 1)]\
                        .rearrange("p h v b -> p h (v b)")
                    ins = dve.scalar_tensor_tensor(cm[p][:, m], pq[m][:], SCALE1, hop, ALU.mult, ALU.add)
                ins.then_inc(s_qk_read, 1)
                dve.wait_ge(s_qk_read, b + 2)
                dve.wait_ge(s_dm, b + 1)
                ins = dve.tensor_tensor(cm[p][:], cm[p][:], dm[p][:], ALU.mult)
                ins.then_inc(s_c, 1)
                dve.wait_ge(s_c, b + 1)
                dve.sem_inc(s_dm_free, 1)

            def back(t, p):
                b = 2 * t + p
                chain = Count(dve, s_dve, 13, 13 * b)
                dve.wait_ge(s_pv, b + 1)
                chain.link(dve.scalar_tensor_tensor(den[:], pv[p][:, :, HW], -1.0, eT[:, vt, bass.ds(H1 * b, H1)],
                                                    ALU.mult, ALU.max))
                chain.link(dve.tensor_tensor(den[:], pv[p][:, :, HW], den[:], ALU.max))
                chain.link(dve.tensor_scalar(den[:], den[:], 1.0e-6, None, ALU.add))
                chain.link(dve.reciprocal(rn[:], den[:]))
                wide = [P, H1, HW]
                chain.link(dve.tensor_tensor(hh[:], pv[p][:, :, 0:HW], rn[:].unsqueeze(2).broadcast_to(wide), ALU.mult))
                chain.link(dve.tensor_reduce(mu[:], hh[:], AX.X, ALU.add))
                chain.link(dve.tensor_scalar(mu[:], mu[:], -1.0 / HW, None, ALU.mult))
                chain.link(dve.tensor_tensor(hh[:], hh[:], mu[:].unsqueeze(2).broadcast_to(wide), ALU.add))
                chain.link(dve.tensor_tensor(sq[:], hh[:], hh[:], ALU.mult))
                dve.tensor_reduce(var[:], sq[:], AX.X, ALU.add).then_inc(s_var, 1)
                dve.wait_ge(s_r8, b + 1)
                chain.link(dve.tensor_tensor(hh[:], hh[:], r8[:].unsqueeze(2).broadcast_to(wide), ALU.mult))
                chain.link(dve.tensor_tensor(y[:], hh[:].rearrange("p h c -> p (h c)"), lnw[:], ALU.mult))
                dve.wait_ge(s_xb, b + 1)
                dve.tensor_tensor(y[:], y[:], x4[p][:], ALU.add).then_inc(s_y, 1)
                dve.wait_ge(s_y, b + 1)
                chain.link(dve.bn_stats(st[:], y[:]))
                dve.nop(nofuse=True)
                dve.bn_aggr(mv[:], st[:]).then_inc(s_mv, 1)
                dve.wait_ge(s_free[p], t + 1)
                dve.wait_ge(s_mv, b + 1)
                dve.wait_ge(s_rstd, b + 1)
                chain.link(dve.tensor_scalar(x5[p][:], y[:], mv[:, 0:1], rstd[:], ALU.subtract, ALU.mult))
                dve.sem_inc(s_x5, 1)
                chain.end()

            front(0, 0)
            with dve.Fori(0, PASSES - 1) as t:
                front(t, 1)
                back(t, 0)
                front(t + 1, 0)
                back(t, 1)
            front(PASSES - 1, 1)
            back(PASSES - 1, 0)
            back(PASSES - 1, 1)


HID1 = P
SHARED = NE


def experts_top2(nc, dram):
    with ExitStack() as ctx:
        def sb(name, shape, dt=F32):
            return ctx.enter_context(nc.sbuf_tensor("f_" + name, shape, dt))

        def two(name, shape, dt=F32):
            return [sb(f"{name}{i}", shape, dt) for i in range(2)]

        sem = phase_semaphores(nc, ctx, "f_")

        def sems(name):
            return [sem(f"{name}{i}") for i in range(2)]

        ident = sb("ident", [P, P])
        w1 = sb("w1", [P, KT, NE + 1, HID1])
        w2 = sb("w2", [P, NE + 1, D])
        b1 = sb("b1", [P, NE + 1])
        b2 = sb("b2", [NE, D])
        bs2 = sb("bs2", [P, D])
        gw = sb("gw", [P, KT, NE])
        rscale = sb("rscale", [P, 1])
        iota8m = sb("iota8m", [P, QT, NE])
        eps = sb("eps", [P, 1])
        x = two("x", [P, QT, D])
        xT = two("xT", [P, KT, S])
        e = sb("e", [P, QT, NE])
        s1 = sb("s1", [P, QT, NE])
        s2 = sb("s2", [P, QT, NE])
        t8 = sb("t8", [P, QT, NE])
        one1 = sb("one1", [P, QT, NE])
        one2 = sb("one2", [P, QT, NE])
        m1 = sb("m1", [P, QT])
        m2 = sb("m2", [P, QT])
        low = sb("low", [P, QT])
        gate = two("gate", [P, QT, NE])
        gT = two("gT", [NE, QT, P])
        h = [sb(f"h{i}", [P, S]) for i in range(2)]
        acc = sb("acc", [P, QT, D])
        st = sb("st", [P, QT, 6])
        mv = sb("mv", [P, QT, 2])
        lnv = sb("lnv", [P, QT])
        rstd = sb("rstd", [P, QT])
        y = two("y", [P, QT, D])
        pm = ctx.enter_context(nc.psum_tensor("f_pm", [P, KT, S], F32))
        pg = ctx.enter_context(nc.psum_tensor("f_pg", [P, QT, NE], F32))
        pgT = ctx.enter_context(nc.psum_tensor("f_pgT", [NE, QT, P], F32))
        ph = [ctx.enter_context(nc.psum_tensor(f"f_ph{i}", [P, S], F32)) for i in range(2)]
        po = [ctx.enter_context(nc.psum_tensor(f"f_po{i}", [P, QT, D], F32)) for i in range(2)]

        s_in = sem("in")
        s_w = sem("w")
        s_x = sems("x")
        s_turned = sem("turned")
        s_xT = sem("xT")
        s_logits = sem("logits")
        s_e = sem("e")
        s_gate = sem("gate")
        s_gT = sem("gT")
        s_gT_copied = sem("gT_copied")
        s_h = sem("h")
        s_gelu = sem("gelu")
        s_o = sem("o")
        s_acc = sem("acc")
        s_done = sem("done")
        s_st = sem("st")
        s_mv = sem("mv")
        s_lnv = sem("lnv")
        s_rstd = sem("rstd")
        s_y = sem("y")
        s_free = sems("free")
        s_sent = sems("sent")
        s_dve = sem("dve")
        block = ctx.enter_context(nc.Block())
        PASSES = B // 2
        N = NE + 1
        ORDER = [SHARED] + list(range(NE))

        @block.sync
        def _(sp):
            def load(b, p):
                sp.dma_start(x[p][:], dram["x5"][bass.ds(b, 1)].rearrange("b (t p) d -> p (b t) d", p=P))\
                    .then_inc(s_x[p], 16)

            sp.dma_start(ident[:], dram["ident"]).then_inc(s_in, 16)
            load(0, 0)
            sp.dma_start(gw[:], dram["gate1"]).then_inc(s_in, 16)
            sp.dma_start(rscale[:], dram["rscale"]).then_inc(s_in, 16)
            sp.dma_start(iota8m[:], dram["iota8m"]).then_inc(s_in, 16)
            sp.dma_start(w1[:], dram["f_w1"]).then_inc(s_in, 16)
            sp.dma_start(b1[:], dram["f_b1"]).then_inc(s_in, 16)
            sp.dma_start(w2[:], dram["f_w2"]).then_inc(s_in, 16)
            sp.dma_start(b2[:], dram["f_b2"]).then_inc(s_in, 16)
            sp.dma_start(bs2[:], dram["rows"][:, R_BS2]).then_inc(s_in, 16)
            load(1, 1)

            def store(b, p):
                sp.wait_ge(s_y, b + 1)
                sp.dma_start(dram["out"][bass.ds(b, 1)].rearrange("b (t p) d -> p (b t) d", p=P), y[p][:])\
                    .then_inc(s_sent[p], 16)

            with sp.Fori(0, PASSES - 1) as t:
                for p in range(2):
                    b = 2 * t + p
                    store(b, p)
                    load(b + 2, p)
                    sp.wait_ge(s_sent[p], 16 * t + 16)
                    sp.sem_inc(s_free[p], 1)
            for p in range(2):
                store(B - 2 + p, p)
            for p in range(2):
                sp.wait_ge(s_sent[p], 16 * PASSES)

        @block.tensor
        def _(pe):
            pe.wait_ge(s_in, 16 * 9)

            def prepare(t, p):
                b = 2 * t + p
                pe.wait_ge(s_x[p], 16 * t + 16)
                for k in range(KT):
                    for qt in range(QT):
                        ins = pe.transpose(pm[:, k, qt * P:(qt + 1) * P], x[p][:, qt, k * P:(k + 1) * P], ident[:])
                ins.then_inc(s_turned, 1)
                pe.wait_ge(s_xT, b + 1)
                for qt in range(QT):
                    for k in range(KT):
                        ins = pe.matmul(pg[:, qt], xT[p][:, k, qt * P:(qt + 1) * P], gw[:, k],
                                        start=(k == 0), stop=(k == KT - 1))
                ins.then_inc(s_logits, 1)

            def hidden(b, p, i):
                if i >= 2:
                    pe.wait_ge(s_gelu, b * N + i - 1)
                for k in range(KT):
                    ins = pe.matmul(ph[i % 2][:], w1[:, k, ORDER[i]], xT[p][:, k], start=(k == 0), stop=(k == KT - 1))
                ins.then_inc(s_h, 1)

            def outer(b, p, i):
                pe.wait_ge(s_gelu, b * N + i + 1)
                if i >= 2:
                    pe.wait_ge(s_acc, b * N + i - 1)
                for qt in range(QT):
                    if i == 0:
                        pe.matmul(po[0][:, qt], gT[p][:, qt], b2[:], start=True, stop=False)
                    ins = pe.matmul(po[i % 2][:, qt], h[i % 2][:, qt * P:(qt + 1) * P], w2[:, ORDER[i]],
                                    start=(i != 0), stop=True)
                ins.then_inc(s_o, 1)

            def main(t, p, following):
                b = 2 * t + p
                hidden(b, p, 0)
                hidden(b, p, 1)
                pe.wait_ge(s_gate, b + 1)
                for qt in range(QT):
                    ins = pe.transpose(pgT[:, qt], gate[p][:, qt], ident[:])
                ins.then_inc(s_gT, 1)
                pe.wait_ge(s_gT_copied, b + 1)
                pe.wait_ge(s_done, b + 1)
                for i in range(N):
                    outer(b, p, i)
                    if i + 2 < N:
                        hidden(b, p, i + 2)
                    if i == 3 and following is not None:
                        following()

            prepare(0, 0)
            with pe.Fori(0, PASSES - 1) as t:
                main(t, 0, lambda: prepare(t, 1))
                main(t, 1, lambda: prepare(t + 1, 0))
            main(PASSES - 1, 0, lambda: prepare(PASSES - 1, 1))
            main(PASSES - 1, 1, None)

        @block.scalar
        def _(act):
            act.wait_ge(s_in, 16 * 9)
            act.wait_ge(s_w, 1)

            def prepare(t, p):
                b = 2 * t + p
                act.wait_ge(s_turned, b + 1)
                act.copy(xT[p][:], pm[:]).then_inc(s_xT, 1)
                act.wait_ge(s_logits, b + 1)
                act.activation(e[:], pg[:], ACT.Exp, scale=-1.0).then_inc(s_e, 1)

            def gelus(t, p, following):
                b = 2 * t + p
                for i in range(N):
                    act.wait_ge(s_h, b * N + i + 1)
                    if i >= 2:
                        act.wait_ge(s_o, b * N + i - 1)
                    act.activation(h[i % 2][:], ph[i % 2][:], ACT.Gelu, bias=b1[:, ORDER[i]:ORDER[i] + 1])\
                        .then_inc(s_gelu, 1)
                    if i == 5 and following is not None:
                        following()
                act.wait_ge(s_mv, b + 1)
                act.activation(lnv[:], mv[:, :, 1], ACT.Ln, bias=eps[:]).then_inc(s_lnv, 1)
                act.wait_ge(s_lnv, b + 1)
                act.activation(rstd[:], lnv[:], ACT.Exp, scale=-0.5).then_inc(s_rstd, 1)

            prepare(0, 0)
            with act.Fori(0, PASSES - 1) as t:
                gelus(t, 0, lambda: prepare(t, 1))
                gelus(t, 1, lambda: prepare(t + 1, 0))
            gelus(PASSES - 1, 0, lambda: prepare(PASSES - 1, 1))
            gelus(PASSES - 1, 1, None)

        @block.vector
        def _(dve):
            dve.memset(eps[:], LN_EPS).then_inc(s_w, 1)
            for p in range(2):
                dve.sem_inc(s_free[p], 1)
            dve.sem_inc(s_done, 1)
            dve.wait_ge(s_in, 16 * 9)
            shape = [P, QT, NE]

            def gating(t, p, chain):
                b = 2 * t + p

                def largest(src, m, onehot):
                    chain.link(dve.tensor_reduce(m[:], src[:], AX.X, ALU.max))
                    chain.link(dve.tensor_tensor(t8[:], src[:], m[:].unsqueeze(2).broadcast_to(shape), ALU.is_equal))
                    chain.link(dve.tensor_tensor(t8[:], t8[:], iota8m[:], ALU.mult))
                    chain.link(dve.tensor_reduce(low[:], t8[:], AX.X, ALU.min))
                    chain.link(dve.tensor_tensor(onehot[:], iota8m[:], low[:].unsqueeze(2).broadcast_to(shape),
                                                 ALU.is_equal))

                dve.wait_ge(s_e, b + 1)
                chain.link(dve.tensor_scalar(s1[:], e[:], 1.0, None, ALU.add))
                chain.link(dve.reciprocal(s2[:], s1[:]))
                chain.link(dve.tensor_scalar(s1[:], s2[:], rscale[:, 0:1], None, ALU.mult))
                largest(s1, m1, one1)
                chain.link(dve.scalar_tensor_tensor(s2[:], one1[:], NEG, s1[:], ALU.mult, ALU.add))
                largest(s2, m2, one2)
                dve.tensor_tensor(m1[:], m1[:], m2[:], ALU.add)
                chain.link(dve.tensor_tensor(one1[:], one1[:], one2[:], ALU.add))
                dve.reciprocal(m2[:], m1[:])
                chain.link(dve.tensor_tensor(s1[:], s1[:], one1[:], ALU.mult))
                dve.tensor_tensor(gate[p][:], s1[:], m2[:].unsqueeze(2).broadcast_to(shape), ALU.mult)\
                    .then_inc(s_gate, 1)
                dve.wait_ge(s_x[p], 16 * t + 16)
                dve.wait_ge(s_turned, b + 1)
                chain.link(dve.tensor_tensor(x[p][:], x[p][:], bs2[:].unsqueeze(1).broadcast_to([P, QT, D]), ALU.add))

            def main(t, p, following):
                b = 2 * t + p
                dve.wait_ge(s_gT, b + 1)
                dve.tensor_copy(gT[p][:], pgT[:]).then_inc(s_gT_copied, 1)
                for i in range(N):
                    dve.wait_ge(s_o, b * N + i + 1)
                    if i == 0:
                        ins = dve.tensor_tensor(acc[:], po[0][:], x[p][:], ALU.add)
                    else:
                        dve.wait_ge(s_acc, b * N + i)
                        for qt in range(QT):
                            ins = dve.scalar_tensor_tensor(
                                acc[:, qt], po[i % 2][:, qt], gate[p][:, qt, ORDER[i]:ORDER[i] + 1], acc[:, qt],
                                ALU.mult, ALU.add)
                    ins.then_inc(s_acc, 1)
                    if i == 6 and following is not None:
                        following()
                dve.wait_ge(s_acc, b * N + N)
                dve.sem_inc(s_done, 1)
                dve.bn_stats(st[:, 0], acc[:, 0])
                dve.bn_stats(st[:, 1], acc[:, 1]).then_inc(s_st, 1)
                dve.wait_ge(s_st, b + 1)
                dve.nop(nofuse=True)
                dve.bn_aggr(mv[:, 0], st[:, 0])
                dve.bn_aggr(mv[:, 1], st[:, 1]).then_inc(s_mv, 1)
                dve.wait_ge(s_free[p], t + 1)
                dve.wait_ge(s_mv, b + 1)
                dve.wait_ge(s_rstd, b + 1)
                for qt in range(QT):
                    ins = dve.tensor_scalar(y[p][:, qt], acc[:, qt], mv[:, qt, 0:1], rstd[:, qt:qt + 1],
                                            ALU.subtract, ALU.mult)
                ins.then_inc(s_y, 1)

            LINKS = 17

            def gate_of(t, p):
                chain = Count(dve, s_dve, LINKS, (2 * t + p) * LINKS)
                gating(t, p, chain)
                chain.end()

            gate_of(0, 0)
            with dve.Fori(0, PASSES - 1) as t:
                main(t, 0, lambda: gate_of(t, 1))
                main(t, 1, lambda: gate_of(t + 1, 0))
            main(PASSES - 1, 0, lambda: gate_of(PASSES - 1, 1))
            main(PASSES - 1, 1, None)


def build(nc, dram, phases):
    with ExitStack() as ctx:
        rows = TableRows(nc, ctx, dram)
        layer0_attention(nc, dram, rows.share(0, GROUPS // 2))
        if phases < 2:
            return
        with ExitStack() as own:
            x2 = own.enter_context(nc.sbuf_tensor("x2_tok", [P, TT, D], F32))
            pos = own.enter_context(nc.sbuf_tensor("pos", [P, TT], I32))
            te = own.enter_context(nc.sbuf_tensor("tile_expert", [P, TILES], I32))
            wtop = own.enter_context(nc.sbuf_tensor("wtop", [P, TT], F32))
            moe_route(nc, dram, x2, pos[:], te[:], wtop[:], lambda pool: None)
            moe_experts(nc, dram, te[:], lambda pool: None)
            moe_combine(nc, dram, x2, pos[:], wtop[:], lambda pool: None)
        if phases < 3:
            return
        layer1_attention(nc, dram, lambda pool: None)
        if phases < 4:
            return
        with ExitStack() as own:
            aT = own.enter_context(nc.sbuf_tensor("aT", [P, 2, BH], F32))
            eT = own.enter_context(nc.sbuf_tensor("eT", [P, 2, BH], F32))
            qblk = own.enter_context(nc.sbuf_tensor("qblk", [P, KT, P, 32], F32))
            kh = own.enter_context(nc.sbuf_tensor("kh", [P, P, 2, BH], F32))
            mlstm_gates(nc, dram, aT, eT, lambda pool: None)
            for vt in range(QT):
                query_blocks(nc, dram, vt, qblk, lambda pool: None)
                hop_scores(nc, dram, vt, qblk, kh, lambda pool: None)
                mlstm_heads(nc, dram, vt, qblk, kh, aT, eT, lambda pool: None)
        if phases < 5:
            return
        experts_top2(nc, dram)


def kernel(phases=9, **a):
    import concourse.bacc as _bacc
    from concourse.bass_utils import run_bass_kernel_spmd as _run

    a = {k: np.asarray(v) for k, v in a.items()}

    def kmajor(m):
        return m.reshape(KT, P, -1).transpose(1, 0, 2)

    def tokens_T(m):
        return m.transpose(0, 2, 1).reshape(B, KT, P, S).transpose(0, 2, 1, 3)

    arrays = {
        "x": a["x"], "xT": tokens_T(a["x"]), "cT": tokens_T(a["ctx_1024"]), "ctx": a["ctx_1024"],
        "w": np.stack([kmajor(m) for m in (
            a["L0_attn_Wq"].T, a["L0_attn_Wk"].T, a["L0_attn_Wv"].T, a["L0_attn_Wo"].T,
            a["L0_xattn_Wq"], a["L0_xattn_Wk"], a["L0_xattn_Wv"], a["L0_xattn_Wp"],
            a["L1_attn_Wq"].T, a["L1_attn_Wk"].T, a["L1_attn_Wv"].T)], axis=1),
        "cols": np.stack([m.reshape(2, P).T for m in (
            a["L0_xattn_bq"], a["L0_xattn_bk"], a["L1_attn_bq"], a["L1_attn_bk"])] + [head_masks()], axis=1),
        "rows": np.broadcast_to(np.stack([
            a["L0_xattn_bv"], a["L0_xattn_bp"], a["L1_attn_bv"], a["L1_xattn_ln_w"], a["L1_xattn_ln_b"],
            a["L1_ffn_bs2"]]), (P, 6, D)),
        "hopsT": hop_units(a["itok_SxS2_0_2016"]), "rpe": a["L1_xattn_rpe"],
        "wg": kmajor(a["L0_ffn_Wg"]), "before": np.triu(np.ones((P, P), np.float32), 1),
        "route": routing_constants(a["L0_ffn_bg"]),
        "w1": a["L0_ffn_W1"].reshape(NE, KT, P, HID).transpose(0, 2, 1, 3),
        "w2": a["L0_ffn_W2"].reshape(NE, HT, P, D).transpose(0, 2, 1, 3),
        "b1": a["L0_ffn_b1"].reshape(NE, HT, P).transpose(0, 2, 1), "b2": a["L0_ffn_b2"],
        "cols1": np.stack([m.reshape(2, P).T for m in (
            a["L1_attn_bq"], a["L1_attn_bk"], pair_swapped(a["L1_attn_bq"]), pair_swapped(a["L1_attn_bk"]),
            pair_signs())], axis=1),
        "rope": rope_tables(),
        "gw": np.concatenate([a["L1_xattn_igate_w"], a["L1_xattn_fgate_w"]]).T.reshape(6, P, 16).transpose(1, 0, 2),
        "gb": np.concatenate([a["L1_xattn_igate_b"], a["L1_xattn_fgate_b"]])[:, None],
        "ctx_ones": values_with_ones(a["ctx_1024"]),
        "gate1": kmajor(a["L1_ffn_gate_W"]), "rscale": np.broadcast_to(a["L1_ffn_route_scale"].reshape(1, 1), (P, 1)),
        "iota8m": np.broadcast_to((np.arange(NE) - NE).astype(np.float32), (P, QT, NE)),
        "f_w1": np.concatenate([a["L1_ffn_W1"], a["L1_ffn_Ws1"][None]]).reshape(NE + 1, KT, P, HID1)
        .transpose(2, 1, 0, 3),
        "f_w2": np.concatenate([a["L1_ffn_W2"], a["L1_ffn_Ws2"][None]]).transpose(1, 0, 2),
        "f_b1": np.concatenate([a["L1_ffn_b1"], a["L1_ffn_bs1"][None]]).T, "f_b2": a["L1_ffn_b2"],
        "masks": window_masks(), "ident": np.eye(P, dtype=np.float32),
    }
    nc = _bacc.Bacc("TRN2", target_bir_lowering=False, num_devices=1)
    dram, given = {}, {}
    for name, m in arrays.items():
        m = np.ascontiguousarray(m)
        given["in_" + name] = m
        dram[name] = nc.dram_tensor("in_" + name, m.shape, mybir.dt.from_np(m.dtype), kind="ExternalInput").ap()
    dram["out"] = nc.dram_tensor("out", (B, S, D), F32, kind="ExternalOutput").ap()
    for name, shape in (("x2", (B, S, D)), ("x3", (B, S, D)), ("xs", (TILES * P, D)), ("ys", (TILES * P, D)),
                        ("x4", (B, S, D)), ("x4T", (B, P, KT, S)), ("gate_i", (B, 8, S)), ("gate_f", (B, 8, S)), ("x5", (B, S, D)),
                        ("runmax", (BH, S))):
        dram[name] = nc.dram_tensor(name, shape, F32, kind="Internal").ap()
    dram[{1: "x2", 2: "x3", 3: "x4", 4: "x5"}.get(phases, "nothing")] = dram["out"]
    dram["pos_rows"] = nc.dram_tensor("pos_rows", (GROUPS, P, GROUP * D), F32, kind="Internal").ap()
    build(nc, dram, phases)
    r = _run(nc, [given], core_ids=[0])
    return r.results[0]["out"]


def head_masks():
    odd = (np.arange(P) // HD) % 2
    return (np.stack([1 - odd, odd], axis=1) / np.sqrt(HD)).astype(np.float32)


def window_masks():
    q, k = np.arange(P)[:, None], np.arange(P)[None, :]
    first = np.where((k <= q) & (k > q - WINDOW), 0.0, NEG)
    q, k = q + P, np.arange(64, 256)[None, :]
    second = np.where((k <= q) & (k > q - WINDOW), 0.0, NEG)
    return np.concatenate([first] * 4 + [second] * 2, axis=1).astype(np.float32)


def hop_units(hops):
    t = hops.T.reshape(2, P, S)
    late = t[:, :, P:].transpose(1, 2, 0).reshape(P, 2 * P)
    return np.concatenate([t[0, :, :P], late], axis=1)


def routing_constants(bg):
    row = np.concatenate([
        np.tile(np.arange(NE) - NE, TT), np.tile(bg, TT), np.tile(np.arange(TT) * P, NE),
        np.repeat(np.arange(TILES), NE)]).astype(np.float32)
    return np.broadcast_to(row, (P, row.size))


def pair_swapped(v):
    return v.reshape(-1, 2)[:, ::-1].reshape(-1)


def pair_signs():
    return np.tile(np.array([-1.0, 1.0], np.float32), D // 2)


def rope_tables():
    head = 128
    pos = np.arange(S, dtype=np.float32)
    inv = np.power(np.float32(10000.0), np.arange(0, head, 2, dtype=np.float32) / np.float32(head))
    rad = pos[:, None] / inv
    t = np.repeat(np.stack((np.sin(rad), np.cos(rad)), axis=-1).reshape(S, -1), 2, axis=-1)
    t = t.T.reshape(KT, P, S).transpose(1, 0, 2)
    return np.stack([t, t / np.float32(np.sqrt(head))], axis=1).astype(np.float32)


def values_with_ones(ctx):
    v = ctx.reshape(B, 2, P, H1, HW).transpose(0, 2, 1, 3, 4)
    return np.concatenate([v, np.ones(v.shape[:-1] + (1,), v.dtype)], axis=-1).reshape(B, P, 2, H1 * (HW + 1))
```

```python
from contextlib import ExitStack

import numpy as np

import concourse.bass as bass
from concourse import mybir

ALU = mybir.AluOpType
ACT = mybir.ActivationFunctionType
AX = mybir.AxisListType
F32 = mybir.dt.float32
BF16 = mybir.dt.bfloat16
I32 = mybir.dt.int32
U32 = mybir.dt.uint32

P = 128
B = 8
S = 256
D = 256
KT = D // P
QT = S // P
NH = 16
HD = D // NH
WINDOW = 64
LN_EPS = 1e-5
NEG = -1.0e30

WQ0, WK0, WV0, WO0, XQ, XK, XV, XP, WQ1, WK1, WV1 = range(11)
C_BQ, C_BK, C_B1Q, C_B1K = range(4)
R_BV, R_BP, R_B1V, R_LNW, R_LNB, R_BS2 = range(6)


class Count:

    def __init__(self, engine, sem, per_pass, base):
        self.engine, self.sem, self.per_pass, self.base, self.n = engine, sem, per_pass, base, 0

    def link(self, ins):
        ins.then_inc(self.sem, 1)
        self.n += 1
        self.engine.wait_ge(self.sem, self.base + self.n)

    def end(self):
        assert self.n == self.per_pass, self.n


def phase_semaphores(nc, ctx, prefix):
    made = []

    def sem(name):
        made.append(nc.alloc_semaphore(prefix + name))
        return made[-1]

    def clear():
        nc.clear_and_free_semaphores(made)
        nc.all_engine_barrier(sem_only=True)

    ctx.callback(clear)
    return sem


def units():
    out = []
    for g in range(4):
        out.append(dict(layer=0, qt=0, g=g, heads=[(t, par) for t in range(2) for par in range(2)], k0=0, nk=128))
    for t in range(2):
        for g in range(4):
            out.append(dict(layer=0, qt=1, g=g, heads=[(t, 0), (t, 1)], k0=64, nk=192))
    for qt in range(QT):
        for t in range(2):
            for g in range(4):
                out.append(dict(layer=1, qt=qt, g=g, heads=[(t, 0), (t, 1)], k0=0, nk=256))
    return out


UNITS = units()
NU = len(UNITS)
NU0 = 12
LAST_OF = {0: NU0 - 1, 1: NU - 1}
ON_ACT = [u for u in range(NU) if u % 4 == 3]
STEPS = 9


NPROBS = 3


def head_of(t, g, par):
    return 8 * t + 2 * g + par


def layer0_attention(nc, dram, pool_share):
    with ExitStack() as ctx:
        def sb(name, shape, dt=F32):
            return ctx.enter_context(nc.sbuf_tensor("a_" + name, shape, dt))

        sem = phase_semaphores(nc, ctx, "a_")

        w = sb("w", [P, 8, KT, D])
        cols = sb("cols", [P, 4, 2])
        rows = sb("rows", [P, 2, D])
        ident = sb("ident", [P, P])
        identb = sb("identb", [P, P], BF16)
        mask0 = sb("mask0", [P, 4, 128], BF16)
        mask1 = sb("mask1", [P, 2, 192], BF16)
        maskf = sb("maskf", [P, 4 * 128 + 2 * 192])
        eps = sb("eps", [P, 1])
        xT = sb("xT", [P, KT, S])
        cT = sb("cT", [P, KT, S])
        xin = sb("xin", [P, QT, D])
        kT = [sb(f"kT{i}", [P, 2, S]) for i in range(2)]
        masks8 = sb("masks8", [P, 8])
        qT = sb("qT", [P, 2, S])
        qm = [sb(f"qm{m}", [P, 2, S]) for m in range(8)]
        v = [sb(f"v{i}", [P, QT, NH, 2 * HD]) for i in range(2)]
        probs = [sb(f"probs{i}", [P, 512]) for i in range(NPROBS)]
        probs_w = [sb(f"probs_w{i}", [P, 2, 256]) for i in range(NPROBS)]
        probsT = [sb(f"probsT{i}", [P, 4, P]) for i in range(2)]
        negmax = sb("negmax", [P, 4, 4])
        rsum = sb("rsum", [P, QT, NH])
        rinv = sb("rinv", [P, QT, NH])
        oT = sb("oT", [P, KT, S])
        y = sb("y", [P, QT, D])
        x1 = sb("x1", [P, QT, D])
        x1T = sb("x1T", [P, KT, S])
        x2 = sb("x2", [P, QT, D])
        st = sb("st", [P, QT, 6])
        mv = sb("mv", [P, QT, 2])
        lnv = sb("lnv", [P, QT])
        rstd = sb("rstd", [P, QT])
        sc = [ctx.enter_context(nc.psum_tensor(f"a_sc{i}", [P, 512], F32)) for i in range(4)]
        pt = [ctx.enter_context(nc.psum_tensor(f"a_pt{i}", [P, 512], F32)) for i in range(2)]
        op = ctx.enter_context(nc.psum_tensor("a_op", [P, 512], F32))
        mi = ctx.enter_context(nc.psum_tensor("a_mi", [P, 2, 256], F32))

        zeros = sb("zeros", [P, TILES * D // 4])
        s_zeroed = sem("zeroed")
        s_const = sem("const")
        s_maskb = sem("maskb")
        s_zero = sem("zero")
        s_xT = sem("xT")
        s_xin = sem("xin")
        s_cT = sem("cT")
        s_step = sem("step")
        s_copied = sem("copied")
        s_scores = sem("scores")
        s_max = sem("max")
        s_exp = sem("exp")
        s_turned = sem("turned")
        s_evac_dve = sem("evac_dve")
        s_evac_act = sem("evac_act")
        s_pv = sem("pv")
        s_rinv = sem("rinv")
        s_qm = sem("qm")
        s_norm = sem("norm")
        s_oT = sem("oT")
        s_stats = sem("stats")
        s_rstd = sem("rstd")
        s_x1 = sem("x1")
        s_x2 = sem("x2")
        s_x2_out = sem("x2_out")
        s_x2_free = sem("x2_free")
        s_dve = sem("dve")
        s_act = sem("act")
        block = ctx.enter_context(nc.Block())

        n_act, n_dve = len(ON_ACT), NU - len(ON_ACT)

        def wait_evac(eng, b, u):
            if u in ON_ACT:
                eng.wait_ge(s_evac_act, b * n_act + ON_ACT.index(u) + 1)
            else:
                before = len([x for x in range(u) if x not in ON_ACT])
                eng.wait_ge(s_evac_dve, b * n_dve + before + 1)

        @block.sync
        def _(sp):
            sp.dma_start(ident[:], dram["ident"]).then_inc(s_const, 16)
            sp.dma_start(w[:, 0:4], dram["w"][:, 0:4]).then_inc(s_const, 16)
            sp.dma_start(cols[:], dram["cols"]).then_inc(s_const, 16)
            sp.dma_start(masks8[:], dram["masks8"]).then_inc(s_const, 16)
            sp.dma_start(xT[:], dram["xT"][0]).then_inc(s_xT, 16)
            sp.dma_start(maskf[:], dram["masks"]).then_inc(s_const, 16)
            sp.dma_start(xin[:], dram["x"][0].rearrange("(t p) d -> p t d", p=P)).then_inc(s_xin, 16)
            sp.dma_start(w[:, 4:8], dram["w"][:, 4:8]).then_inc(s_const, 16)
            sp.dma_start(rows[:], dram["rows"][:, 0:2]).then_inc(s_const, 16)
            sp.dma_start(cT[:], dram["cT"][0]).then_inc(s_cT, 16)
            sp.wait_ge(s_zero, 1)
            for i in range(4):
                sp.dma_start(dram["xs"].rearrange("(p r) d -> p (r d)", p=P)[:, i * zeros.shape[1]:(i + 1) * zeros.shape[1]],
                             zeros[:]).then_inc(s_zeroed, 16)

            def store(b):
                sp.wait_ge(s_x2, b + 1)
                sp.dma_start(dram["x2"][bass.ds(b, 1)].rearrange("b (t p) d -> p (b t) d", p=P),
                             x2[:]).then_inc(s_x2_out, 16)

            with sp.Fori(0, B - 1) as b:
                sp.wait_ge(s_step, b * STEPS + 3)
                sp.dma_start(xT[:], dram["xT"][bass.ds(b + 1, 1)].rearrange("b p k s -> p (b k) s"))\
                    .then_inc(s_xT, 16)
                sp.wait_ge(s_copied, b * STEPS + 5)
                sp.dma_start(xin[:], dram["x"][bass.ds(b + 1, 1)].rearrange("b (t p) d -> p (b t) d", p=P))\
                    .then_inc(s_xin, 16)
                sp.wait_ge(s_step, b * STEPS + 6)
                sp.dma_start(cT[:], dram["cT"][bass.ds(b + 1, 1)].rearrange("b p k s -> p (b k) s"))\
                    .then_inc(s_cT, 16)
                store(b)
                sp.wait_ge(s_x2_out, 16 * b + 16)
                sp.sem_inc(s_x2_free, 1)
            store(B - 1)
            sp.wait_ge(s_x2_out, 16 * B)
            sp.wait_ge(s_zeroed, 64)

        @block.gpsimd
        def _(pool):
            pool.memset(zeros[:], 0.0).then_inc(s_zero, 1)
            for i in range(NPROBS):
                pool.memset(probs_w[i][:, :, 0:64], 0.0).then_inc(s_zero, 1)
            for i in range(2):
                pool.memset(v[i][:], 0.0).then_inc(s_zero, 1)
            pool_share(pool)

        @block.scalar
        def _(act):
            act.preload_act_table_set("natural_log_exp_and_others")
            act.wait_ge(s_zero, NPROBS + 3)

            def exps(b, u):
                un = UNITS[u]
                act.wait_ge(s_max, b * NU + u + 1)
                if u >= NPROBS:
                    act.wait_ge(s_turned, b * NU + u - NPROBS + 1)
                for j, (t, par) in enumerate(un["heads"]):
                    h = head_of(t, un["g"], par)
                    if un["layer"] == 0 and un["qt"] == 1:
                        dst = probs_w[u % NPROBS][:, j, 64:256]
                    else:
                        dst = probs[u % NPROBS][:, j * un["nk"]:(j + 1) * un["nk"]]
                    ins = act.activation(dst, sc[u % 4][:, j * un["nk"]:(j + 1) * un["nk"]], ACT.Exp,
                                         bias=negmax[:, u % 4, j:j + 1],
                                         accum_out=rsum[:, un["qt"], h:h + 1])
                ins.then_inc(s_exp, 1)

            def evac(b, u):
                act.wait_ge(s_turned, b * NU + u + 1)
                if u >= 2:
                    act.wait_ge(s_pv, b * NU + u - 1)
                act.copy(probsT[u % 2][:], pt[u % 2][:]).then_inc(s_evac_act, 1)

            def layer(b, us):
                for u in list(us) + [None]:
                    if u is not None:
                        exps(b, u)
                    before = us[-1] if u is None else u - 1
                    if before in ON_ACT and before >= us[0]:
                        evac(b, before)

            def step(b, n):
                act.wait_ge(s_step, b * STEPS + n + 1)

            def rsqrt(b, n):
                act.wait_ge(s_stats, 2 * b + n + 1)
                act.activation(lnv[:], mv[:, :, 1], ACT.Ln, bias=eps[:]).then_inc(s_act, 1)
                act.wait_ge(s_act, 2 * b + n + 1)
                act.activation(rstd[:], lnv[:], ACT.Exp, scale=-0.5).then_inc(s_rstd, 1)

            def outputs(b, n):
                act.wait_ge(s_pv, b * NU + LAST_OF[n] + 1)
                act.copy(oT[:], op[:]).then_inc(s_oT, 1)

            def pairs(ap, par):
                return ap[:, :, par::2, par * HD:(par + 1) * HD]

            with act.Fori(0, B) as b:
                step(b, 0)
                act.copy(kT[0][:], mi[:]).then_inc(s_copied, 1)
                step(b, 2)
                heads = mi[:].rearrange("p t (h d) -> p t h d", d=HD)
                act.copy(pairs(v[0], 0), heads[:, :, 0::2])
                act.copy(pairs(v[0], 1), heads[:, :, 1::2]).then_inc(s_copied, 1)
                layer(b, range(NU0))
                outputs(b, 0)
                step(b, 4)
                act.activation(kT[1][:, 0], mi[:, 0], ACT.Identity, bias=cols[:, C_BK, 0:1])
                act.activation(kT[1][:, 1], mi[:, 1], ACT.Identity, bias=cols[:, C_BK, 1:2])\
                    .then_inc(s_copied, 1)
                rsqrt(b, 0)
                step(b, 6)
                act.copy(x1T[:], mi[:]).then_inc(s_copied, 1)
                layer(b, range(NU0, NU))
                outputs(b, 1)
                rsqrt(b, 1)

        @block.tensor
        def _(pe):
            pe.wait_ge(s_const, 16 * 7)
            pe.wait_ge(s_maskb, 4)

            def free(b, n):
                pe.wait_ge(s_copied, b * STEPS + n + 1)

            def project_T(b, n, wi, src):
                free(b, n)
                for et in range(2):
                    for k in range(KT):
                        ins = pe.matmul(mi[:, et], w[:, wi, k, et * P:(et + 1) * P], src[:, k, :],
                                        start=(k == 0), stop=(k == KT - 1))
                ins.then_inc(s_step, 1)

            def project(b, n, wi, srcT):
                free(b, n)
                for qt in range(QT):
                    for k in range(KT):
                        ins = pe.matmul(mi[:, qt], srcT[:, k, qt * P:(qt + 1) * P], w[:, wi, k, :],
                                        start=(k == 0), stop=(k == KT - 1))
                ins.then_inc(s_step, 1)

            def turn(b, n, src):
                free(b, n)
                for k in range(KT):
                    for qt in range(QT):
                        ins = pe.transpose(mi[:, k, qt * P:(qt + 1) * P], src[:, qt, k * P:(k + 1) * P], ident[:])
                ins.then_inc(s_step, 1)

            def scores(b, u):
                un = UNITS[u]
                L, g, nk, qt = un["layer"], un["g"], un["nk"], un["qt"]
                bank = sc[u % 4]
                if u >= 4:
                    pe.wait_ge(s_exp, b * NU + u - 3)
                if L == 0:
                    mask = mask0 if qt == 0 else mask1
                    width = len(un["heads"]) * nk
                    pe.matmul(bank[:, 0:width], identb[:], mask[:].rearrange("p h k -> p (h k)"),
                              start=True, stop=True, skip_group_check=True)
                if u in (0, 1, 2, 3) or u - NU0 in (0, 1, 2, 3):
                    pe.wait_ge(s_qm, b * 16 + L * 8 + 2 * g + 2)
                for j, (t, par) in enumerate(un["heads"]):
                    ins = pe.matmul(bank[:, j * nk:(j + 1) * nk],
                                    qm[2 * g + par][:, t, qt * P:(qt + 1) * P], kT[L][:, t, un["k0"]:un["k0"] + nk],
                                    start=(L == 1), stop=True, skip_group_check=True)
                ins.then_inc(s_scores, 1)

            def transposes(b, u):
                un = UNITS[u]
                pe.wait_ge(s_norm, b * NU + u + 1)
                if u >= 2:
                    wait_evac(pe, b, u - 2)
                if un["layer"] == 0 and un["qt"] == 1:
                    src = probs_w[u % NPROBS][:].rearrange("p h k -> p (h k)")
                else:
                    src = probs[u % NPROBS][:]
                for c in range(4):
                    ins = pe.transpose(pt[u % 2][:, c * P:(c + 1) * P], src[:, c * P:(c + 1) * P], ident[:])
                ins.then_inc(s_turned, 1)

            def pv(b, u):
                un = UNITS[u]
                wait_evac(pe, b, u)
                nc_ = 1 if un["nk"] == 128 else 2
                g = un["g"]
                for j, (t, par) in enumerate(un["heads"]):
                    at = t * S + un["qt"] * P
                    for c in range(nc_):
                        ins = pe.matmul(op[32 * g:32 * g + 32, at:at + P],
                                        v[un["layer"]][:, c, head_of(t, g, par), :],
                                        probsT[u % 2][:, j * nc_ + c, :],
                                        start=(par == 0 and c == 0), stop=(par == 1 and c == nc_ - 1),
                                        skip_group_check=True)
                ins.then_inc(s_pv, 1)

            def layer(b, us):
                n = len(us)
                for i in range(3):
                    scores(b, us[i])
                for i in range(n + 2):
                    if i + 3 < n:
                        scores(b, us[i + 3])
                    if i < n:
                        transposes(b, us[i])
                    if i >= 2:
                        pv(b, us[i - 2])

            with pe.Fori(0, B) as b:
                pe.wait_ge(s_xT, 16 * b + 16)
                project_T(b, 0, WK0, xT)
                project_T(b, 1, WQ0, xT)
                project(b, 2, WV0, xT)
                free(b, 3)
                layer(b, range(NU0))
                pe.wait_ge(s_oT, 2 * b + 1)
                project(b, 3, WO0, oT)
                pe.wait_ge(s_cT, 16 * b + 16)
                project_T(b, 4, XK, cT)
                project(b, 5, XV, cT)
                pe.wait_ge(s_x1, b + 1)
                turn(b, 6, x1)
                free(b, 7)
                project_T(b, 7, XQ, x1T)
                free(b, 8)
                layer(b, range(NU0, NU))
                pe.wait_ge(s_oT, 2 * b + 2)
                project(b, 8, XP, oT)

        @block.vector
        def _(dve):
            dve.memset(eps[:], LN_EPS).then_inc(s_maskb, 1)
            dve.sem_inc(s_copied, 1)
            dve.sem_inc(s_x2_free, 1)
            dve.wait_ge(s_const, 16 * 7)
            dve.tensor_copy(mask0[:].rearrange("p h k -> p (h k)"), maskf[:, 0:512]).then_inc(s_maskb, 1)
            dve.tensor_copy(mask1[:].rearrange("p h k -> p (h k)"), maskf[:, 512:896]).then_inc(s_maskb, 1)
            dve.tensor_copy(identb[:], ident[:]).then_inc(s_maskb, 1)

            def row_max(b, u):
                un = UNITS[u]
                n = len(un["heads"])
                dve.wait_ge(s_scores, b * NU + u + 1)
                dve.tensor_reduce(negmax[:, u % 4, 0:n],
                                  sc[u % 4][:, 0:n * un["nk"]].rearrange("p (h k) -> p h k", h=n),
                                  AX.X, ALU.max, negate=True).then_inc(s_max, 1)

            def evac(b, u):
                dve.wait_ge(s_turned, b * NU + u + 1)
                if u >= 2:
                    dve.wait_ge(s_pv, b * NU + u - 1)
                dve.tensor_copy(probsT[u % 2][:].rearrange("p h k -> p (h k)"), pt[u % 2][:])\
                    .then_inc(s_evac_dve, 1)

            def normalise(b, u):
                un = UNITS[u]
                hs = [head_of(t, un["g"], par) for t, par in un["heads"]]
                dve.wait_ge(s_exp, b * NU + u + 1)
                r = rsum[:, un["qt"]].rearrange("p (t h) -> p t h", t=2)
                ri = rinv[:, un["qt"]].rearrange("p (t h) -> p t h", t=2)
                g, (t0, t1) = un["g"], (un["heads"][0][0], un["heads"][-1][0] + 1)
                dve.reciprocal(ri[:, t0:t1, 2 * g:2 * g + 2], r[:, t0:t1, 2 * g:2 * g + 2]).then_inc(s_rinv, 1)
                dve.wait_ge(s_rinv, b * NU + u + 1)
                for j, h in enumerate(hs):
                    if un["layer"] == 0 and un["qt"] == 1:
                        p = probs_w[u % NPROBS][:, j, 64:256]
                    else:
                        p = probs[u % NPROBS][:, j * un["nk"]:(j + 1) * un["nk"]]
                    ins = dve.tensor_scalar(p, p, rinv[:, un["qt"], h:h + 1], None, ALU.mult)
                ins.then_inc(s_norm, 1)

            def layer(b, us):
                n = len(us)
                for i in range(n + 2):
                    if i < n:
                        row_max(b, us[i])
                    if 1 <= i <= n:
                        normalise(b, us[i - 1])
                    if i >= 2 and us[i - 2] not in ON_ACT:
                        evac(b, us[i - 2])

            def mask_queries(b, L):
                for m in range(8):
                    dve.tensor_scalar(qm[m][:], qT[:], masks8[:, m:m + 1], None, ALU.mult).then_inc(s_qm, 1)

            def statistics(b, n, chain):
                dve.bn_stats(st[:, 0], y[:, 0])
                chain.link(dve.bn_stats(st[:, 1], y[:, 1]))
                dve.nop(nofuse=True)
                dve.bn_aggr(mv[:, 0], st[:, 0])
                dve.bn_aggr(mv[:, 1], st[:, 1]).then_inc(s_stats, 1)

            def scaled(b, n, dst, done):
                dve.wait_ge(s_rstd, 2 * b + n + 1)
                dve.wait_ge(s_stats, 2 * b + n + 1)
                for qt in range(QT):
                    ins = dve.tensor_scalar(dst[:, qt], y[:, qt], mv[:, qt, 0:1], rstd[:, qt:qt + 1],
                                            ALU.subtract, ALU.mult)
                ins.then_inc(done, 1)

            with dve.Fori(0, B) as b:
                chain = Count(dve, s_dve, 3, b * 3)
                dve.wait_ge(s_step, b * STEPS + 2)
                dve.tensor_copy(qT[:], mi[:]).then_inc(s_copied, 1)
                dve.wait_ge(s_copied, b * STEPS + 3)
                mask_queries(b, 0)
                layer(b, range(NU0))
                dve.wait_ge(s_step, b * STEPS + 4)
                dve.wait_ge(s_xin, 16 * b + 16)
                dve.tensor_tensor(y[:], mi[:], xin[:], ALU.add).then_inc(s_copied, 1)
                dve.wait_ge(s_copied, b * STEPS + 5)
                statistics(b, 0, chain)
                dve.wait_ge(s_step, b * STEPS + 6)
                for par in range(2):
                    own = rows[:, 0].rearrange("p (h d) -> p h d", d=HD)[:, par::2]
                    ins = dve.tensor_tensor(
                        v[1][:, :, par::2, par * HD:(par + 1) * HD],
                        mi[:].rearrange("p t (h d) -> p t h d", d=HD)[:, :, par::2],
                        own.unsqueeze(1).broadcast_to([P, QT, NH // 2, HD]), ALU.add)
                ins.then_inc(s_copied, 1)
                scaled(b, 0, x1, s_x1)
                dve.wait_ge(s_step, b * STEPS + 8)
                for et in range(2):
                    ins = dve.tensor_scalar(qT[:, et], mi[:, et], cols[:, C_BQ, et:et + 1], None, ALU.add)
                ins.then_inc(s_copied, 1)
                dve.wait_ge(s_copied, b * STEPS + 9)
                mask_queries(b, 1)
                layer(b, range(NU0, NU))
                chain.link(dve.tensor_tensor(x1[:], x1[:], rows[:, 1].unsqueeze(1).broadcast_to([P, QT, D]), ALU.add))
                dve.wait_ge(s_step, b * STEPS + 9)
                dve.tensor_tensor(y[:], mi[:], x1[:], ALU.add).then_inc(s_copied, 1)
                dve.wait_ge(s_copied, b * STEPS + 10)
                statistics(b, 1, chain)
                dve.wait_ge(s_x2_free, b + 1)
                scaled(b, 1, x2, s_x2)
                chain.end()


GROUP = 4
UNITS_R = P + 2 * P
GROUPS = UNITS_R // GROUP


class TableRows:

    def __init__(self, nc, ctx, dram):
        self.nc, self.dram = nc, dram
        self.idx = ctx.enter_context(nc.sbuf_tensor("r_idx", [P, UNITS_R], I32))
        self.cur = [ctx.enter_context(nc.sbuf_tensor(f"r_cur{i}", [P, GROUP], I32)) for i in range(2)]
        self.buf = [ctx.enter_context(nc.sbuf_tensor(f"r_buf{i}", [P, GROUP, D], F32)) for i in range(2)]
        self.s_idx = ctx.enter_context(nc.semaphore("r_idx_loaded"))
        self.s_cur = [ctx.enter_context(nc.semaphore(f"r_cur_ready{i}")) for i in range(2)]
        self.s_got = [ctx.enter_context(nc.semaphore(f"r_got{i}")) for i in range(2)]
        self.s_sent = [ctx.enter_context(nc.semaphore(f"r_sent{i}")) for i in range(2)]

    def start(self, pool):
        pool.dma_start(self.idx[:], self.dram["hopsT"]).then_inc(self.s_idx, 16)
        pool.wait_ge(self.s_idx, 16)

    def group(self, pool, g, i, first=False):
        turn = g // 2
        if not first:
            pool.wait_ge(self.s_sent[i], turn * 16)
        pool.tensor_copy(self.cur[i][:], self.idx[:, bass.ds(g * GROUP, GROUP)]).then_inc(self.s_cur[i], 1)
        pool.wait_ge(self.s_cur[i], turn + 1)
        pool.nop(nofuse=True)
        for j in range(GROUP):
            pool.indirect_dma_start(
                out=self.buf[i][:, j, :], out_offset=None, in_=self.dram["rpe"],
                in_offset=bass.IndirectOffsetOnAxis(ap=self.cur[i][:, j:j + 1], axis=0))\
                .then_inc(self.s_got[i], 16)

    def send(self, pool, g, i):
        pool.wait_ge(self.s_got[i], (g // 2 + 1) * 16 * GROUP)
        pool.dma_start(self.dram["pos_rows"][bass.ds(g, 1)].rearrange("g p n -> p (g n)"),
                       self.buf[i][:].rearrange("p j d -> p (j d)")).then_inc(self.s_sent[i], 16)

    def share(self, first, last):
        def run(pool):
            lo = first
            if first == 0:
                self.start(pool)
                self.group(pool, 0, 0, True)
                self.group(pool, 1, 1, True)
                self.send(pool, 0, 0)
                self.send(pool, 1, 1)
                lo = 1
            with pool.Fori(lo, last) as t:
                self.group(pool, 2 * t, 0)
                self.group(pool, 2 * t + 1, 1)
                self.send(pool, 2 * t, 0)
                self.send(pool, 2 * t + 1, 1)
        return run


NE = 8
HID = 1024
HT = HID // P
TT = B * QT
TILES = TT + NE - 1
NEG_BIG = 1.0e30


def first_max_onehot(dve, link, lg, mx, t8, low, onehot, iota8m):
    shape = [P, TT, NE]
    link(dve.tensor_reduce(mx, lg, AX.X, ALU.max))
    link(dve.tensor_tensor(t8, lg, mx.unsqueeze(2).broadcast_to(shape), ALU.is_equal))
    link(dve.tensor_tensor(t8, t8, iota8m, ALU.mult))
    link(dve.tensor_reduce(low, t8, AX.X, ALU.min))
    link(dve.tensor_tensor(onehot, iota8m, low.unsqueeze(2).broadcast_to(shape), ALU.is_equal))


def moe_route(nc, dram, x2, pos, te, wtop, pool_share):
    with ExitStack() as ctx:
        def sb(name, shape, dt=F32):
            return ctx.enter_context(nc.sbuf_tensor("b_" + name, shape, dt))

        sem = phase_semaphores(nc, ctx, "b_")

        ident = sb("ident", [P, P])
        before = sb("before", [P, P])
        ones = sb("ones", [P, P])
        wg = sb("wg", [P, KT, NE])
        consts = sb("consts", [P, 3 * TT * NE + NE * TILES])
        iota8m = consts[:, 0:TT * NE].rearrange("p (t e) -> p t e", e=NE)
        bg = consts[:, TT * NE:2 * TT * NE].rearrange("p (t e) -> p t e", e=NE)
        steps = consts[:, 2 * TT * NE:3 * TT * NE].rearrange("p (e j) -> p e j", e=NE)
        tile_no = consts[:, 3 * TT * NE:].rearrange("p (i e) -> p i e", e=NE)
        xT = [sb(f"xT{i}", [P, KT, 4, P]) for i in range(2)]
        lg = sb("lg", [P, TT, NE])
        mx = sb("mx", [P, TT])
        t8 = sb("t8", [P, TT, NE])
        low = sb("low", [P, TT])
        onehot = sb("onehot", [P, TT, NE])
        ex = sb("ex", [P, TT, NE])
        z = sb("z", [P, TT])
        run = [sb(f"run{i}", [P, TT, NE]) for i in range(2)]
        tot = sb("tot", [P, TT, NE])
        need = sb("need", [P, NE])
        cum = [sb(f"cum{i}", [P, NE]) for i in range(2)]
        base = sb("base", [P, NE])
        posf = sb("posf", [P, TT])
        tmpi = sb("tmpi", [P, TILES, NE])
        tef = sb("tef", [P, TILES])
        pt = [ctx.enter_context(nc.psum_tensor(f"b_pt{i}", [P, 4, P], F32)) for i in range(4)]
        pl = ctx.enter_context(nc.psum_tensor("b_pl", [P, TT, NE], F32))
        pr = ctx.enter_context(nc.psum_tensor("b_pr", [P, TT, NE], F32))
        pc = ctx.enter_context(nc.psum_tensor("b_pc", [P, TT, NE], F32))

        s_in = sem("in")
        s_x = sem("x")
        s_turned = sem("turned")
        s_xT = [sem("xT_act"), sem("xT_dve")]
        s_logits = sem("logits")
        s_cent = sem("centred")
        s_ex = sem("ex")
        s_onehot = sem("onehot")
        s_ranks = sem("ranks")
        s_pos = sem("pos")
        s_te = sem("te")
        s_rows = sem("rows")
        s_dve = sem("dve")
        block = ctx.enter_context(nc.Block())

        @block.sync
        def _(sp):
            sp.dma_start(x2[:], dram["x2"].rearrange("b (t p) d -> p (b t) d", p=P)).then_inc(s_x, 16)
            sp.dma_start(ident[:], dram["ident"]).then_inc(s_in, 16)
            sp.dma_start(wg[:], dram["wg"]).then_inc(s_in, 16)
            sp.dma_start(before[:], dram["before"]).then_inc(s_in, 16)
            sp.dma_start(consts[:], dram["route"]).then_inc(s_in, 16)

        @block.tensor
        def _(pe):
            pe.wait_ge(s_in, 64)
            pe.wait_ge(s_x, 16)
            for q in range(4):
                if q >= 2:
                    pe.wait_ge(s_xT[0], q - 1)
                    pe.wait_ge(s_xT[1], q - 1)
                for k in range(KT):
                    for j in range(4):
                        ins = pe.transpose(pt[2 * (q % 2) + k][:, j], x2[:, 4 * q + j, k * P:(k + 1) * P], ident[:])
                ins.then_inc(s_turned, 1)
                pe.wait_ge(s_xT[0], q + 1)
                pe.wait_ge(s_xT[1], q + 1)
                for j in range(4):
                    for k in range(KT):
                        ins = pe.matmul(pl[:, 4 * q + j], xT[q % 2][:, k, j], wg[:, k], start=(k == 0),
                                        stop=(k == KT - 1), skip_group_check=True)
            ins.then_inc(s_logits, 1)
            pe.wait_ge(s_onehot, 1)
            pe.matmul(pr[:], before[:], onehot[:], start=True, stop=True)
            pe.matmul(pc[:], ones[:], onehot[:], start=True, stop=True).then_inc(s_ranks, 1)

        @block.scalar
        def _(act):
            for q in range(4):
                act.wait_ge(s_turned, q + 1)
                if q >= 2:
                    act.wait_ge(s_turned, q + 1)
                act.copy(xT[q % 2][:, 0], pt[2 * (q % 2)][:]).then_inc(s_xT[0], 1)
            act.wait_ge(s_cent, 1)
            act.activation(ex[:], ex[:], ACT.Exp).then_inc(s_ex, 1)

        @block.vector
        def _(dve):
            n = [0]

            def link(ins):
                ins.then_inc(s_dve, 1)
                n[0] += 1
                dve.wait_ge(s_dve, n[0])

            dve.memset(ones[:], 1.0)
            for q in range(4):
                dve.wait_ge(s_turned, q + 1)
                dve.tensor_copy(xT[q % 2][:, 1], pt[2 * (q % 2) + 1][:]).then_inc(s_xT[1], 1)
            dve.wait_ge(s_in, 64)
            dve.wait_ge(s_logits, 1)
            link(dve.tensor_tensor(lg[:], pl[:], bg, ALU.add))
            first_max_onehot(dve, link, lg[:], mx[:], t8[:], low[:], onehot[:], iota8m)
            dve.tensor_tensor(ex[:], lg[:], mx[:].unsqueeze(2).broadcast_to([P, TT, NE]), ALU.subtract)\
                .then_inc(s_cent, 1)
            dve.sem_inc(s_onehot, 1)
            dve.wait_ge(s_ex, 1)
            link(dve.tensor_reduce(z[:], ex[:], AX.X, ALU.add))
            dve.reciprocal(wtop, z[:])
            dve.wait_ge(s_ranks, 1)
            link(dve.tensor_copy(tot[:], pc[:]))
            src = tot
            for i, d in enumerate((1, 2, 4, 8)):
                dst = run[i % 2]
                dve.tensor_copy(dst[:, 0:d], src[:, 0:d])
                link(dve.tensor_tensor(dst[:, d:TT], src[:, d:TT], src[:, 0:TT - d], ALU.add))
                src = dst
            link(dve.tensor_tensor(t8[:].rearrange("p t e -> p (t e)").rearrange("p (e j) -> p e j", e=NE),
                                   src[:, TT - 1].unsqueeze(2).broadcast_to([P, NE, TT]), steps, ALU.is_gt))
            link(dve.tensor_reduce(need[:], t8[:].rearrange("p t e -> p (t e)").rearrange("p (e j) -> p e j", e=NE),
                                   AX.X, ALU.add))
            c = need
            for i, d in enumerate((1, 2, 4)):
                dst = cum[i % 2]
                dve.tensor_copy(dst[:, 0:d], c[:, 0:d])
                link(dve.tensor_tensor(dst[:, d:NE], c[:, d:NE], c[:, 0:NE - d], ALU.add))
                c = dst
            link(dve.tensor_tensor(tmpi[:], c[:].unsqueeze(1).broadcast_to([P, TILES, NE]), tile_no, ALU.is_le))
            link(dve.tensor_reduce(tef[:], tmpi[:], AX.X, ALU.add))
            link(dve.tensor_scalar(te, tef[:], float(NE - 1), None, ALU.min))
            link(dve.tensor_tensor(base[:], c[:], need[:], ALU.subtract))
            link(dve.tensor_scalar(base[:], base[:], float(P), None, ALU.mult))
            link(dve.tensor_tensor(t8[:], src[:], tot[:], ALU.subtract))
            link(dve.tensor_tensor(t8[:], t8[:], pr[:], ALU.add))
            link(dve.tensor_tensor(t8[:], t8[:], base[:].unsqueeze(1).broadcast_to([P, TT, NE]), ALU.add))
            link(dve.tensor_tensor(t8[:], t8[:], onehot[:], ALU.mult))
            link(dve.tensor_reduce(posf[:], t8[:], AX.X, ALU.add))
            dve.tensor_copy(pos, posf[:]).then_inc(s_pos, 1)

        @block.gpsimd
        def _(pool):
            pool.wait_ge(s_pos, 1)
            pool.wait_ge(s_x, 16)
            for t in range(TT):
                pool.indirect_dma_start(
                    out=dram["xs"], out_offset=bass.IndirectOffsetOnAxis(ap=pos[:, t:t + 1], axis=0),
                    in_=x2[:, t, :], in_offset=None).then_inc(s_rows, 16)
            pool.wait_ge(s_rows, 16 * TT)
            pool_share(pool)


def moe_experts(nc, dram, te, pool_share):
    with ExitStack() as ctx:
        def sb(name, shape, dt=F32):
            return ctx.enter_context(nc.sbuf_tensor("e_" + name, shape, dt))

        sem = phase_semaphores(nc, ctx, "e_")

        ident = sb("ident", [P, P])
        w1 = [sb(f"w1{i}", [P, KT, HID]) for i in range(2)]
        w2 = [sb(f"w2{i}", [P, HT, D]) for i in range(2)]
        b1 = [sb(f"b1{i}", [P, HT]) for i in range(2)]
        b2 = [sb(f"b2{i}", [P, D]) for i in range(2)]
        xs = [sb(f"xs{i}", [P, D]) for i in range(2)]
        xsT = [sb(f"xsT{i}", [P, KT, P]) for i in range(2)]
        h = [sb(f"h{i}", [P, HT, P]) for i in range(2)]
        ys = [sb(f"ys{i}", [P, D]) for i in range(2)]
        pt = ctx.enter_context(nc.psum_tensor("e_pt", [P, KT, P], F32))
        ph = [ctx.enter_context(nc.psum_tensor(f"e_ph{i}", [P, HT, P], F32)) for i in range(2)]
        po = [ctx.enter_context(nc.psum_tensor(f"e_po{i}", [P, D], F32)) for i in range(2)]

        s_in = sem("in")
        s_w1 = [sem(f"w1_{i}") for i in range(2)]
        s_b1 = [sem(f"b1_{i}") for i in range(2)]
        s_w2 = [sem(f"w2_{i}") for i in range(2)]
        s_turned = sem("turned")
        s_xsT = sem("xsT")
        s_half = sem("half")
        s_hid = sem("hid")
        s_silu = sem("silu")
        s_out = sem("out")
        s_ys = sem("ys")
        s_sent = [sem(f"sent{i}") for i in range(2)]
        block = ctx.enter_context(nc.Block())

        @block.sync
        def _(sp):
            sp.dma_start(ident[:], dram["ident"]).then_inc(s_in, 16)

            def load(i, p, first):
                e = sp.value_load(te[0:1, bass.ds(i, 1)], min_val=0, max_val=NE - 1)
                if not first:
                    sp.wait_ge(s_hid, i - 1)
                    sp.wait_ge(s_turned, i - 1)
                sp.dma_start(w1[p][:], dram["w1"][bass.ds(e, 1)].rearrange("e p k h -> p (e k) h")).then_inc(s_w1[p], 16)
                sp.dma_start(xs[p][:], dram["xs"][bass.ds(i * P, P), :]).then_inc(s_w1[p], 16)
                if not first:
                    sp.wait_ge(s_silu, i - 1)
                sp.dma_start(b1[p][:], dram["b1"][bass.ds(e, 1)].rearrange("e p h -> p (e h)")).then_inc(s_b1[p], 16)
                if not first:
                    sp.wait_ge(s_ys, i - 1)
                sp.dma_start(w2[p][:], dram["w2"][bass.ds(e, 1)].rearrange("e p k h -> p (e k) h")).then_inc(s_w2[p], 16)
                sp.dma_start(b2[p][:], dram["b2"][bass.ds(e, 1), :].broadcast_to([P, D])).then_inc(s_w2[p], 16)

            def store(i, p):
                sp.wait_ge(s_ys, i + 1)
                sp.dma_start(dram["ys"][bass.ds(i * P, P), :], ys[p][:]).then_inc(s_sent[p], 16)

            load(0, 0, True)
            load(1, 1, True)
            with sp.Fori(0, TILES - 3, 2) as i:
                load(i + 2, 0, False)
                store(i, 0)
                load(i + 3, 1, False)
                store(i + 1, 1)
            load(TILES - 1, 0, False)
            for i in range(TILES - 3, TILES):
                store(i, i % 2)
            sp.wait_ge(s_sent[0], 16 * (TILES // 2 + 1))
            sp.wait_ge(s_sent[1], 16 * (TILES // 2))

        @block.gpsimd
        def _(pool):
            pool_share(pool)

        @block.tensor
        def _(pe):
            pe.wait_ge(s_in, 16)

            def hidden(i, p, turn):
                pe.wait_ge(s_w1[p], turn * 32 + 32)
                for k in range(KT):
                    ins = pe.transpose(pt[:, k], xs[p][:, k * P:(k + 1) * P], ident[:])
                ins.then_inc(s_turned, 1)
                pe.wait_ge(s_xsT, i + 1)
                for c in range(HT):
                    for k in range(KT):
                        ins = pe.matmul(ph[p][:, c], w1[p][:, k, c * P:(c + 1) * P], xsT[p][:, k],
                                        start=(k == 0), stop=(k == KT - 1), skip_group_check=True)
                    if c == HT // 2 - 1:
                        ins.then_inc(s_half, 1)
                ins.then_inc(s_hid, 1)

            def outer(i, p, turn):
                pe.wait_ge(s_silu, i + 1)
                pe.wait_ge(s_w2[p], turn * 32 + 32)
                for c in range(HT):
                    ins = pe.matmul(po[p][:], h[p][:, c], w2[p][:, c], start=(c == 0), stop=(c == HT - 1))
                ins.then_inc(s_out, 1)

            hidden(0, 0, 0)
            with pe.Fori(0, TILES // 2) as t:
                hidden(2 * t + 1, 1, t)
                outer(2 * t, 0, t)
                hidden(2 * t + 2, 0, t + 1)
                outer(2 * t + 1, 1, t)
            outer(TILES - 1, 0, TILES // 2)

        @block.scalar
        def _(act):
            def silu(i, p, turn):
                act.wait_ge(s_b1[p], turn * 16 + 16)
                for c in range(HT):
                    if c == 0:
                        act.wait_ge(s_half, i + 1)
                    if c == HT // 2:
                        act.wait_ge(s_hid, i + 1)
                    ins = act.activation(h[p][:, c], ph[p][:, c], ACT.Silu, bias=b1[p][:, c:c + 1])
                ins.then_inc(s_silu, 1)

            silu(0, 0, 0)
            with act.Fori(0, TILES // 2) as t:
                silu(2 * t + 1, 1, t)
                silu(2 * t + 2, 0, t + 1)

        @block.vector
        def _(dve):
            def turned(i, p):
                dve.wait_ge(s_turned, i + 1)
                dve.tensor_copy(xsT[p][:], pt[:]).then_inc(s_xsT, 1)

            def finish(i, p, turn, first):
                dve.wait_ge(s_out, i + 1)
                if not first:
                    dve.wait_ge(s_sent[p], turn * 16)
                dve.tensor_tensor(ys[p][:], po[p][:], b2[p][:], ALU.add).then_inc(s_ys, 1)

            turned(0, 0)
            turned(1, 1)
            finish(0, 0, 0, True)
            turned(2, 0)
            finish(1, 1, 0, True)
            with dve.Fori(1, TILES // 2) as t:
                turned(2 * t + 1, 1)
                finish(2 * t, 0, t, False)
                turned(2 * t + 2, 0)
                finish(2 * t + 1, 1, t, False)
            finish(TILES - 1, 0, TILES // 2, False)


def moe_combine(nc, dram, x2, pos, wtop, pool_share):
    with ExitStack() as ctx:
        def sb(name, shape, dt=F32):
            return ctx.enter_context(nc.sbuf_tensor("m_" + name, shape, dt))

        sem = phase_semaphores(nc, ctx, "m_")

        y = sb("y", [P, TT, D])
        st = sb("st", [P, TT, 6])
        mv = sb("mv", [P, TT, 2])
        lnv = sb("lnv", [P, TT])
        rstd = sb("rstd", [P, TT])
        eps = sb("eps", [P, 1])
        s_y = [sem(f"y{t}") for t in range(TT)]
        s_eps = sem("eps")
        s_dve = sem("dve")
        s_mv = sem("mv")
        s_lnv = sem("lnv")
        s_rstd = sem("rstd")
        s_x3 = sem("x3")
        s_sent = sem("sent")
        block = ctx.enter_context(nc.Block())

        @block.gpsimd
        def _(pool):
            for t in range(TT):
                pool.indirect_dma_start(
                    out=y[:, t, :], out_offset=None, in_=dram["ys"],
                    in_offset=bass.IndirectOffsetOnAxis(ap=pos[:, t:t + 1], axis=0)).then_inc(s_y[t], 16)
            pool_share(pool)

        @block.vector
        def _(dve):
            dve.memset(eps[:], LN_EPS).then_inc(s_eps, 1)
            for t in range(TT):
                dve.wait_ge(s_y[t], 16)
                dve.scalar_tensor_tensor(y[:, t], y[:, t], wtop[:, t:t + 1], x2[:, t], ALU.mult, ALU.add)\
                    .then_inc(s_dve, 1)
                dve.wait_ge(s_dve, 2 * t + 1)
                dve.bn_stats(st[:, t], y[:, t]).then_inc(s_dve, 1)
                dve.wait_ge(s_dve, 2 * t + 2)
                dve.bn_aggr(mv[:, t], st[:, t]).then_inc(s_mv, 1)
            dve.wait_ge(s_mv, TT)
            dve.wait_ge(s_rstd, 1)
            for t in range(TT):
                dve.tensor_scalar(y[:, t], y[:, t], mv[:, t, 0:1], rstd[:, t:t + 1],
                                  ALU.subtract, ALU.mult).then_inc(s_x3, 1)

        @block.scalar
        def _(act):
            act.wait_ge(s_eps, 1)
            act.wait_ge(s_mv, TT)
            act.activation(lnv[:], mv[:, :, 1], ACT.Ln, bias=eps[:]).then_inc(s_lnv, 1)
            act.wait_ge(s_lnv, 1)
            act.activation(rstd[:], lnv[:], ACT.Exp, scale=-0.5).then_inc(s_rstd, 1)

        @block.sync
        def _(sp):
            for q in range(4):
                sp.wait_ge(s_x3, 4 * q + 4)
                sp.dma_start(dram["x3"][2 * q:2 * q + 2].rearrange("b (t p) d -> p (b t) d", p=P),
                             y[:, 4 * q:4 * q + 4]).then_inc(s_sent, 16)
            sp.wait_ge(s_sent, 64)


def layer1_attention(nc, dram, pool_share):
    with ExitStack() as ctx:
        def sb(name, shape, dt=F32):
            return ctx.enter_context(nc.sbuf_tensor("c_" + name, shape, dt))

        def two(name, shape, dt=F32):
            return [sb(f"{name}{i}", shape, dt) for i in range(2)]

        sem = phase_semaphores(nc, ctx, "c_")

        def sems(name):
            return [sem(f"{name}{i}") for i in range(2)]

        ident = sb("ident", [P, P])
        w = sb("w", [P, 3, KT, D])
        wr = sb("wr", [P, 2, KT, D])
        cols = sb("cols", [P, 5, 2])
        br = sb("br", [P, 2, 2])
        bv = sb("bv", [P, D])
        rope = sb("rope", [P, KT, S])
        ropeq = sb("ropeq", [P, KT, S])
        gw = sb("gw", [P, 6, 16])
        gwc = sb("gwc", [P, KT, 16])
        gb = sb("gb", [16, 1])
        eps = sb("eps", [P, 1])
        x = two("x", [P, QT, D])
        xT = two("xT", [P, KT, S])
        cT = two("cT", [P, KT, S])
        qT = two("qT", [P, KT, S])
        kT = two("kT", [P, KT, S])
        v = two("v", [P, QT, D])
        negmax = two("negmax", [P, QT])
        rsum = two("rsum", [P, QT])
        rinv = two("rinv", [P, QT])
        probs = two("probs", [P, QT, S])
        probsT = two("probsT", [P, 4, P])
        y = two("y", [P, QT, D])
        st = two("st", [P, QT, 6])
        mv = two("mv", [P, QT, 2])
        lnv = two("lnv", [P, QT])
        rstd = two("rstd", [P, QT])
        x4 = two("x4", [P, QT, D])
        x4T = two("x4T", [P, KT, S])
        gates = two("gates", [16, S])
        pm = [ctx.enter_context(nc.psum_tensor(f"c_pm{i}", [P, 2, 256], F32)) for i in range(2)]
        ps = [ctx.enter_context(nc.psum_tensor(f"c_ps{i}", [P, 2, 256], F32)) for i in range(2)]
        pt = [ctx.enter_context(nc.psum_tensor(f"c_pt{i}", [P, 4, P], F32)) for i in range(2)]
        po = [ctx.enter_context(nc.psum_tensor(f"c_po{i}", [P, 2, 256], F32)) for i in range(2)]

        s_in = sem("in")
        s_w = sem("w")
        s_x = sems("x")
        s_cT = sems("cT")
        s_step = sems("step")
        s_copied = sems("copied")
        s_scores = sems("scores")
        s_max = sems("max")
        s_exp = sems("exp")
        s_turned = sems("turned")
        s_evac = sems("evac")
        s_pv = sems("pv")
        s_stats = sems("stats")
        s_lnv = sems("lnv")
        s_rstd = sems("rstd")
        s_x4 = sems("x4")
        s_free = sems("free")
        s_sent = sems("sent")
        s_sent_g = sems("sent_g")
        s_dve = sem("dve")
        block = ctx.enter_context(nc.Block())
        STEPS1 = 6
        PASSES = B // 2

        @block.sync
        def _(sp):
            sp.dma_start(ident[:], dram["ident"]).then_inc(s_in, 16)
            sp.dma_start(w[:], dram["w"][:, WQ1:WQ1 + 3]).then_inc(s_in, 16)
            sp.dma_start(cols[:], dram["cols1"]).then_inc(s_in, 16)
            sp.dma_start(bv[:], dram["rows"][:, R_B1V]).then_inc(s_in, 16)
            sp.dma_start(rope[:], dram["rope"][:, 0]).then_inc(s_in, 16)
            sp.dma_start(ropeq[:], dram["rope"][:, 1]).then_inc(s_in, 16)
            sp.dma_start(gw[:], dram["gw"]).then_inc(s_in, 16)
            sp.dma_start(gb[:], dram["gb"]).then_inc(s_in, 16)

            def load_x(b, p):
                sp.dma_start(x[p][:], dram["x3"][bass.ds(b, 1)].rearrange("b (t p) d -> p (b t) d", p=P))\
                    .then_inc(s_x[p], 16)

            def load_c(b, p):
                sp.dma_start(cT[p][:], dram["cT"][bass.ds(b, 1)].rearrange("b p k s -> p (b k) s"))\
                    .then_inc(s_cT[p], 16)

            def store(t, p):
                b = 2 * t + p
                sp.wait_ge(s_x4[p], t + 1)
                sp.dma_start(dram["x4"][bass.ds(b, 1)].rearrange("b (t p) d -> p (b t) d", p=P), x4[p][:])\
                    .then_inc(s_sent[p], 16)
                sp.wait_ge(s_copied[p], t * STEPS1 + 6)
                sp.dma_start(dram["x4T"][bass.ds(b, 1)].rearrange("b p k s -> p (b k) s"), x4T[p][:])\
                    .then_inc(s_sent[p], 16)
                sp.wait_ge(s_copied[p], t * STEPS1 + 7)
                for g, name in enumerate(("gate_i", "gate_f")):
                    sp.dma_start(dram[name][bass.ds(b, 1)].rearrange("b h s -> (b h) s"),
                                 gates[p][8 * g:8 * g + 8, :]).then_inc(s_sent_g[p], 16)

            for p in range(2):
                load_x(p, p)
                load_c(p, p)
            with sp.Fori(0, PASSES - 1) as t:
                for p in range(2):
                    sp.wait_ge(s_stats[p], t + 1)
                    load_x(2 * t + 2 + p, p)
                for p in range(2):
                    store(t, p)
                    sp.wait_ge(s_step[p], t * STEPS1 + 6)
                    load_c(2 * t + 2 + p, p)
                for p in range(2):
                    sp.wait_ge(s_sent[p], 32 * t + 32)
                    sp.wait_ge(s_sent_g[p], 32 * t + 32)
                    sp.sem_inc(s_free[p], 1)
            for p in range(2):
                store(PASSES - 1, p)
            for p in range(2):
                sp.wait_ge(s_sent[p], 32 * PASSES)
                sp.wait_ge(s_sent_g[p], 32 * PASSES)

        @block.gpsimd
        def _(pool):
            pool_share(pool)

        @block.tensor
        def _(pe):
            pe.wait_ge(s_in, 16 * 8)
            pe.wait_ge(s_w, 6)

            def free(t, p, n):
                pe.wait_ge(s_copied[p], t * STEPS1 + n + 1)

            def turn(t, p, n, src):
                free(t, p, n)
                for k in range(KT):
                    for qt in range(QT):
                        ins = pe.transpose(pm[p][:, k, qt * P:(qt + 1) * P], src[p][:, qt, k * P:(k + 1) * P], ident[:])
                ins.then_inc(s_step[p], 1)

            def project_T(t, p, n, wi):
                free(t, p, n)
                for et in range(2):
                    for k in range(KT):
                        ins = pe.matmul(pm[p][:, et], wr[:, wi, k, et * P:(et + 1) * P], xT[p][:, k, :],
                                        start=(k == 0), stop=(k == KT - 1))
                ins.then_inc(s_step[p], 1)

            with pe.Fori(0, PASSES) as t:
                for p in range(2):
                    pe.wait_ge(s_x[p], 16 * t + 16)
                    turn(t, p, 0, x)
                for p in range(2):
                    project_T(t, p, 1, 1)
                for p in range(2):
                    project_T(t, p, 2, 0)
                for p in range(2):
                    free(t, p, 3)
                    for qt in range(QT):
                        for k in range(KT):
                            ins = pe.matmul(pm[p][:, qt], xT[p][:, k, qt * P:(qt + 1) * P], w[:, 2, k, :],
                                            start=(k == 0), stop=(k == KT - 1))
                    ins.then_inc(s_step[p], 1)
                for p in range(2):
                    for qt in range(QT):
                        for k in range(KT):
                            ins = pe.matmul(ps[p][:, qt], qT[p][:, k, qt * P:(qt + 1) * P], kT[p][:, k, :],
                                            start=(k == 0), stop=(k == KT - 1))
                    ins.then_inc(s_scores[p], 1)
                for p in range(2):
                    pe.wait_ge(s_exp[p], t + 1)
                    for qt in range(QT):
                        for c in range(2):
                            ins = pe.transpose(pt[p][:, 2 * qt + c], probs[p][:, qt, c * P:(c + 1) * P], ident[:])
                    ins.then_inc(s_turned[p], 1)
                for p in range(2):
                    free(t, p, 4)
                    pe.wait_ge(s_evac[p], t + 1)
                    for qt in range(QT):
                        for c in range(2):
                            ins = pe.matmul(po[p][:, qt], probsT[p][:, 2 * qt + c], v[p][:, c, :],
                                            start=(c == 0), stop=(c == 1))
                    ins.then_inc(s_pv[p], 1)
                for p in range(2):
                    pe.wait_ge(s_x4[p], t + 1)
                    turn(t, p, 4, x4)
                for p in range(2):
                    free(t, p, 5)
                    pe.wait_ge(s_cT[p], 16 * t + 16)
                    for k in range(KT):
                        pe.matmul(pm[p][0:16, 0], gw[:, k, :], x4T[p][:, k, :], start=(k == 0), stop=False)
                    for k in range(KT):
                        ins = pe.matmul(pm[p][0:16, 0], gwc[:, k, :], cT[p][:, k, :], start=False, stop=(k == KT - 1))
                    ins.then_inc(s_step[p], 1)

        @block.scalar
        def _(act):
            act.wait_ge(s_in, 16 * 8)
            with act.Fori(0, PASSES) as t:
                for p in range(2):
                    act.wait_ge(s_step[p], t * STEPS1 + 1)
                    act.copy(xT[p][:], pm[p][:]).then_inc(s_copied[p], 1)
                for p in range(2):
                    act.wait_ge(s_step[p], t * STEPS1 + 4)
                    act.copy(v[p][:], pm[p][:]).then_inc(s_copied[p], 1)
                for p in range(2):
                    act.wait_ge(s_max[p], t + 1)
                    for qt in range(QT):
                        ins = act.activation(probs[p][:, qt], ps[p][:, qt], ACT.Exp, bias=negmax[p][:, qt:qt + 1],
                                             accum_out=rsum[p][:, qt:qt + 1])
                    ins.then_inc(s_exp[p], 1)
                for p in range(2):
                    act.wait_ge(s_turned[p], t + 1)
                    act.copy(probsT[p][:], pt[p][:]).then_inc(s_evac[p], 1)
                for p in range(2):
                    act.wait_ge(s_stats[p], t + 1)
                    act.activation(lnv[p][:], mv[p][:, :, 1], ACT.Ln, bias=eps[:]).then_inc(s_lnv[p], 1)
                    act.wait_ge(s_lnv[p], t + 1)
                    act.activation(rstd[p][:], lnv[p][:], ACT.Exp, scale=-0.5).then_inc(s_rstd[p], 1)
                for p in range(2):
                    act.wait_ge(s_free[p], t + 1)
                    act.wait_ge(s_step[p], t * STEPS1 + 5)
                    act.copy(x4T[p][:], pm[p][:]).then_inc(s_copied[p], 1)
                for p in range(2):
                    act.wait_ge(s_step[p], t * STEPS1 + 6)
                    act.activation(gates[p][:], pm[p][0:16, 0], ACT.Identity, bias=gb[:]).then_inc(s_copied[p], 1)

        @block.vector
        def _(dve):
            dve.memset(eps[:], LN_EPS).then_inc(s_w, 1)
            for p in range(2):
                dve.sem_inc(s_copied[p], 1)
                dve.sem_inc(s_free[p], 1)
            dve.wait_ge(s_in, 16 * 8)
            src = w[:, 0:2].rearrange("p w k (i two) -> p (w k i) two", two=2)
            dst = wr[:].rearrange("p w k (i two) -> p (w k i) two", two=2)
            dve.tensor_tensor(dst[:, :, 0], src[:, :, 0], src[:, :, 1], ALU.subtract).then_inc(s_w, 1)
            dve.tensor_tensor(dst[:, :, 1], src[:, :, 1], src[:, :, 0], ALU.add).then_inc(s_w, 1)
            for i in range(2):
                dve.scalar_tensor_tensor(br[:, i], cols[:, 2 + i], cols[:, 4, 0:1], cols[:, i], ALU.mult, ALU.add)\
                    .then_inc(s_w, 1)
            dve.tensor_tensor(gwc[:], gw[:, 2:4], gw[:, 4:6], ALU.add).then_inc(s_w, 1)
            dve.wait_ge(s_w, 6)
            with dve.Fori(0, PASSES) as t:
                chain = Count(dve, s_dve, 6, t * 6)
                for p in range(2):
                    dve.wait_ge(s_step[p], t * STEPS1 + 2)
                    for et in range(2):
                        ins = dve.scalar_tensor_tensor(kT[p][:, et], pm[p][:, et], br[:, 1, et:et + 1], rope[:, et],
                                                       ALU.add, ALU.mult)
                    ins.then_inc(s_copied[p], 1)
                for p in range(2):
                    dve.wait_ge(s_step[p], t * STEPS1 + 3)
                    for et in range(2):
                        ins = dve.scalar_tensor_tensor(qT[p][:, et], pm[p][:, et], br[:, 0, et:et + 1], ropeq[:, et],
                                                       ALU.add, ALU.mult)
                    ins.then_inc(s_copied[p], 1)
                for p in range(2):
                    dve.wait_ge(s_scores[p], t + 1)
                    dve.tensor_reduce(negmax[p][:], ps[p][:], AX.X, ALU.max, negate=True).then_inc(s_max[p], 1)
                for p in range(2):
                    dve.wait_ge(s_x[p], 16 * t + 16)
                    dve.tensor_tensor(y[p][:], x[p][:], bv[:].unsqueeze(1).broadcast_to([P, QT, D]), ALU.add)
                    dve.wait_ge(s_exp[p], t + 1)
                    chain.link(dve.reciprocal(rinv[p][:], rsum[p][:]))
                for p in range(2):
                    dve.wait_ge(s_pv[p], t + 1)
                    for qt in range(QT):
                        ins = dve.scalar_tensor_tensor(y[p][:, qt], po[p][:, qt], rinv[p][:, qt:qt + 1], y[p][:, qt],
                                                       ALU.mult, ALU.add)
                    chain.link(ins)
                    dve.bn_stats(st[p][:, 0], y[p][:, 0])
                    chain.link(dve.bn_stats(st[p][:, 1], y[p][:, 1]))
                    dve.nop(nofuse=True)
                    dve.bn_aggr(mv[p][:, 0], st[p][:, 0])
                    dve.bn_aggr(mv[p][:, 1], st[p][:, 1]).then_inc(s_stats[p], 1)
                for p in range(2):
                    dve.wait_ge(s_free[p], t + 1)
                    dve.wait_ge(s_rstd[p], t + 1)
                    dve.wait_ge(s_stats[p], t + 1)
                    for qt in range(QT):
                        ins = dve.tensor_scalar(x4[p][:, qt], y[p][:, qt], mv[p][:, qt, 0:1], rstd[p][:, qt:qt + 1],
                                                ALU.subtract, ALU.mult)
                    ins.then_inc(s_x4[p], 1)
                chain.end()


H1 = 8
HW = D // H1
BH = B * H1
SCALE1 = float(1.0 / np.sqrt(np.float32(HW)))


def mlstm_gates(nc, dram, aT, eT, pool_share):
    with ExitStack() as ctx:
        def sb(name, shape, dt=F32):
            return ctx.enter_context(nc.sbuf_tensor("g_" + name, shape, dt))

        sem = phase_semaphores(nc, ctx, "g_")

        ident = sb("ident", [P, P])
        gi = sb("gi", [BH, S])
        gf = sb("gf", [BH, S])
        ab = sb("ab", [BH, S])
        ex = sb("ex", [BH, S])
        l1 = sb("l1", [BH, S])
        ls = sb("ls", [BH, S])
        ones = sb("ones", [BH, S])
        one = sb("one", [BH, 1])
        cs = sb("cs", [BH, S])
        a = sb("a", [BH, S])
        m = sb("m", [BH, S])
        en = sb("en", [BH, S])
        pt = ctx.enter_context(nc.psum_tensor("g_pt", [P, 2, 2, BH], F32))
        s_in = sem("in")
        s_ones = sem("ones")
        s_abs = sem("abs")
        s_ex = sem("ex")
        s_l1 = sem("l1")
        s_a = sem("a")
        s_m = sem("m")
        s_mld = sem("mld")
        s_en = sem("en")
        s_turned = sem("turned")
        s_done = sem("done")
        s_sent = sem("sent")
        s_dve = sem("dve")
        block = ctx.enter_context(nc.Block())

        @block.sync
        def _(sp):
            sp.dma_start(gf[:], dram["gate_f"].rearrange("b h s -> (b h) s")).then_inc(s_in, 16)
            sp.dma_start(gi[:], dram["gate_i"].rearrange("b h s -> (b h) s")).then_inc(s_in, 16)
            sp.dma_start(ident[:], dram["ident"]).then_inc(s_in, 16)
            sp.wait_ge(s_m, 1)
            sp.dma_start(dram["runmax"], m[:]).then_inc(s_sent, 16)
            sp.wait_ge(s_sent, 16)

        @block.gpsimd
        def _(pool):
            pool_share(pool)

        @block.scalar
        def _(act):
            act.wait_ge(s_abs, 1)
            act.activation(ex[:], ab[:], ACT.Exp, scale=-1.0).then_inc(s_ex, 1)
            act.wait_ge(s_ex, 1)
            act.activation(l1[:], ex[:], ACT.Ln, bias=one[:]).then_inc(s_l1, 1)
            act.wait_ge(s_mld, 1)
            act.activation(en[:], ab[:], ACT.Exp, scale=-1.0).then_inc(s_en, 1)

        @block.vector
        def _(dve):
            n = [0]

            def link(ins):
                ins.then_inc(s_dve, 1)
                n[0] += 1
                dve.wait_ge(s_dve, n[0])

            dve.memset(ones[:], 1.0)
            link(dve.memset(one[:], 1.0))
            dve.wait_ge(s_in, 48)
            dve.scalar_tensor_tensor(ab[:], gf[:], -1.0, gf[:], ALU.mult, ALU.max).then_inc(s_abs, 1)
            link(dve.tensor_scalar(ls[:], gf[:], 0.0, None, ALU.min))
            dve.wait_ge(s_l1, 1)
            link(dve.tensor_tensor(ls[:], ls[:], l1[:], ALU.subtract))
            link(dve.tensor_tensor_scan(cs[:], ones[:], ls[:], 0.0, ALU.mult, ALU.add))
            dve.tensor_tensor(a[:], gi[:], cs[:], ALU.subtract).then_inc(s_a, 1)
            dve.wait_ge(s_a, 1)
            dve.tensor_tensor_scan(m[:], a[:], a[:], -3.0e38, ALU.max, ALU.max).then_inc(s_m, 1)
            dve.wait_ge(s_m, 1)
            dve.wait_ge(s_ex, 1)
            dve.tensor_tensor(ab[:], cs[:], m[:], ALU.add).then_inc(s_mld, 1)
            dve.wait_ge(s_turned, 1)
            dve.tensor_copy(aT[:], pt[:, 0])
            dve.tensor_copy(eT[:], pt[:, 1]).then_inc(s_done, 1)

        @block.tensor
        def _(pe):
            pe.wait_ge(s_in, 48)
            pe.wait_ge(s_a, 1)
            pe.wait_ge(s_en, 1)
            for i, src in enumerate((a, en)):
                for t in range(2):
                    ins = pe.transpose(pt[:, i, t], src[:, t * P:(t + 1) * P], ident[0:BH, 0:BH])
            ins.then_inc(s_turned, 1)


def query_blocks(nc, dram, vt, qblk, pool_share):
    with ExitStack() as ctx:
        xq = ctx.enter_context(nc.sbuf_tensor(f"q{vt}_xq", [P, B, KT, P], F32))
        sem = phase_semaphores(nc, ctx, f"q{vt}_")
        s_xq = sem("xq_in")
        s_zero = sem("zero")
        block = ctx.enter_context(nc.Block())

        @block.sync
        def _(sp):
            for b in range(B):
                sp.dma_start(xq[:, b], dram["x4T"][b, :, :, vt * P:(vt + 1) * P]).then_inc(s_xq, 16)

        def fill(eng, copy, hp):
            src = xq[32 * hp:32 * hp + 32].rearrange("p b k v -> p (k v) b")
            dst = qblk[32 * hp:32 * hp + 32].rearrange("p k v n -> p (k v) n")[:, :, 8 * hp:8 * hp + 8]
            copy(dst, src)

        @block.gpsimd
        def _(pool):
            if vt == 0:
                pool.memset(qblk[:, 1], 0.0).then_inc(s_zero, 1)
            pool_share(pool)

        @block.vector
        def _(dve):
            if vt == 0:
                dve.memset(qblk[:, 0], 0.0).then_inc(s_zero, 1)
                dve.wait_ge(s_zero, 2)
            dve.wait_ge(s_xq, 16 * B)
            for hp in range(2):
                fill(dve, dve.tensor_copy, hp)

        @block.scalar
        def _(act):
            if vt == 0:
                act.wait_ge(s_zero, 2)
            act.wait_ge(s_xq, 16 * B)
            for hp in range(2, 4):
                fill(act, act.copy, hp)


def hop_scores(nc, dram, vt, qblk, kh, pool_share):
    first = 0 if vt == 0 else P // GROUP
    groups = P * (vt + 1) // GROUP
    queries = GROUP // (vt + 1)
    ring = 4
    passes = groups // ring
    N = BH // KT
    with ExitStack() as ctx:
        sem = phase_semaphores(nc, ctx, f"h{vt}_")

        ident = ctx.enter_context(nc.sbuf_tensor(f"h{vt}_ident", [P, P], F32))
        rows = [ctx.enter_context(nc.sbuf_tensor(f"h{vt}_rows{i}", [P, GROUP, D], F32)) for i in range(ring)]
        rT = [ctx.enter_context(nc.sbuf_tensor(f"h{vt}_rT{i}", [P, KT, GROUP, P], F32)) for i in range(2)]
        qs = [ctx.enter_context(nc.sbuf_tensor(f"h{vt}_qs{i}", [P, KT, queries, N], F32)) for i in range(2)]
        sc = [ctx.enter_context(nc.sbuf_tensor(f"h{vt}_sc{i}", [P, KT, P], F32)) for i in range(2)]
        pt = [[ctx.enter_context(nc.psum_tensor(f"h{vt}_pt{i}{k}", [P, GROUP, P], F32)) for k in range(KT)]
              for i in range(2)]
        pc = [ctx.enter_context(nc.psum_tensor(f"h{vt}_pc{i}", [P, KT, P], F32)) for i in range(2)]
        po = [ctx.enter_context(nc.psum_tensor(f"h{vt}_po{i}", [P, KT, GROUP, N], F32)) for i in range(2)]
        s_in = sem("in")
        s_rows = [sem(f"rows{i}") for i in range(ring)]
        s_turned = sem("turned")
        s_rT = [sem("rT_act"), sem("rT_dve")]
        s_qs = sem("queries")
        s_prod = sem("prod")
        s_sc = [sem("sc_act"), sem("sc_dve")]
        s_back = sem("back")
        s_kh = [sem("kh_act"), sem("kh_dve")]
        block = ctx.enter_context(nc.Block())

        @block.sync
        def _(sp):
            sp.dma_start(ident[:], dram["ident"]).then_inc(s_in, 16)

            def load(n, i):
                sp.dma_start(rows[i][:].rearrange("p j d -> p (j d)"),
                             dram["pos_rows"][bass.ds(first + n, 1)].rearrange("g p n -> p (g n)"))\
                    .then_inc(s_rows[i], 16)

            for i in range(ring):
                load(i, i)
            with sp.Fori(0, passes - 1) as t:
                for i in range(ring):
                    sp.wait_ge(s_turned, 4 * t + i + 1)
                    load(4 * t + ring + i, i)

        @block.gpsimd
        def _(pool):
            pool.sem_inc(s_prod, 2)
            pool.sem_inc(s_back, 2)
            pool_share(pool)
            with pool.Fori(0, passes) as t:
                for i in range(ring):
                    n = 4 * t + i
                    pool.wait_ge(s_prod, n + 1)
                    pool.tensor_copy(qs[i % 2][:], qblk[:, :, bass.ds(n * queries, queries)]).then_inc(s_qs, 1)

        @block.tensor
        def _(pe):
            pe.wait_ge(s_in, 16)

            def turn(t, i):
                pe.wait_ge(s_rows[i], 16 * t + 16)
                for k in range(KT):
                    for j in range(GROUP):
                        ins = pe.transpose(pt[i % 2][k][:, j], rows[i][:, j, k * P:(k + 1) * P], ident[:])
                ins.then_inc(s_turned, 1)

            def product(t, i):
                n = 4 * t + i
                pe.wait_ge(s_qs, n + 1)
                pe.wait_ge(s_rT[0], n + 1)
                pe.wait_ge(s_rT[1], n + 1)
                for k in range(KT):
                    for j in range(GROUP):
                        ins = pe.matmul(pc[i % 2][N * j:N * j + N, k], qs[i % 2][:, k, j // (vt + 1)],
                                        rT[i % 2][:, k, j], start=True, stop=True, skip_group_check=True)
                ins.then_inc(s_prod, 1)

            def back(t, i):
                pe.wait_ge(s_sc[i % 2], 2 * t + i // 2 + 1)
                pe.wait_ge(s_kh[i % 2], 2 * t + i // 2 + 1)
                for k in range(KT):
                    ins = pe.transpose(po[i % 2][:, k].rearrange("p j n -> p (j n)"), sc[i % 2][:, k], ident[:])
                ins.then_inc(s_back, 1)

            def group(t, i, start=False, end=False):
                if i < ring - 1:
                    turn(t, i + 1)
                elif not end:
                    turn(t + 1, 0)
                product(t, i)
                if i > 0:
                    back(t, i - 1)
                elif not start:
                    back(t - 1, ring - 1)

            turn(0, 0)
            for i in range(ring):
                group(0, i, start=True)
            with pe.Fori(1, passes - 1) as t:
                for i in range(ring):
                    group(t, i)
            for i in range(ring):
                group(passes - 1, i, end=True)
            back(passes - 1, ring - 1)

        def evacuate(eng, copy, which):
            eng.sem_inc(s_kh[which], 1)

            def rows_of(t, i):
                n = 4 * t + i
                eng.wait_ge(s_prod, n + 1)
                eng.wait_ge(s_turned, n + 1)
                copy(rT[i % 2][:, which], pt[i % 2][which][:]).then_inc(s_rT[which], 1)

            def scores_of(t, i):
                n = 4 * t + i
                eng.wait_ge(s_prod, n + 3)
                eng.wait_ge(s_back, n + 1)
                copy(sc[i % 2][:], pc[i % 2][:]).then_inc(s_sc[which], 1)

            def keep(t, i):
                n = 4 * t + i
                eng.wait_ge(s_back, n + 3)
                if vt == 0:
                    dst = kh[:, bass.ds(n * GROUP, GROUP), 0].rearrange("p v (k n) -> p k v n", k=KT)
                else:
                    dst = kh[:, bass.ds(n * queries, queries)].rearrange("p v t (k n) -> p k (v t) n", k=KT)
                copy(dst, po[i % 2][:]).then_inc(s_kh[which], 1)

            def group(t, i, start=False, end=False):
                if i < ring - 1:
                    rows_of(t, i + 1)
                elif not end:
                    rows_of(t + 1, 0)
                if i % 2 == which:
                    scores_of(t, i)
                elif i > 0:
                    keep(t, i - 1)
                elif not start:
                    keep(t - 1, ring - 1)

            rows_of(0, 0)
            for i in range(ring):
                group(0, i, start=True)
            with eng.Fori(1, passes - 1) as t:
                for i in range(ring):
                    group(t, i)
            for i in range(ring):
                group(passes - 1, i, end=True)
            if which == 1:
                keep(passes - 1, ring - 1)

        @block.scalar
        def _(act):
            evacuate(act, act.copy, 0)

        @block.vector
        def _(dve):
            evacuate(dve, dve.tensor_copy, 1)


def mlstm_heads(nc, dram, vt, qblk, kh, aT, eT):
    mts = range(vt + 1)
    nm = len(mts)
    with ExitStack() as ctx:
        def sb(name, shape, dt=F32):
            return ctx.enter_context(nc.sbuf_tensor(f"l{vt}_" + name, shape, dt))

        def two(name, shape, dt=F32):
            return [sb(f"{name}{i}", shape, dt) for i in range(2)]

        sem = phase_semaphores(nc, ctx, f"l{vt}_")

        def sems(name):
            return [sem(f"{name}{i}") for i in range(2)]

        lnw = sb("lnw", [P, D])
        lnb = sb("lnb", [P, D])
        eps = sb("eps", [P, 1])
        cT = two("cT", [P, KT, S])
        va = two("va", [P, 2, H1 * (HW + 1)])
        x4 = two("x4", [P, D])
        mb = two("mb", [P, H1, P])
        dm = two("dm", [P, nm, H1, P])
        cm = two("cm", [P, nm, H1, P])
        den = sb("den", [P, H1])
        rn = sb("rn", [P, H1])
        hh = sb("hh", [P, H1, HW])
        sq = sb("sq", [P, H1, HW])
        mu = sb("mu", [P, H1])
        var = sb("var", [P, H1])
        lnv8 = sb("lnv8", [P, H1])
        r8 = sb("r8", [P, H1])
        y = sb("y", [P, D])
        st = sb("st", [P, 6])
        mv = sb("mv", [P, 2])
        lnv = sb("lnv", [P, 1])
        rstd = sb("rstd", [P, 1])
        x5 = two("x5", [P, D])
        pq = [ctx.enter_context(nc.psum_tensor(f"l{vt}_pq{m}", [P, H1, P], F32)) for m in mts]
        pv = [ctx.enter_context(nc.psum_tensor(f"l{vt}_pv{i}", [P, H1, HW + 1], F32)) for i in range(2)]

        s_in = sem("in")
        s_w = sem("w")
        s_q = sems("q")
        s_va = sems("va")
        s_x4 = sems("x4")
        s_mb = sems("mb")
        s_pool = sem("pool")
        s_arg = sem("arg")
        s_dm = sem("dm")
        s_dm_free = sem("dm_free")
        s_qk = sem("qk")
        s_qk_read = sem("qk_read")
        s_c = sem("c")
        s_pv = sem("pv")
        s_var = sem("var")
        s_ln8 = sem("ln8")
        s_r8 = sem("r8")
        s_xb = sem("xb")
        s_y = sem("y")
        s_mv = sem("mv")
        s_lnv = sem("lnv")
        s_rstd = sem("rstd")
        s_x5 = sem("x5")
        s_free = sems("free")
        s_sent = sems("sent")
        s_dve = sem("dve")
        block = ctx.enter_context(nc.Block())
        PASSES = B // 2

        @block.sync
        def _(sp):
            sp.dma_start(lnw[:], dram["rows"][:, R_LNW]).then_inc(s_in, 16)
            sp.dma_start(lnb[:], dram["rows"][:, R_LNB]).then_inc(s_in, 16)

            def load(b, p, first):
                if not first:
                    sp.wait_ge(s_qk, b - 1)
                one = bass.ds(b, 1)
                sp.dma_start(cT[p][:], dram["cT"][one].rearrange("b p k s -> p (b k) s")).then_inc(s_q[p], 16)
                if not first:
                    sp.wait_ge(s_arg, b - 1)
                sp.dma_start(mb[p][:], dram["runmax"].rearrange("(b h) s -> b h s", h=H1)[
                    one, :, vt * P:(vt + 1) * P].broadcast_to([P, H1, P])).then_inc(s_mb[p], 16)
                if not first:
                    sp.wait_ge(s_pv, b - 1)
                sp.dma_start(va[p][:], dram["ctx_ones"][one].rearrange("b p m n -> p (b m) n")).then_inc(s_va[p], 16)
                if not first:
                    sp.wait_ge(s_y, b - 1)
                sp.dma_start(x4[p][:], dram["x4"][one, vt * P:(vt + 1) * P].rearrange("b p d -> p (b d)"))\
                    .then_inc(s_x4[p], 16)

            def store(b, p):
                sp.wait_ge(s_x5, b + 1)
                sp.dma_start(dram["x5"][bass.ds(b, 1), vt * P:(vt + 1) * P].rearrange("b p d -> p (b d)"), x5[p][:])\
                    .then_inc(s_sent[p], 16)

            load(0, 0, True)
            load(1, 1, True)
            with sp.Fori(0, PASSES - 1) as t:
                for p in range(2):
                    load(2 * t + 2 + p, p, False)
                    store(2 * t + p, p)
                for p in range(2):
                    sp.wait_ge(s_sent[p], 16 * t + 16)
                    sp.sem_inc(s_free[p], 1)
            for p in range(2):
                store(B - 2 + p, p)
            for p in range(2):
                sp.wait_ge(s_sent[p], 16 * PASSES)

        @block.gpsimd
        def _(pool):
            pool.wait_ge(s_w, 2)

            def args(t, p):
                b = 2 * t + p
                pool.wait_ge(s_mb[p], 16 * t + 16)
                pool.wait_ge(s_dm_free, b + 1)
                pool.nop(nofuse=True)
                pool.nop(nofuse=True)
                for m in mts:
                    ins = pool.tensor_tensor(
                        dm[p][:, m], aT[:, m, bass.ds(H1 * b, H1)].unsqueeze(2).broadcast_to([P, H1, P]), mb[p][:],
                        ALU.subtract)
                ins.then_inc(s_pool, 1)
                pool.wait_ge(s_pool, b + 1)
                pool.nop(nofuse=True)
                pool.affine_select(out=dm[p][:, vt], in_=dm[p][:, vt], compare_op=ALU.is_ge, fill=NEG, base=0,
                                   pattern=[[0, H1], [1, P]], channel_multiplier=-1).then_inc(s_arg, 1)
                pool.wait_ge(s_x4[p], 16 * t + 16)
                pool.tensor_tensor(x4[p][:], x4[p][:], lnb[:], ALU.add).then_inc(s_xb, 1)

            with pool.Fori(0, PASSES) as t:
                args(t, 0)
                args(t, 1)

        @block.tensor
        def _(pe):
            def qk(t, p):
                b = 2 * t + p
                pe.wait_ge(s_q[p], 16 * t + 16)
                pe.wait_ge(s_qk_read, b + 1)
                for m in mts:
                    for k in range(KT):
                        q = qblk[:, k].rearrange("p v (h b) -> p h v b", b=B)[:, :, :, bass.ds(b, 1)]\
                            .rearrange("p h v b -> p h (v b)")
                        ins = pe.matmul(pq[m][:, 4 * k:4 * k + 4], cT[p][:, k, m * P:(m + 1) * P], q,
                                        start=True, stop=True, skip_group_check=True)
                ins.then_inc(s_qk, 1)

            def values(t, p):
                b = 2 * t + p
                pe.wait_ge(s_va[p], 16 * t + 16)
                pe.wait_ge(s_c, b + 1)
                for h in range(H1):
                    for m in mts:
                        ins = pe.matmul(pv[p][:, h], cm[p][:, m, h], va[p][:, m, h * (HW + 1):(h + 1) * (HW + 1)],
                                        start=(m == 0), stop=(m == nm - 1), skip_group_check=True)
                ins.then_inc(s_pv, 1)

            qk(0, 0)
            with pe.Fori(0, PASSES - 1) as t:
                qk(t, 1)
                values(t, 0)
                qk(t + 1, 0)
                values(t, 1)
            qk(PASSES - 1, 1)
            values(PASSES - 1, 0)
            values(PASSES - 1, 1)

        @block.scalar
        def _(act):
            act.wait_ge(s_w, 2)

            def decay(t, p):
                b = 2 * t + p
                act.wait_ge(s_arg, b + 1)
                act.activation(dm[p][:], dm[p][:], ACT.Exp).then_inc(s_dm, 1)

            def roots(t, p):
                b = 2 * t + p
                act.wait_ge(s_var, b + 1)
                act.activation(lnv8[:], var[:], ACT.Ln, bias=eps[:], scale=1.0 / HW).then_inc(s_ln8, 1)
                act.wait_ge(s_ln8, b + 1)
                act.activation(r8[:], lnv8[:], ACT.Exp, scale=-0.5).then_inc(s_r8, 1)
                act.wait_ge(s_mv, b + 1)
                act.activation(lnv[:], mv[:, 1:2], ACT.Ln, bias=eps[:]).then_inc(s_lnv, 1)
                act.wait_ge(s_lnv, b + 1)
                act.activation(rstd[:], lnv[:], ACT.Exp, scale=-0.5).then_inc(s_rstd, 1)

            decay(0, 0)
            with act.Fori(0, PASSES - 1) as t:
                decay(t, 1)
                roots(t, 0)
                decay(t + 1, 0)
                roots(t, 1)
            decay(PASSES - 1, 1)
            roots(PASSES - 1, 0)
            roots(PASSES - 1, 1)

        @block.vector
        def _(dve):
            dve.memset(eps[:], LN_EPS).then_inc(s_w, 1)
            dve.sem_inc(s_qk_read, 1)
            dve.sem_inc(s_dm_free, 2)
            for p in range(2):
                dve.sem_inc(s_free[p], 1)
            dve.wait_ge(s_in, 32)
            dve.tensor_scalar(lnw[:], lnw[:], 1.0, None, ALU.add).then_inc(s_w, 1)
            dve.wait_ge(s_w, 2)
            def front(t, p):
                b = 2 * t + p
                dve.wait_ge(s_qk, b + 1)
                for m in mts:
                    hop = kh[:, :, m, :].rearrange("p v (h b) -> p h v b", b=B)[:, :, :, bass.ds(b, 1)]\
                        .rearrange("p h v b -> p h (v b)")
                    ins = dve.scalar_tensor_tensor(cm[p][:, m], pq[m][:], SCALE1, hop, ALU.mult, ALU.add)
                ins.then_inc(s_qk_read, 1)
                dve.wait_ge(s_qk_read, b + 2)
                dve.wait_ge(s_dm, b + 1)
                ins = dve.tensor_tensor(cm[p][:], cm[p][:], dm[p][:], ALU.mult)
                ins.then_inc(s_c, 1)
                dve.wait_ge(s_c, b + 1)
                dve.sem_inc(s_dm_free, 1)

            def back(t, p):
                b = 2 * t + p
                chain = Count(dve, s_dve, 13, 13 * b)
                dve.wait_ge(s_pv, b + 1)
                chain.link(dve.scalar_tensor_tensor(den[:], pv[p][:, :, HW], -1.0, eT[:, vt, bass.ds(H1 * b, H1)],
                                                    ALU.mult, ALU.max))
                chain.link(dve.tensor_tensor(den[:], pv[p][:, :, HW], den[:], ALU.max))
                chain.link(dve.tensor_scalar(den[:], den[:], 1.0e-6, None, ALU.add))
                chain.link(dve.reciprocal(rn[:], den[:]))
                wide = [P, H1, HW]
                chain.link(dve.tensor_tensor(hh[:], pv[p][:, :, 0:HW], rn[:].unsqueeze(2).broadcast_to(wide), ALU.mult))
                chain.link(dve.tensor_reduce(mu[:], hh[:], AX.X, ALU.add))
                chain.link(dve.tensor_scalar(mu[:], mu[:], -1.0 / HW, None, ALU.mult))
                chain.link(dve.tensor_tensor(hh[:], hh[:], mu[:].unsqueeze(2).broadcast_to(wide), ALU.add))
                chain.link(dve.tensor_tensor(sq[:], hh[:], hh[:], ALU.mult))
                dve.tensor_reduce(var[:], sq[:], AX.X, ALU.add).then_inc(s_var, 1)
                dve.wait_ge(s_r8, b + 1)
                chain.link(dve.tensor_tensor(hh[:], hh[:], r8[:].unsqueeze(2).broadcast_to(wide), ALU.mult))
                chain.link(dve.tensor_tensor(y[:], hh[:].rearrange("p h c -> p (h c)"), lnw[:], ALU.mult))
                dve.wait_ge(s_xb, b + 1)
                dve.tensor_tensor(y[:], y[:], x4[p][:], ALU.add).then_inc(s_y, 1)
                dve.wait_ge(s_y, b + 1)
                chain.link(dve.bn_stats(st[:], y[:]))
                dve.nop(nofuse=True)
                dve.bn_aggr(mv[:], st[:]).then_inc(s_mv, 1)
                dve.wait_ge(s_free[p], t + 1)
                dve.wait_ge(s_mv, b + 1)
                dve.wait_ge(s_rstd, b + 1)
                chain.link(dve.tensor_scalar(x5[p][:], y[:], mv[:, 0:1], rstd[:], ALU.subtract, ALU.mult))
                dve.sem_inc(s_x5, 1)
                chain.end()

            front(0, 0)
            with dve.Fori(0, PASSES - 1) as t:
                front(t, 1)
                back(t, 0)
                front(t + 1, 0)
                back(t, 1)
            front(PASSES - 1, 1)
            back(PASSES - 1, 0)
            back(PASSES - 1, 1)


HID1 = P
SHARED = NE


class ExpertWeights:

    def __init__(self, nc, ctx, dram):
        self.dram = dram

        def sb(name, shape):
            return ctx.enter_context(nc.sbuf_tensor("fw_" + name, shape, F32))

        self.tiles = {
            "ident": sb("ident", [P, P]),
            "gate1": sb("gate1", [P, KT, P]),
            "rscale": sb("rscale", [P, 1]),
            "iota8m": sb("iota8m", [P, QT, NE]),
            "f_w1": sb("w1", [P, KT, NE + 1, HID1]),
            "f_b1": sb("b1", [P, NE + 1]),
            "f_w2": sb("w2", [P, NE + 1, D]),
            "f_b2": sb("b2", [P, D]),
            "bs2": sb("bs2", [P, D]),
        }
        self.s_loaded = ctx.enter_context(nc.semaphore("f_weights_loaded"))

    def load(self, pool):
        for name, tile in self.tiles.items():
            src = self.dram["rows"][:, R_BS2] if name == "bs2" else self.dram[name]
            pool.dma_start(tile[:], src).then_inc(self.s_loaded, 16)

    def wait(self, eng):
        eng.wait_ge(self.s_loaded, 16 * len(self.tiles))


def experts_top2(nc, dram, weights):
    with ExitStack() as ctx:
        def sb(name, shape, dt=F32):
            return ctx.enter_context(nc.sbuf_tensor("f_" + name, shape, dt))

        def ring(n, name, shape, dt=F32):
            return [sb(f"{name}{i}", shape, dt) for i in range(n)]

        sem = phase_semaphores(nc, ctx, "f_")

        def sems(name):
            return [sem(f"{name}{i}") for i in range(2)]

        ident, gw, rscale, iota8m, w1, b1, w2, b2, bs2 = (
            weights.tiles[n] for n in ("ident", "gate1", "rscale", "iota8m", "f_w1", "f_b1", "f_w2", "f_b2", "bs2"))
        x = ring(2, "x", [P, QT, D])
        xT = ring(2, "xT", [P, KT, S])
        e = sb("e", [P, QT, NE])
        s1 = sb("s1", [P, QT, NE])
        s2 = sb("s2", [P, QT, NE])
        t8 = sb("t8", [P, QT, NE])
        one1 = sb("one1", [P, QT, NE])
        one2 = sb("one2", [P, QT, NE])
        m1 = sb("m1", [P, QT])
        m2 = sb("m2", [P, QT])
        low = sb("low", [P, QT])
        gate = ring(2, "gate", [P, QT, P])
        gT = ring(2, "gT", [P, QT, P])
        h = ring(3, "h", [P, S])
        acc = ring(2, "acc", [P, QT, D])
        st = sb("st", [P, QT, 6])
        mv = sb("mv", [P, QT, 2])
        eps = sb("eps", [P, 1])
        lnv = sb("lnv", [P, QT])
        rstd = sb("rstd", [P, QT])
        y = ring(2, "y", [P, QT, D])
        pm = ctx.enter_context(nc.psum_tensor("f_pm", [P, KT, S], F32))
        pg = ctx.enter_context(nc.psum_tensor("f_pg", [P, QT, P], F32))
        pgT = ctx.enter_context(nc.psum_tensor("f_pgT", [P, QT, P], F32))
        ph = [ctx.enter_context(nc.psum_tensor(f"f_ph{i}", [P, S], F32)) for i in range(3)]
        po = [ctx.enter_context(nc.psum_tensor(f"f_po{i}", [P, QT, D], F32)) for i in range(2)]

        s_x = sems("x")
        s_turned = sem("turned")
        s_xT = sem("xT")
        s_xb = sem("xb")
        s_logits = sem("logits")
        s_e = sem("e")
        s_zero = sem("zero")
        s_gate = sem("gate")
        s_gT = sem("gT")
        s_gT_copied = sem("gT_copied")
        s_h = sem("h")
        s_gelu = sem("gelu")
        s_o = sem("o")
        s_acc = sem("acc")
        s_st = sem("st")
        s_mv = sem("mv")
        s_lnv = sem("lnv")
        s_rstd = sem("rstd")
        s_y = sem("y")
        s_free = sems("free")
        s_sent = sems("sent")
        s_dve = sem("dve")
        block = ctx.enter_context(nc.Block())
        PASSES = B // 2
        N = NE + 1
        ORDER = [SHARED] + list(range(NE))

        @block.sync
        def _(sp):
            def load(b, p):
                sp.dma_start(x[p][:], dram["x5"][bass.ds(b, 1)].rearrange("b (t p) d -> p (b t) d", p=P))\
                    .then_inc(s_x[p], 16)

            def store(b, p):
                sp.wait_ge(s_y, b + 1)
                sp.dma_start(dram["out"][bass.ds(b, 1)].rearrange("b (t p) d -> p (b t) d", p=P), y[p][:])\
                    .then_inc(s_sent[p], 16)

            load(0, 0)
            load(1, 1)
            def reload(b, p):
                sp.wait_ge(s_acc, (b - 2) * N + 1)
                load(b, p)

            def store_and_free(t, p):
                store(2 * t + p, p)
                sp.wait_ge(s_sent[p], 16 * t + 16)
                sp.sem_inc(s_free[p], 1)

            reload(2, 0)
            with sp.Fori(0, PASSES - 2) as t:
                reload(2 * t + 3, 1)
                store_and_free(t, 0)
                reload(2 * t + 4, 0)
                store_and_free(t, 1)
            reload(B - 1, 1)
            store_and_free(PASSES - 2, 0)
            store_and_free(PASSES - 2, 1)
            for p in range(2):
                store(B - 2 + p, p)
            for p in range(2):
                sp.wait_ge(s_sent[p], 16 * PASSES)

        @block.gpsimd
        def _(pool):
            for p in range(2):
                pool.memset(gate[p][:], 0.0).then_inc(s_zero, 1)
            weights.wait(pool)

            def bias(t, p):
                pool.wait_ge(s_x[p], 16 * t + 16)
                pool.wait_ge(s_turned, 2 * t + p + 1)
                pool.tensor_tensor(x[p][:], x[p][:], bs2[:].unsqueeze(1).broadcast_to([P, QT, D]), ALU.add)\
                    .then_inc(s_xb, 1)

            with pool.Fori(0, PASSES) as t:
                for p in range(2):
                    bias(t, p)

        @block.tensor
        def _(pe):
            weights.wait(pe)

            def turn(t, p):
                pe.wait_ge(s_x[p], 16 * t + 16)
                for k in range(KT):
                    for qt in range(QT):
                        ins = pe.transpose(pm[:, k, qt * P:(qt + 1) * P], x[p][:, qt, k * P:(k + 1) * P], ident[:])
                ins.then_inc(s_turned, 1)

            def logits(t, p):
                pe.wait_ge(s_xT, 2 * t + p + 1)
                for qt in range(QT):
                    for k in range(KT):
                        ins = pe.matmul(pg[:, qt], xT[p][:, k, qt * P:(qt + 1) * P], gw[:, k],
                                        start=(k == 0), stop=(k == KT - 1))
                ins.then_inc(s_logits, 1)

            def turn_gates(t, p):
                pe.wait_ge(s_gate, 2 * t + p + 1)
                for qt in range(QT):
                    ins = pe.transpose(pgT[:, qt], gate[p][:, qt], ident[:])
                ins.then_inc(s_gT, 1)

            def hidden(b, p, i, emptied=True):
                if emptied:
                    pe.wait_ge(s_gelu, b * N + i - 2)
                for k in range(KT):
                    ins = pe.matmul(ph[i % 3][:], w1[:, k, ORDER[i]], xT[p][:, k], start=(k == 0), stop=(k == KT - 1))
                ins.then_inc(s_h, 1)

            def outer(b, p, i, emptied):
                pe.wait_ge(s_gelu, b * N + i + 1)
                if emptied:
                    pe.wait_ge(s_acc, b * N + i - 1)
                for qt in range(QT):
                    if i == 0:
                        pe.matmul(po[p][:, qt], gT[p][:, qt], b2[:], start=True, stop=False)
                    ins = pe.matmul(po[(p + i) % 2][:, qt], h[i % 3][:, qt * P:(qt + 1) * P], w2[:, ORDER[i]],
                                    start=(i != 0), stop=True)
                ins.then_inc(s_o, 1)

            def batch(t, p, first, last):
                b = 2 * t + p
                for i in range(N):
                    if i + 2 < N:
                        hidden(b, p, i + 2, not (first and i == 0))
                    elif not last:
                        hidden(b + 1, 1 - p, i + 2 - N)
                    if i == 0:
                        pe.wait_ge(s_gT_copied, b + 1)
                    outer(b, p, i, not (first and i < 2))
                    if not last:
                        following = (t + p, 1 - p)
                        if i == 0:
                            turn(*following)
                        elif i == 2:
                            logits(*following)
                        elif i == 8:
                            turn_gates(*following)

            turn(0, 0)
            logits(0, 0)
            hidden(0, 0, 0, False)
            hidden(0, 0, 1, False)
            turn_gates(0, 0)
            batch(0, 0, True, False)
            batch(0, 1, False, False)
            with pe.Fori(1, PASSES - 1) as t:
                batch(t, 0, False, False)
                batch(t, 1, False, False)
            batch(PASSES - 1, 0, False, False)
            batch(PASSES - 1, 1, False, True)

        @block.scalar
        def _(act):
            weights.wait(act)
            act.wait_ge(s_zero, 3)

            def rows(b, p):
                act.wait_ge(s_turned, b + 1)
                act.copy(xT[p][:], pm[:]).then_inc(s_xT, 1)

            def exps(b):
                act.wait_ge(s_logits, b + 1)
                act.activation(e[:], pg[:, :, 0:NE], ACT.Exp, scale=-1.0).then_inc(s_e, 1)

            def root(b):
                act.wait_ge(s_mv, b + 1)
                act.activation(lnv[:], mv[:, :, 1], ACT.Ln, bias=eps[:]).then_inc(s_lnv, 1)
                act.wait_ge(s_lnv, b + 1)
                act.activation(rstd[:], lnv[:], ACT.Exp, scale=-0.5).then_inc(s_rstd, 1)

            def batch(t, p, first, last):
                b = 2 * t + p
                for i in range(N):
                    act.wait_ge(s_h, b * N + i + 1)
                    if not (first and i < 3):
                        act.wait_ge(s_o, b * N + i - 2)
                    act.activation(h[i % 3][:], ph[i % 3][:], ACT.Gelu, bias=b1[:, ORDER[i]:ORDER[i] + 1])\
                        .then_inc(s_gelu, 1)
                    if i == 0:
                        act.wait_ge(s_gT, b + 1)
                        act.copy(gT[p][:], pgT[:]).then_inc(s_gT_copied, 1)
                    if not last:
                        if i == 2:
                            rows(b + 1, 1 - p)
                        elif i == 4:
                            exps(b + 1)
                    if i == 7 and not first:
                        root(b - 1)

            rows(0, 0)
            exps(0)
            batch(0, 0, True, False)
            batch(0, 1, False, False)
            with act.Fori(1, PASSES - 1) as t:
                batch(t, 0, False, False)
                batch(t, 1, False, False)
            batch(PASSES - 1, 0, False, False)
            batch(PASSES - 1, 1, False, True)
            root(B - 1)

        @block.vector
        def _(dve):
            dve.memset(eps[:], LN_EPS).then_inc(s_zero, 1)
            for p in range(2):
                dve.sem_inc(s_free[p], 1)
            weights.wait(dve)
            dve.wait_ge(s_zero, 2)
            shape = [P, QT, NE]
            LINKS = 16

            def largest(chain, src, m, onehot):
                chain.link(dve.tensor_reduce(m[:], src[:], AX.X, ALU.max))
                chain.link(dve.tensor_tensor(t8[:], src[:], m[:].unsqueeze(2).broadcast_to(shape), ALU.is_equal))
                chain.link(dve.tensor_tensor(t8[:], t8[:], iota8m[:], ALU.mult))
                chain.link(dve.tensor_reduce(low[:], t8[:], AX.X, ALU.min))
                chain.link(dve.tensor_tensor(onehot[:], iota8m[:], low[:].unsqueeze(2).broadcast_to(shape),
                                             ALU.is_equal))

            def gating(t, p, chain, part):
                if part == 0:
                    dve.wait_ge(s_e, 2 * t + p + 1)
                    chain.link(dve.tensor_scalar(s1[:], e[:], 1.0, None, ALU.add))
                    chain.link(dve.reciprocal(s2[:], s1[:]))
                    chain.link(dve.tensor_scalar(s1[:], s2[:], rscale[:, 0:1], None, ALU.mult))
                elif part == 1:
                    largest(chain, s1, m1, one1)
                elif part == 2:
                    chain.link(dve.scalar_tensor_tensor(s2[:], one1[:], NEG, s1[:], ALU.mult, ALU.add))
                    largest(chain, s2, m2, one2)
                else:
                    dve.tensor_tensor(m1[:], m1[:], m2[:], ALU.add)
                    chain.link(dve.tensor_tensor(one1[:], one1[:], one2[:], ALU.add))
                    dve.reciprocal(m2[:], m1[:])
                    chain.link(dve.tensor_tensor(s1[:], s1[:], one1[:], ALU.mult))
                    dve.tensor_tensor(gate[p][:, :, 0:NE], s1[:], m2[:].unsqueeze(2).broadcast_to(shape), ALU.mult)\
                        .then_inc(s_gate, 1)

            def norm(t, p, part):
                b = 2 * t + p
                if part == 0:
                    dve.wait_ge(s_acc, b * N + N)
                    dve.bn_stats(st[:, 0], acc[p][:, 0])
                    dve.bn_stats(st[:, 1], acc[p][:, 1]).then_inc(s_st, 1)
                elif part == 1:
                    dve.wait_ge(s_st, b + 1)
                    dve.nop(nofuse=True)
                    dve.bn_aggr(mv[:, 0], st[:, 0])
                    dve.bn_aggr(mv[:, 1], st[:, 1]).then_inc(s_mv, 1)
                else:
                    dve.wait_ge(s_free[p], t + 1)
                    dve.wait_ge(s_rstd, b + 1)
                    for qt in range(QT):
                        ins = dve.tensor_scalar(y[p][:, qt], acc[p][:, qt], mv[:, qt, 0:1], rstd[:, qt:qt + 1],
                                                ALU.subtract, ALU.mult)
                    ins.then_inc(s_y, 1)

            def batch(t, p, before, last):
                b = 2 * t + p
                chain = Count(dve, s_dve, LINKS, (b + 1) * LINKS)
                for i in range(N):
                    dve.wait_ge(s_o, b * N + i + 1)
                    if i == 0:
                        dve.wait_ge(s_xb, b + 1)
                        if before == 2:
                            dve.wait_ge(s_y, b - 1)
                        ins = dve.tensor_tensor(acc[p][:], po[p][:], x[p][:], ALU.add)
                    else:
                        dve.wait_ge(s_acc, b * N + i)
                        for qt in range(QT):
                            ins = dve.scalar_tensor_tensor(
                                acc[p][:, qt], po[(p + i) % 2][:, qt], gate[p][:, qt, ORDER[i]:ORDER[i] + 1],
                                acc[p][:, qt], ALU.mult, ALU.add)
                    ins.then_inc(s_acc, 1)
                    if i in (0, 1, 8) and before > 0:
                        norm(t + p - 1, 1 - p, min(i, 2))
                    if i in (4, 5, 6, 7) and not last:
                        gating(t + p, 1 - p, chain, i - 4)
                if not last:
                    chain.end()

            chain = Count(dve, s_dve, LINKS, 0)
            for part in range(4):
                gating(0, 0, chain, part)
            chain.end()
            batch(0, 0, 0, False)
            batch(0, 1, 1, False)
            with dve.Fori(1, PASSES - 1) as t:
                batch(t, 0, 2, False)
                batch(t, 1, 2, False)
            batch(PASSES - 1, 0, 2, False)
            batch(PASSES - 1, 1, 2, True)
            for part in range(3):
                norm(PASSES - 1, 1, part)


def build(nc, dram, phases):
    with ExitStack() as ctx:
        rows = TableRows(nc, ctx, dram)
        layer0_attention(nc, dram, rows.share(0, GROUPS // 2))
        if phases < 2:
            return
        with ExitStack() as own:
            x2 = own.enter_context(nc.sbuf_tensor("x2_tok", [P, TT, D], F32))
            pos = own.enter_context(nc.sbuf_tensor("pos", [P, TT], I32))
            te = own.enter_context(nc.sbuf_tensor("tile_expert", [P, TILES], I32))
            wtop = own.enter_context(nc.sbuf_tensor("wtop", [P, TT], F32))
            moe_route(nc, dram, x2, pos[:], te[:], wtop[:], lambda pool: None)
            moe_experts(nc, dram, te[:], lambda pool: None)
            moe_combine(nc, dram, x2, pos[:], wtop[:], lambda pool: None)
        if phases < 3:
            return
        layer1_attention(nc, dram, lambda pool: None)
        if phases < 4:
            return
        weights = ExpertWeights(nc, ctx, dram)
        with ExitStack() as own:
            aT = own.enter_context(nc.sbuf_tensor("aT", [P, 2, BH], F32))
            eT = own.enter_context(nc.sbuf_tensor("eT", [P, 2, BH], F32))
            qblk = own.enter_context(nc.sbuf_tensor("qblk", [P, KT, P, 32], F32))
            kh = own.enter_context(nc.sbuf_tensor("kh", [P, P, 2, BH], F32))
            mlstm_gates(nc, dram, aT, eT, lambda pool: None)
            for vt in range(QT):
                query_blocks(nc, dram, vt, qblk, lambda pool: None)
                hop_scores(nc, dram, vt, qblk, kh, lambda pool: weights.load(pool) if vt == 0 else None)
                mlstm_heads(nc, dram, vt, qblk, kh, aT, eT)
        if phases < 5:
            return
        experts_top2(nc, dram, weights)


def kernel(phases=9, **a):
    import concourse.bacc as _bacc
    from concourse.bass_utils import run_bass_kernel_spmd as _run

    a = {k: np.asarray(v) for k, v in a.items()}

    def kmajor(m):
        return m.reshape(KT, P, -1).transpose(1, 0, 2)

    def tokens_T(m):
        return m.transpose(0, 2, 1).reshape(B, KT, P, S).transpose(0, 2, 1, 3)

    arrays = {
        "x": a["x"], "xT": tokens_T(a["x"]), "cT": tokens_T(a["ctx_1024"]), "ctx": a["ctx_1024"],
        "w": np.stack([kmajor(m) for m in (
            a["L0_attn_Wq"].T, a["L0_attn_Wk"].T, a["L0_attn_Wv"].T, a["L0_attn_Wo"].T,
            a["L0_xattn_Wq"], a["L0_xattn_Wk"], a["L0_xattn_Wv"], a["L0_xattn_Wp"],
            a["L1_attn_Wq"].T, a["L1_attn_Wk"].T, a["L1_attn_Wv"].T)], axis=1),
        "cols": np.stack([m.reshape(2, P).T for m in (
            a["L0_xattn_bq"], a["L0_xattn_bk"], a["L1_attn_bq"], a["L1_attn_bk"])], axis=1),
        "rows": np.broadcast_to(np.stack([
            a["L0_xattn_bv"], a["L0_xattn_bp"], a["L1_attn_bv"], a["L1_xattn_ln_w"], a["L1_xattn_ln_b"],
            a["L1_ffn_bs2"]]), (P, 6, D)),
        "hopsT": hop_units(a["itok_SxS2_0_2016"]), "rpe": a["L1_xattn_rpe"],
        "wg": kmajor(a["L0_ffn_Wg"]), "before": np.triu(np.ones((P, P), np.float32), 1),
        "route": routing_constants(a["L0_ffn_bg"]),
        "w1": a["L0_ffn_W1"].reshape(NE, KT, P, HID).transpose(0, 2, 1, 3),
        "w2": a["L0_ffn_W2"].reshape(NE, HT, P, D).transpose(0, 2, 1, 3),
        "b1": a["L0_ffn_b1"].reshape(NE, HT, P).transpose(0, 2, 1), "b2": a["L0_ffn_b2"],
        "cols1": np.stack([m.reshape(2, P).T for m in (
            a["L1_attn_bq"], a["L1_attn_bk"], pair_swapped(a["L1_attn_bq"]), pair_swapped(a["L1_attn_bk"]),
            pair_signs())], axis=1),
        "rope": rope_tables(),
        "gw": np.concatenate([a["L1_xattn_igate_w"], a["L1_xattn_fgate_w"]]).T.reshape(6, P, 16).transpose(1, 0, 2),
        "gb": np.concatenate([a["L1_xattn_igate_b"], a["L1_xattn_fgate_b"]])[:, None],
        "ctx_ones": values_with_ones(a["ctx_1024"]),
        "gate1": padded(kmajor(a["L1_ffn_gate_W"]), 2), "rscale": np.broadcast_to(a["L1_ffn_route_scale"].reshape(1, 1), (P, 1)),
        "iota8m": np.broadcast_to((np.arange(NE) - NE).astype(np.float32), (P, QT, NE)),
        "f_w1": np.concatenate([a["L1_ffn_W1"], a["L1_ffn_Ws1"][None]]).reshape(NE + 1, KT, P, HID1)
        .transpose(2, 1, 0, 3),
        "f_w2": np.concatenate([a["L1_ffn_W2"], a["L1_ffn_Ws2"][None]]).transpose(1, 0, 2),
        "f_b1": np.concatenate([a["L1_ffn_b1"], a["L1_ffn_bs1"][None]]).T, "f_b2": padded(a["L1_ffn_b2"], 0),
        "masks8": head_masks(), "masks": window_masks(), "ident": np.eye(P, dtype=np.float32),
    }
    nc = _bacc.Bacc("TRN2", target_bir_lowering=False, num_devices=1)
    dram, given = {}, {}
    for name, m in arrays.items():
        m = np.ascontiguousarray(m)
        given["in_" + name] = m
        dram[name] = nc.dram_tensor("in_" + name, m.shape, mybir.dt.from_np(m.dtype), kind="ExternalInput").ap()
    dram["out"] = nc.dram_tensor("out", (B, S, D), F32, kind="ExternalOutput").ap()
    for name, shape in (("x2", (B, S, D)), ("x3", (B, S, D)), ("xs", (TILES * P, D)), ("ys", (TILES * P, D)),
                        ("x4", (B, S, D)), ("x4T", (B, P, KT, S)), ("gate_i", (B, 8, S)), ("gate_f", (B, 8, S)), ("x5", (B, S, D)),
                        ("runmax", (BH, S))):
        dram[name] = nc.dram_tensor(name, shape, F32, kind="Internal").ap()
    dram[{1: "x2", 2: "x3", 3: "x4", 4: "x5"}.get(phases, "nothing")] = dram["out"]
    dram["pos_rows"] = nc.dram_tensor("pos_rows", (GROUPS, P, GROUP * D), F32, kind="Internal").ap()
    build(nc, dram, phases)
    r = _run(nc, [given], core_ids=[0])
    return r.results[0]["out"]


def padded(m, axis):
    return np.pad(m, [(0, P - n if i == axis else 0) for i, n in enumerate(m.shape)])


def head_masks():
    head = np.arange(P)[:, None] // HD
    return ((head == np.arange(8)) / np.sqrt(HD)).astype(np.float32)


def window_masks():
    q, k = np.arange(P)[:, None], np.arange(P)[None, :]
    first = np.where((k <= q) & (k > q - WINDOW), 0.0, NEG)
    q, k = q + P, np.arange(64, 256)[None, :]
    second = np.where((k <= q) & (k > q - WINDOW), 0.0, NEG)
    return np.concatenate([first] * 4 + [second] * 2, axis=1).astype(np.float32)


def hop_units(hops):
    t = hops.T.reshape(2, P, S)
    late = t[:, :, P:].transpose(1, 2, 0).reshape(P, 2 * P)
    return np.concatenate([t[0, :, :P], late], axis=1)


def routing_constants(bg):
    row = np.concatenate([
        np.tile(np.arange(NE) - NE, TT), np.tile(bg, TT), np.tile(np.arange(TT) * P, NE),
        np.repeat(np.arange(TILES), NE)]).astype(np.float32)
    return np.broadcast_to(row, (P, row.size))


def pair_swapped(v):
    return v.reshape(-1, 2)[:, ::-1].reshape(-1)


def pair_signs():
    return np.tile(np.array([-1.0, 1.0], np.float32), D // 2)


def rope_tables():
    head = 128
    pos = np.arange(S, dtype=np.float32)
    inv = np.power(np.float32(10000.0), np.arange(0, head, 2, dtype=np.float32) / np.float32(head))
    rad = pos[:, None] / inv
    t = np.repeat(np.stack((np.sin(rad), np.cos(rad)), axis=-1).reshape(S, -1), 2, axis=-1)
    t = t.T.reshape(KT, P, S).transpose(1, 0, 2)
    return np.stack([t, t / np.float32(np.sqrt(head))], axis=1).astype(np.float32)


def values_with_ones(ctx):
    v = ctx.reshape(B, 2, P, H1, HW).transpose(0, 2, 1, 3, 4)
    return np.concatenate([v, np.ones(v.shape[:-1] + (1,), v.dtype)], axis=-1).reshape(B, P, 2, H1 * (HW + 1))
```

```python
from contextlib import ExitStack

import numpy as np

import concourse.bass as bass
from concourse import mybir

ALU = mybir.AluOpType
ACT = mybir.ActivationFunctionType
AX = mybir.AxisListType
F32 = mybir.dt.float32
BF16 = mybir.dt.bfloat16
I32 = mybir.dt.int32
U32 = mybir.dt.uint32

P = 128
B = 8
S = 256
D = 256
KT = D // P
QT = S // P
NH = 16
HD = D // NH
WINDOW = 64
LN_EPS = 1e-5
NEG = -1.0e30

WQ0, WK0, WV0, WO0, XQ, XK, XV, XP, WQ1, WK1, WV1 = range(11)
C_BQ, C_BK, C_B1Q, C_B1K = range(4)
R_BV, R_BP, R_B1V, R_LNW, R_LNB, R_BS2 = range(6)


class Count:

    def __init__(self, engine, sem, per_pass, base):
        self.engine, self.sem, self.per_pass, self.base, self.n = engine, sem, per_pass, base, 0

    def link(self, ins):
        ins.then_inc(self.sem, 1)
        self.n += 1
        self.engine.wait_ge(self.sem, self.base + self.n)

    def end(self):
        assert self.n == self.per_pass, self.n


def phase_semaphores(nc, ctx, prefix):
    made = []

    def sem(name):
        made.append(nc.alloc_semaphore(prefix + name))
        return made[-1]

    def clear():
        nc.clear_and_free_semaphores(made)
        nc.all_engine_barrier(sem_only=True)

    ctx.callback(clear)
    return sem


def units():
    out = []
    for g in range(4):
        out.append(dict(layer=0, qt=0, g=g, heads=[(t, par) for t in range(2) for par in range(2)], k0=0, nk=128))
    for t in range(2):
        for g in range(4):
            out.append(dict(layer=0, qt=1, g=g, heads=[(t, 0), (t, 1)], k0=64, nk=192))
    for qt in range(QT):
        for t in range(2):
            for g in range(4):
                out.append(dict(layer=1, qt=qt, g=g, heads=[(t, 0), (t, 1)], k0=0, nk=256))
    return out


UNITS = units()
NU = len(UNITS)
NU0 = 12
OF_LAYER = (range(NU0), range(NU0, NU))
ON_ACT = (1, 3)
WO, K0, Q0, V0, TURN, XP_, XQ_, XK_, XV_ = range(9)
STEPS = 9


NPROBS = 4


def head_of(t, g, par):
    return 8 * t + 2 * g + par


def layer0_attention(nc, dram, pool_share):
    with ExitStack() as ctx:
        def sb(name, shape, dt=F32):
            return ctx.enter_context(nc.sbuf_tensor("a_" + name, shape, dt))

        sem = phase_semaphores(nc, ctx, "a_")

        w = sb("w", [P, 8, KT, D])
        cols = sb("cols", [P, 4, 2])
        rows = sb("rows", [P, 2, D])
        ident = sb("ident", [P, P])
        identb = sb("identb", [P, P], BF16)
        mask0 = sb("mask0", [P, 4, 128], BF16)
        mask1 = sb("mask1", [P, 2, 192], BF16)
        maskf = sb("maskf", [P, 4 * 128 + 2 * 192])
        eps = sb("eps", [P, 1])
        xT = sb("xT", [P, KT, S])
        cT = sb("cT", [P, KT, S])
        xin = sb("xin", [P, QT, D])
        kT = [sb(f"kT{i}", [P, 2, S]) for i in range(2)]
        masks8 = sb("masks8", [P, 8])
        qT = sb("qT", [P, 2, S])
        qm = [[sb(f"qm{L}{m}", [P, 2, S]) for m in range(8)] for L in range(2)]
        v = [sb(f"v{i}", [P, QT, NH, 2 * HD]) for i in range(2)]
        probs = [sb(f"probs{i}", [P, 512]) for i in range(NPROBS)]
        probs_w = [sb(f"probs_w{i}", [P, 2, 256]) for i in range(NPROBS)]
        probsT = [sb(f"probsT{i}", [P, 4, P]) for i in range(2)]
        negmax = sb("negmax", [P, 4, 4])
        rsum = sb("rsum", [P, QT, NH])
        rinv = sb("rinv", [P, QT, NH])
        oT = sb("oT", [P, KT, S])
        y = [sb(f"y{i}", [P, QT, D]) for i in range(2)]
        x1 = sb("x1", [P, QT, D])
        x1r = sb("x1r", [P, QT, D])
        x1T = sb("x1T", [P, KT, S])
        x2 = sb("x2", [P, QT, D])
        st = sb("st", [P, QT, 6])
        mv = sb("mv", [P, QT, 2])
        lnv = sb("lnv", [P, QT])
        rstd = sb("rstd", [P, QT])
        sc = [ctx.enter_context(nc.psum_tensor(f"a_sc{i}", [P, 512], F32)) for i in range(4)]
        pt = [ctx.enter_context(nc.psum_tensor(f"a_pt{i}", [P, 512], F32)) for i in range(2)]
        op = ctx.enter_context(nc.psum_tensor("a_op", [P, 512], F32))
        mi = ctx.enter_context(nc.psum_tensor("a_mi", [P, 2, 256], F32))

        zeros = sb("zeros", [P, TILES * D // 4])
        s_zeroed = sem("zeroed")
        s_const = sem("const")
        s_maskb = sem("maskb")
        s_zero = sem("zero")
        s_xT = sem("xT")
        s_xin = sem("xin")
        s_cT = sem("cT")
        s_step = sem("step")
        s_copied = sem("copied")
        s_scores = sem("scores")
        s_max = sem("max")
        s_exp = sem("exp")
        s_turned = sem("turned")
        s_evac_dve = sem("evac_dve")
        s_evac_act = sem("evac_act")
        s_pv = sem("pv")
        s_rinv = sem("rinv")
        s_qm = [sem(f"qm{L}") for L in range(2)]
        s_norm = sem("norm")
        s_oT = sem("oT")
        s_stats = sem("stats")
        s_rstd = sem("rstd")
        s_x1 = sem("x1")
        s_x1r = sem("x1r")
        s_x2 = sem("x2")
        s_x2_out = sem("x2_out")
        s_x2_free = sem("x2_free")
        s_dve = sem("dve")
        s_ln = sem("ln")
        block = ctx.enter_context(nc.Block())

        def step_of(b, n):
            return 3 + b * STEPS + n

        def wait_evac(eng, base4, u):
            mine = ON_ACT if u % 4 in ON_ACT else [x for x in range(4) if x not in ON_ACT]
            eng.wait_ge(s_evac_act if u % 4 in ON_ACT else s_evac_dve,
                        base4 * len(mine) + u // 4 * len(mine) + list(mine).index(u % 4) + 1)

        def unit_at(i, L, before, after):
            n = len(OF_LAYER[L])
            if i < 0:
                return None if before is None else (before, UNITS[OF_LAYER[before][i]])
            if i >= n:
                return None if after is None else (after, UNITS[OF_LAYER[after][i - n]])
            return L, UNITS[OF_LAYER[L][i]]

        def schedule(run, others, loop):
            def alone(part, b):
                for _, work in others(part, b):
                    work()

            alone("first", 0)
            run(0, 0, None, None, [], (0, 2), 0, None)
            alone("A", 0)
            run(3, 0, None, 1, others("B", 0), (step_of(0, K0), step_of(0, V0)), 1, None)

            def round_(b):
                run(7 * b - 1, 1, 0, 0, others("A", b), (step_of(b - 1, XK_), step_of(b - 1, XV_)), 2 * b,
                    step_of(b - 1, XP_))
                run(7 * b + 3, 0, 1, 1, others("B", b), (step_of(b, K0), step_of(b, V0)), 2 * b + 1, step_of(b, WO))

            loop(round_)
            b = B - 1
            run(7 * b - 1, 1, 0, None, others("A", b), (step_of(b - 1, XK_), step_of(b - 1, XV_)), 2 * b,
                (step_of(b - 1, XP_), step_of(b, WO)))
            alone("B", b)
            run(7 * b + 3, 1, None, None, [], (step_of(b, XK_), step_of(b, XV_)), 2 * b + 1, step_of(b, XP_))
            alone("last", b + 1)

        @block.sync
        def _(sp):
            sp.dma_start(ident[:], dram["ident"]).then_inc(s_const, 16)
            sp.dma_start(w[:, 0:4], dram["w"][:, 0:4]).then_inc(s_const, 16)
            sp.dma_start(cols[:], dram["cols"]).then_inc(s_const, 16)
            sp.dma_start(masks8[:], dram["masks8"]).then_inc(s_const, 16)
            sp.dma_start(xT[:], dram["xT"][0]).then_inc(s_xT, 16)
            sp.dma_start(maskf[:], dram["masks"]).then_inc(s_const, 16)
            sp.dma_start(xin[:], dram["x"][0].rearrange("(t p) d -> p t d", p=P)).then_inc(s_xin, 16)
            sp.dma_start(w[:, 4:8], dram["w"][:, 4:8]).then_inc(s_const, 16)
            sp.dma_start(rows[:], dram["rows"][:, 0:2]).then_inc(s_const, 16)
            sp.dma_start(cT[:], dram["cT"][0]).then_inc(s_cT, 16)
            sp.wait_ge(s_zero, 1)
            for i in range(4):
                sp.dma_start(dram["xs"].rearrange("(p r) d -> p (r d)", p=P)[:, i * zeros.shape[1]:(i + 1) * zeros.shape[1]],
                             zeros[:]).then_inc(s_zeroed, 16)

            def load_xT(b):
                sp.dma_start(xT[:], dram["xT"][bass.ds(b, 1)].rearrange("b p k s -> p (b k) s")).then_inc(s_xT, 16)

            def store(b):
                sp.wait_ge(s_x2, b + 2)
                sp.dma_start(dram["x2"][bass.ds(b, 1)].rearrange("b (t p) d -> p (b t) d", p=P),
                             x2[:]).then_inc(s_x2_out, 16)
                sp.wait_ge(s_x2_out, 16 * b + 16)
                sp.sem_inc(s_x2_free, 1)

            def round_(b, first=False, last=False):
                sp.wait_ge(s_copied, step_of(b, WO) + 2)
                sp.dma_start(xin[:], dram["x"][bass.ds(b + 1, 1)].rearrange("b (t p) d -> p (b t) d", p=P))\
                    .then_inc(s_xin, 16)
                if not last:
                    sp.wait_ge(s_step, step_of(b, V0) + 1)
                    load_xT(b + 2)
                if not first:
                    store(b - 1)
                sp.wait_ge(s_step, step_of(b, XV_) + 1)
                sp.dma_start(cT[:], dram["cT"][bass.ds(b + 1, 1)].rearrange("b p k s -> p (b k) s"))\
                    .then_inc(s_cT, 16)

            sp.wait_ge(s_step, 3)
            load_xT(1)
            round_(0, first=True)
            with sp.Fori(1, B - 2) as b:
                round_(b)
            round_(B - 2, last=True)
            store(B - 2)
            store(B - 1)
            sp.wait_ge(s_zeroed, 64)

        @block.gpsimd
        def _(pool):
            pool.memset(zeros[:], 0.0).then_inc(s_zero, 1)
            for i in range(NPROBS):
                pool.memset(probs_w[i][:, :, 0:64], 0.0).then_inc(s_zero, 1)
            for i in range(2):
                pool.memset(v[i][:], 0.0).then_inc(s_zero, 1)
            pool_share(pool)

        @block.scalar
        def _(act):
            act.preload_act_table_set("natural_log_exp_and_others")
            act.wait_ge(s_zero, NPROBS + 3)
            act.wait_ge(s_const, 16 * 7)

            def exps(g, i, L, un, first):
                act.wait_ge(s_max, g + 1)
                if not first:
                    act.wait_ge(s_turned, g - NPROBS + 1)
                for j, (t, par) in enumerate(un["heads"]):
                    h = head_of(t, un["g"], par)
                    if L == 0 and un["qt"] == 1:
                        dst = probs_w[i % NPROBS][:, j, 64:256]
                    else:
                        dst = probs[i % NPROBS][:, j * un["nk"]:(j + 1) * un["nk"]]
                    ins = act.activation(dst, sc[i % 4][:, j * un["nk"]:(j + 1) * un["nk"]], ACT.Exp,
                                         bias=negmax[:, i % 4, j:j + 1],
                                         accum_out=rsum[:, un["qt"], h:h + 1])
                ins.then_inc(s_exp, 1)

            def evac(g, i, first):
                act.wait_ge(s_turned, g + 1)
                if not first:
                    act.wait_ge(s_pv, g - 1)
                act.copy(probsT[i % 2][:], pt[i % 2][:]).then_inc(s_evac_act, 1)

            def outputs(units, read):
                act.wait_ge(s_pv, units)
                if read is not None:
                    act.wait_ge(s_step, read + 1)
                act.copy(oT[:], op[:]).then_inc(s_oT, 1)

            def run(base4, L, before, after, work, kv, count, read):
                base, n = 4 * base4, len(OF_LAYER[L])
                very_first = count == 0 if isinstance(count, int) else False
                read_before, read_own = read if isinstance(read, tuple) else (read, read)
                for i in range(n + (1 if after is None else 0)):
                    if i < n:
                        exps(base + i, i, *unit_at(i, L, before, after), very_first and i < NPROBS)
                    if (i > 0 or before is not None) and (i - 1) % 4 in ON_ACT:
                        evac(base + i - 1, i - 1, very_first and i - 1 < 2)
                    if i == 2 and before is not None:
                        outputs(base, read_before)
                    for at, what in work:
                        if at == i:
                            what()
                if after is None:
                    outputs(base + n, read_own)

            def step(idx):
                act.wait_ge(s_step, idx + 1)

            def rsqrt(j):
                act.wait_ge(s_stats, j + 1)
                act.activation(lnv[:], mv[:, :, 1], ACT.Ln, bias=eps[:]).then_inc(s_ln, 1)
                act.wait_ge(s_ln, j + 1)
                act.activation(rstd[:], lnv[:], ACT.Exp, scale=-0.5).then_inc(s_rstd, 1)

            def keys(L, idx, units):
                step(idx)
                if units is not None:
                    act.wait_ge(s_pv, units)
                if L == 0:
                    act.copy(kT[0][:], mi[:]).then_inc(s_copied, 1)
                else:
                    for et in range(2):
                        ins = act.activation(kT[1][:, et], mi[:, et], ACT.Identity, bias=cols[:, C_BK, et:et + 1])
                    ins.then_inc(s_copied, 1)

            def queries(L, idx):
                step(idx)
                if L == 0:
                    act.copy(qT[:], mi[:]).then_inc(s_copied, 1)
                else:
                    for et in range(2):
                        ins = act.activation(qT[:, et], mi[:, et], ACT.Identity, bias=cols[:, C_BQ, et:et + 1])
                    ins.then_inc(s_copied, 1)

            def mask_queries(L, idx, units, ms):
                act.wait_ge(s_copied, idx + 2)
                if units is not None:
                    act.wait_ge(s_pv, units)
                for m in ms:
                    act.activation(qm[L][m][:], qT[:], ACT.Copy, scale=masks8[:, m:m + 1]).then_inc(s_qm[L], 1)

            def pairs(ap, par):
                return ap[:, :, par::2, par * HD:(par + 1) * HD]

            def values(idx, units):
                step(idx)
                if units is not None:
                    act.wait_ge(s_pv, units)
                heads = mi[:].rearrange("p t (h d) -> p t h d", d=HD)
                act.copy(pairs(v[0], 0), heads[:, :, 0::2])
                act.copy(pairs(v[0], 1), heads[:, :, 1::2]).then_inc(s_copied, 1)

            def turned(idx):
                step(idx)
                act.copy(x1T[:], mi[:]).then_inc(s_copied, 1)

            def masks(at, L, idx, units):
                return [(at + q, lambda ms=(2 * q, 2 * q + 1): mask_queries(L, idx, units, ms)) for q in range(4)]

            def others(part, b):
                if part == "first":
                    return [(0, lambda: keys(0, 0, None)), (0, lambda: queries(0, 1)), *masks(0, 0, 1, None),
                            (0, lambda: values(2, None))]
                if part == "last":
                    return [(0, lambda: rsqrt(2 * B - 1))]
                if part == "A":
                    first, last = isinstance(b, int) and b == 0, isinstance(b, int) and b == B - 1
                    units = 12 if first else 28 * b - 4
                    before_turn = [] if last else [
                        (6, lambda: keys(0, step_of(b, K0), units)), (8, lambda: queries(0, step_of(b, Q0))),
                        *masks(8, 0, step_of(b, Q0), units), (10, lambda: values(step_of(b, V0), units))]
                    return [(5, lambda: rsqrt(0 if first else 2 * b - 1)), *before_turn,
                            (12, lambda: turned(step_of(b, TURN)))]
                units = 28 * b + 12
                own = [(8, lambda: keys(1, step_of(b, XK_), units))]
                if isinstance(b, int) and b == B - 1:
                    units = 28 * b + 12
                    own = [(8, lambda: keys(1, step_of(b, XK_), units))]
                return ([] if isinstance(b, int) and b == 0 else [(5, lambda: rsqrt(2 * b))]) + [
                    (6, lambda: queries(1, step_of(b, XQ_))), *masks(6, 1, step_of(b, XQ_), units), *own]

            def loop(round_):
                with act.Fori(1, B - 1) as b:
                    round_(b)

            schedule(run, others, loop)

        @block.tensor
        def _(pe):
            pe.wait_ge(s_const, 16 * 7)
            pe.wait_ge(s_maskb, 4)

            def free(idx):
                pe.wait_ge(s_copied, idx + 1)

            def skip(idx):
                free(idx)
                pe.sem_inc(s_step, 1)
                pe.sem_inc(s_copied, 1)

            def project_T(idx, wi, src):
                free(idx)
                for et in range(2):
                    for k in range(KT):
                        ins = pe.matmul(mi[:, et], w[:, wi, k, et * P:(et + 1) * P], src[:, k, :],
                                        start=(k == 0), stop=(k == KT - 1))
                ins.then_inc(s_step, 1)

            def project(idx, wi, srcT):
                free(idx)
                for qt in range(QT):
                    for k in range(KT):
                        ins = pe.matmul(mi[:, qt], srcT[:, k, qt * P:(qt + 1) * P], w[:, wi, k, :],
                                        start=(k == 0), stop=(k == KT - 1))
                ins.then_inc(s_step, 1)

            def turn(idx, src):
                free(idx)
                for k in range(KT):
                    for qt in range(QT):
                        ins = pe.transpose(mi[:, k, qt * P:(qt + 1) * P], src[:, qt, k * P:(k + 1) * P], ident[:])
                ins.then_inc(s_step, 1)

            def scores(g, i, L, un, first, k_ready, b):
                hg, nk, qt = un["g"], un["nk"], un["qt"]
                bank = sc[i % 4]
                if not first:
                    pe.wait_ge(s_exp, g - 3)
                if L == 0:
                    mask = mask0 if qt == 0 else mask1
                    width = len(un["heads"]) * nk
                    pe.matmul(bank[:, 0:width], identb[:], mask[:].rearrange("p h k -> p (h k)"),
                              start=True, stop=True, skip_group_check=True)
                if i == 0:
                    pe.wait_ge(s_copied, k_ready + 2)
                if i < 4:
                    pe.wait_ge(s_qm[L], b * 8 + 2 * hg + 2)
                for j, (t, par) in enumerate(un["heads"]):
                    ins = pe.matmul(bank[:, j * nk:(j + 1) * nk],
                                    qm[L][2 * hg + par][:, t, qt * P:(qt + 1) * P], kT[L][:, t, un["k0"]:un["k0"] + nk],
                                    start=(L == 1), stop=True, skip_group_check=True)
                ins.then_inc(s_scores, 1)

            def transposes(base4, i, L, un, first):
                g = 4 * base4 + i
                pe.wait_ge(s_norm, g + 1)
                if not first:
                    wait_evac(pe, base4 if i >= 2 else base4 - 1, i - 2 if i >= 2 else i + 2)
                if L == 0 and un["qt"] == 1:
                    src = probs_w[i % NPROBS][:].rearrange("p h k -> p (h k)")
                else:
                    src = probs[i % NPROBS][:]
                for c in range(4):
                    ins = pe.transpose(pt[i % 2][:, c * P:(c + 1) * P], src[:, c * P:(c + 1) * P], ident[:])
                ins.then_inc(s_turned, 1)

            def pv(base4, i, L, un):
                wait_evac(pe, base4 if i >= 0 else base4 - 1, i if i >= 0 else i + 4)
                nc_ = 1 if un["nk"] == 128 else 2
                g = un["g"]
                for j, (t, par) in enumerate(un["heads"]):
                    at = t * S + un["qt"] * P
                    for c in range(nc_):
                        ins = pe.matmul(op[32 * g:32 * g + 32, at:at + P],
                                        v[L][:, c, head_of(t, g, par), :],
                                        probsT[i % 2][:, j * nc_ + c, :],
                                        start=(par == 0 and c == 0), stop=(par == 1 and c == nc_ - 1),
                                        skip_group_check=True)
                ins.then_inc(s_pv, 1)

            def run(base4, L, before, after, work, kv, count, read):
                base, n = 4 * base4, len(OF_LAYER[L])
                very_first = isinstance(count, int) and count == 0
                b_own, b_next, k_next = batches(L, count, kv)
                if before is None:
                    for i in range(3):
                        scores(base + i, i, *unit_at(i, L, before, after), very_first, kv[0], b_own)
                for i in range(n + (2 if after is None else 0)):
                    if i + 3 < n:
                        scores(base + i + 3, i + 3, *unit_at(i + 3, L, before, after), very_first and i + 3 < 4, kv[0], b_own)
                    elif i < n and after is not None:
                        scores(base + i + 3, i + 3 - n, *unit_at(i + 3, L, before, after), False, k_next, b_next)
                    if i < n:
                        transposes(base4, i, *unit_at(i, L, before, after), very_first and i < 2)
                    if i >= 2 or before is not None:
                        if i == 2:
                            pe.wait_ge(s_copied, kv[1] + 2)
                            if not very_first:
                                pe.wait_ge(s_oT, count)
                        pv(base4, i - 2, *unit_at(i - 2, L, before, after))
                    for at, what in work:
                        if at == i:
                            what()

            def batches(L, count, kv):
                if isinstance(count, int):
                    b = count // 2
                    if count == 0:
                        return 0, None, None
                    if count % 2 == 1 and L == 0:
                        return b + 1, b, step_of(b, XK_)
                    if count % 2 == 1:
                        return b, None, None
                    return b - 1, b + 1, step_of(b, K0)
                b = in_loop[0]
                return (b - 1, b + 1, step_of(b, K0)) if L == 1 else (b + 1, b, step_of(b, XK_))

            in_loop = [None]

            def residual(idx, wi, outputs):
                pe.wait_ge(s_oT, outputs)
                project(idx, wi, oT)

            def context(idx, b, product, wi):
                pe.wait_ge(s_cT, 16 * b + 16)
                product(idx, wi, cT)

            def inputs(idx, b, product, wi):
                pe.wait_ge(s_xT, 16 * b + 16)
                product(idx, wi, xT)

            def turn_x1(idx, b):
                pe.wait_ge(s_x1, b + 1)
                turn(idx, x1)

            def queries_x1(idx, b):
                pe.wait_ge(s_copied, step_of(b, TURN) + 2)
                project_T(idx, XQ, x1T)

            def others(part, b):
                if part == "first":
                    return [(0, lambda: inputs(0, 0, project_T, WK0)), (0, lambda: inputs(1, 0, project_T, WQ0)),
                            (0, lambda: inputs(2, 0, project, WV0))]
                first, last = isinstance(b, int) and b == 0, isinstance(b, int) and b == B - 1
                if part == "last":
                    return [(0, lambda: residual(step_of(b, 0), XP, 2 * B))]
                if part == "A":
                    out = [(2, lambda: residual(step_of(b, WO), WO0, 1 if first else 2 * b))]
                    if last:
                        out += [(4, lambda n=n: skip(step_of(b, n))) for n in (K0, Q0, V0)]
                    else:
                        out += [(4, lambda: inputs(step_of(b, K0), b + 1, project_T, WK0)),
                                (6, lambda: inputs(step_of(b, Q0), b + 1, project_T, WQ0)),
                                (8, lambda: inputs(step_of(b, V0), b + 1, project, WV0))]
                    return out + [(10, lambda: turn_x1(step_of(b, TURN), b))]
                return [(2, (lambda: skip(step_of(b, XP_))) if first else
                         (lambda: residual(step_of(b, XP_), XP, 2 * b + 1))),
                        (4, lambda: queries_x1(step_of(b, XQ_), b)),
                        (6, lambda: context(step_of(b, XK_), b, project_T, XK)),
                        (8, lambda: context(step_of(b, XV_), b, project, XV))]

            def loop(round_):
                with pe.Fori(1, B - 1) as b:
                    in_loop[0] = b
                    round_(b)

            schedule(run, others, loop)

        @block.vector
        def _(dve):
            dve.memset(eps[:], LN_EPS).then_inc(s_maskb, 1)
            dve.sem_inc(s_copied, 1)
            dve.sem_inc(s_x2, 1)
            dve.sem_inc(s_x2_free, 1)
            dve.wait_ge(s_const, 16 * 7)
            dve.tensor_copy(mask0[:].rearrange("p h k -> p (h k)"), maskf[:, 0:512]).then_inc(s_maskb, 1)
            dve.tensor_copy(mask1[:].rearrange("p h k -> p (h k)"), maskf[:, 512:896]).then_inc(s_maskb, 1)
            dve.tensor_copy(identb[:], ident[:]).then_inc(s_maskb, 1)

            def row_max(g, i, L, un):
                n = len(un["heads"])
                dve.wait_ge(s_scores, g + 1)
                dve.tensor_reduce(negmax[:, i % 4, 0:n],
                                  sc[i % 4][:, 0:n * un["nk"]].rearrange("p (h k) -> p h k", h=n),
                                  AX.X, ALU.max, negate=True).then_inc(s_max, 1)

            def evac(g, i, first):
                dve.wait_ge(s_turned, g + 1)
                if not first:
                    dve.wait_ge(s_pv, g - 1)
                dve.tensor_copy(probsT[i % 2][:].rearrange("p h k -> p (h k)"), pt[i % 2][:])\
                    .then_inc(s_evac_dve, 1)

            def normalise(g, i, L, un):
                hs = [head_of(t, un["g"], par) for t, par in un["heads"]]
                dve.wait_ge(s_exp, g + 1)
                r = rsum[:, un["qt"]].rearrange("p (t h) -> p t h", t=2)
                ri = rinv[:, un["qt"]].rearrange("p (t h) -> p t h", t=2)
                hg, (t0, t1) = un["g"], (un["heads"][0][0], un["heads"][-1][0] + 1)
                dve.reciprocal(ri[:, t0:t1, 2 * hg:2 * hg + 2], r[:, t0:t1, 2 * hg:2 * hg + 2]).then_inc(s_rinv, 1)
                dve.wait_ge(s_rinv, g + 1)
                for j, h in enumerate(hs):
                    if L == 0 and un["qt"] == 1:
                        p = probs_w[i % NPROBS][:, j, 64:256]
                    else:
                        p = probs[i % NPROBS][:, j * un["nk"]:(j + 1) * un["nk"]]
                    ins = dve.tensor_scalar(p, p, rinv[:, un["qt"], h:h + 1], None, ALU.mult)
                ins.then_inc(s_norm, 1)

            def run(base4, L, before, after, work, kv, count, read):
                base, n = 4 * base4, len(OF_LAYER[L])
                very_first = isinstance(count, int) and count == 0
                for i in range(n + (2 if after is None else 0)):
                    if i < n:
                        row_max(base + i, i, *unit_at(i, L, before, after))
                    if (i > 0 or before is not None) and i <= n:
                        normalise(base + i - 1, i - 1, *unit_at(i - 1, L, before, after))
                    if (i > 1 or before is not None) and (i - 2) % 4 not in ON_ACT:
                        evac(base + i - 2, i - 2, very_first and i - 2 < 2)
                    for at, what in work:
                        if at == i:
                            what()

            def statistics(j, L):
                dve.bn_stats(st[:, 0], y[L][:, 0])
                dve.bn_stats(st[:, 1], y[L][:, 1]).then_inc(s_dve, 1)
                dve.wait_ge(s_dve, j + 1)
                dve.nop(nofuse=True)
                dve.bn_aggr(mv[:, 0], st[:, 0])
                dve.bn_aggr(mv[:, 1], st[:, 1]).then_inc(s_stats, 1)

            def scaled(j, L, dst, done):
                dve.wait_ge(s_rstd, j + 1)
                dve.wait_ge(s_stats, j + 1)
                for qt in range(QT):
                    ins = dve.tensor_scalar(dst[:, qt], y[L][:, qt], mv[:, qt, 0:1], rstd[:, qt:qt + 1],
                                            ALU.subtract, ALU.mult)
                ins.then_inc(done, 1)

            def windowed(idx, b, j, first):
                dve.wait_ge(s_step, idx + 1)
                dve.wait_ge(s_xin, 16 * b + 16)
                if not first:
                    dve.wait_ge(s_x1, b)
                dve.tensor_tensor(y[0][:], mi[:], xin[:], ALU.add).then_inc(s_copied, 1)
                dve.wait_ge(s_copied, idx + 2)
                statistics(j, 0)

            def crossed(idx, b, j):
                dve.wait_ge(s_step, idx + 1)
                dve.wait_ge(s_x1r, b + 1)
                dve.wait_ge(s_x2, b + 1)
                dve.tensor_tensor(y[1][:], mi[:], x1r[:], ALU.add).then_inc(s_copied, 1)
                dve.wait_ge(s_copied, idx + 2)
                statistics(j, 1)

            def scaled_x2(b, j):
                dve.wait_ge(s_x2_free, b + 1)
                scaled(j, 1, x2, s_x2)

            def with_bias(b):
                dve.wait_ge(s_x1, b + 1)
                dve.tensor_tensor(x1r[:], x1[:], rows[:, 1].unsqueeze(1).broadcast_to([P, QT, D]), ALU.add)\
                    .then_inc(s_x1r, 1)

            def scaled_x1(b, j, first):
                if not first:
                    dve.wait_ge(s_x1r, b)
                scaled(j, 0, x1, s_x1)

            def values(idx, units):
                dve.wait_ge(s_step, idx + 1)
                dve.wait_ge(s_pv, units)
                for par in range(2):
                    own = rows[:, 0].rearrange("p (h d) -> p h d", d=HD)[:, par::2]
                    ins = dve.tensor_tensor(
                        v[1][:, :, par::2, par * HD:(par + 1) * HD],
                        mi[:].rearrange("p t (h d) -> p t h d", d=HD)[:, :, par::2],
                        own.unsqueeze(1).broadcast_to([P, QT, NH // 2, HD]), ALU.add)
                ins.then_inc(s_copied, 1)

            def others(part, b):
                if part == "first":
                    return []
                first = isinstance(b, int) and b == 0
                if part == "last":
                    return [(0, lambda: crossed(step_of(b, 0), B - 1, 2 * B - 1)),
                            (0, lambda: scaled_x2(B - 1, 2 * B - 1))]
                if part == "A":
                    j = 0 if first else 2 * b - 1
                    return [(4, lambda: windowed(step_of(b, WO), b, j, first)), (6, lambda: scaled_x1(b, j, first))]
                out = [] if first else [(4, lambda: crossed(step_of(b, XP_), b - 1, 2 * b)),
                                        (6, lambda: scaled_x2(b - 1, 2 * b))]
                return out + [(7, lambda: with_bias(b)), (10, lambda: values(step_of(b, XV_), 28 * b + 12))]

            def loop(round_):
                with dve.Fori(1, B - 1) as b:
                    round_(b)

            schedule(run, others, loop)


GROUP = 4
UNITS_R = P + 2 * P
GROUPS = UNITS_R // GROUP


GATHERED_FIRST = 38


class TableRows:

    def __init__(self, nc, ctx, dram):
        self.nc, self.dram = nc, dram
        self.idx = ctx.enter_context(nc.sbuf_tensor("r_idx", [P, UNITS_R], I32))
        self.cur = [ctx.enter_context(nc.sbuf_tensor(f"r_cur{i}", [P, GROUP], I32)) for i in range(2)]
        self.buf = [ctx.enter_context(nc.sbuf_tensor(f"r_buf{i}", [P, GROUP, D], F32)) for i in range(2)]
        self.s_idx = ctx.enter_context(nc.semaphore("r_idx_loaded"))
        self.s_cur = [ctx.enter_context(nc.semaphore(f"r_cur_ready{i}")) for i in range(2)]
        self.s_got = [ctx.enter_context(nc.semaphore(f"r_got{i}")) for i in range(2)]
        self.s_sent = [ctx.enter_context(nc.semaphore(f"r_sent{i}")) for i in range(2)]

    def start(self, pool):
        pool.dma_start(self.idx[:], self.dram["hopsT"]).then_inc(self.s_idx, 16)
        pool.wait_ge(self.s_idx, 16)

    def group(self, pool, g, i, first=False):
        turn = g // 2
        if not first:
            pool.wait_ge(self.s_sent[i], turn * 16)
        pool.tensor_copy(self.cur[i][:], self.idx[:, bass.ds(g * GROUP, GROUP)]).then_inc(self.s_cur[i], 1)
        pool.wait_ge(self.s_cur[i], turn + 1)
        pool.nop(nofuse=True)
        for j in range(GROUP):
            pool.indirect_dma_start(
                out=self.buf[i][:, j, :], out_offset=None, in_=self.dram["rpe"],
                in_offset=bass.IndirectOffsetOnAxis(ap=self.cur[i][:, j:j + 1], axis=0))\
                .then_inc(self.s_got[i], 16)

    def send(self, pool, g, i):
        pool.wait_ge(self.s_got[i], (g // 2 + 1) * 16 * GROUP)
        pool.dma_start(self.dram["pos_rows"][bass.ds(g, 1)].rearrange("g p n -> p (g n)"),
                       self.buf[i][:].rearrange("p j d -> p (j d)")).then_inc(self.s_sent[i], 16)

    def share(self, first, last):
        def run(pool):
            lo = first
            if first == 0:
                self.start(pool)
                self.group(pool, 0, 0, True)
                self.group(pool, 1, 1, True)
                self.send(pool, 0, 0)
                self.send(pool, 1, 1)
                lo = 1
            with pool.Fori(lo, last) as t:
                self.group(pool, 2 * t, 0)
                self.group(pool, 2 * t + 1, 1)
                self.send(pool, 2 * t, 0)
                self.send(pool, 2 * t + 1, 1)
        return run


NE = 8
HID = 1024
HT = HID // P
TT = B * QT
TILES = TT + NE - 1
NEG_BIG = 1.0e30


def first_max_onehot(dve, link, lg, mx, t8, low, onehot, iota8m):
    shape = [P, TT, NE]
    link(dve.tensor_reduce(mx, lg, AX.X, ALU.max))
    link(dve.tensor_tensor(t8, lg, mx.unsqueeze(2).broadcast_to(shape), ALU.is_equal))
    link(dve.tensor_tensor(t8, t8, iota8m, ALU.mult))
    link(dve.tensor_reduce(low, t8, AX.X, ALU.min))
    link(dve.tensor_tensor(onehot, iota8m, low.unsqueeze(2).broadcast_to(shape), ALU.is_equal))


def moe_route(nc, dram, x2, pos, te, wtop, pool_share):
    with ExitStack() as ctx:
        def sb(name, shape, dt=F32):
            return ctx.enter_context(nc.sbuf_tensor("b_" + name, shape, dt))

        sem = phase_semaphores(nc, ctx, "b_")

        ident = sb("ident", [P, P])
        before = sb("before", [P, P])
        ones = sb("ones", [P, P])
        wg = sb("wg", [P, KT, NE])
        consts = sb("consts", [P, 3 * TT * NE + NE * TILES])
        iota8m = consts[:, 0:TT * NE].rearrange("p (t e) -> p t e", e=NE)
        bg = consts[:, TT * NE:2 * TT * NE].rearrange("p (t e) -> p t e", e=NE)
        steps = consts[:, 2 * TT * NE:3 * TT * NE].rearrange("p (e j) -> p e j", e=NE)
        tile_no = consts[:, 3 * TT * NE:].rearrange("p (i e) -> p i e", e=NE)
        xT = [sb(f"xT{i}", [P, KT, 4, P]) for i in range(2)]
        lg = sb("lg", [P, TT, NE])
        mx = sb("mx", [P, TT])
        t8 = sb("t8", [P, TT, NE])
        low = sb("low", [P, TT])
        onehot = sb("onehot", [P, TT, NE])
        ex = sb("ex", [P, TT, NE])
        z = sb("z", [P, TT])
        run = [sb(f"run{i}", [P, TT, NE]) for i in range(2)]
        tot = sb("tot", [P, TT, NE])
        need = sb("need", [P, NE])
        cum = [sb(f"cum{i}", [P, NE]) for i in range(2)]
        base = sb("base", [P, NE])
        posf = sb("posf", [P, TT])
        tmpi = sb("tmpi", [P, TILES, NE])
        tef = sb("tef", [P, TILES])
        pt = [ctx.enter_context(nc.psum_tensor(f"b_pt{i}", [P, 4, P], F32)) for i in range(4)]
        pl = ctx.enter_context(nc.psum_tensor("b_pl", [P, TT, NE], F32))
        pr = ctx.enter_context(nc.psum_tensor("b_pr", [P, TT, NE], F32))
        pc = ctx.enter_context(nc.psum_tensor("b_pc", [P, TT, NE], F32))

        s_in = sem("in")
        s_x = sem("x")
        s_turned = sem("turned")
        s_xT = [sem("xT_act"), sem("xT_dve")]
        s_logits = sem("logits")
        s_cent = sem("centred")
        s_ex = sem("ex")
        s_onehot = sem("onehot")
        s_ranks = sem("ranks")
        s_pos = sem("pos")
        s_te = sem("te")
        s_rows = sem("rows")
        s_dve = sem("dve")
        block = ctx.enter_context(nc.Block())

        @block.sync
        def _(sp):
            sp.dma_start(x2[:], dram["x2"].rearrange("b (t p) d -> p (b t) d", p=P)).then_inc(s_x, 16)
            sp.dma_start(ident[:], dram["ident"]).then_inc(s_in, 16)
            sp.dma_start(wg[:], dram["wg"]).then_inc(s_in, 16)
            sp.dma_start(before[:], dram["before"]).then_inc(s_in, 16)
            sp.dma_start(consts[:], dram["route"]).then_inc(s_in, 16)

        @block.tensor
        def _(pe):
            pe.wait_ge(s_in, 64)
            pe.wait_ge(s_x, 16)
            def turn(q):
                for k in range(KT):
                    for j in range(4):
                        ins = pe.transpose(pt[2 * (q % 2) + k][:, j], x2[:, 4 * q + j, k * P:(k + 1) * P], ident[:])
                ins.then_inc(s_turned, 1)

            turn(0)
            for q in range(4):
                if q + 1 < 4:
                    turn(q + 1)
                pe.wait_ge(s_xT[0], q + 1)
                pe.wait_ge(s_xT[1], q + 1)
                for j in range(4):
                    for k in range(KT):
                        ins = pe.matmul(pl[:, 4 * q + j], xT[q % 2][:, k, j], wg[:, k], start=(k == 0),
                                        stop=(k == KT - 1), skip_group_check=True)
            ins.then_inc(s_logits, 1)
            pe.wait_ge(s_onehot, 1)
            pe.matmul(pr[:], before[:], onehot[:], start=True, stop=True)
            pe.matmul(pc[:], ones[:], onehot[:], start=True, stop=True).then_inc(s_ranks, 1)

        @block.scalar
        def _(act):
            for q in range(4):
                act.wait_ge(s_turned, q + 1)
                if q >= 2:
                    act.wait_ge(s_turned, q + 1)
                act.copy(xT[q % 2][:, 0], pt[2 * (q % 2)][:]).then_inc(s_xT[0], 1)
            act.wait_ge(s_cent, 1)
            act.activation(ex[:], ex[:], ACT.Exp).then_inc(s_ex, 1)

        @block.vector
        def _(dve):
            n = [0]

            def link(ins):
                ins.then_inc(s_dve, 1)
                n[0] += 1
                dve.wait_ge(s_dve, n[0])

            dve.memset(ones[:], 1.0)
            for q in range(4):
                dve.wait_ge(s_turned, q + 1)
                dve.tensor_copy(xT[q % 2][:, 1], pt[2 * (q % 2) + 1][:]).then_inc(s_xT[1], 1)
            dve.wait_ge(s_in, 64)
            dve.wait_ge(s_logits, 1)
            link(dve.tensor_tensor(lg[:], pl[:], bg, ALU.add))
            first_max_onehot(dve, link, lg[:], mx[:], t8[:], low[:], onehot[:], iota8m)
            dve.tensor_tensor(ex[:], lg[:], mx[:].unsqueeze(2).broadcast_to([P, TT, NE]), ALU.subtract)\
                .then_inc(s_cent, 1)
            dve.sem_inc(s_onehot, 1)
            dve.wait_ge(s_ex, 1)
            link(dve.tensor_reduce(z[:], ex[:], AX.X, ALU.add))
            dve.reciprocal(wtop, z[:])
            dve.wait_ge(s_ranks, 1)
            link(dve.tensor_copy(tot[:], pc[:]))
            src = tot
            for i, d in enumerate((1, 2, 4, 8)):
                dst = run[i % 2]
                dve.tensor_copy(dst[:, 0:d], src[:, 0:d])
                link(dve.tensor_tensor(dst[:, d:TT], src[:, d:TT], src[:, 0:TT - d], ALU.add))
                src = dst
            link(dve.tensor_tensor(t8[:].rearrange("p t e -> p (t e)").rearrange("p (e j) -> p e j", e=NE),
                                   src[:, TT - 1].unsqueeze(2).broadcast_to([P, NE, TT]), steps, ALU.is_gt))
            link(dve.tensor_reduce(need[:], t8[:].rearrange("p t e -> p (t e)").rearrange("p (e j) -> p e j", e=NE),
                                   AX.X, ALU.add))
            c = need
            for i, d in enumerate((1, 2, 4)):
                dst = cum[i % 2]
                dve.tensor_copy(dst[:, 0:d], c[:, 0:d])
                link(dve.tensor_tensor(dst[:, d:NE], c[:, d:NE], c[:, 0:NE - d], ALU.add))
                c = dst
            link(dve.tensor_tensor(tmpi[:], c[:].unsqueeze(1).broadcast_to([P, TILES, NE]), tile_no, ALU.is_le))
            link(dve.tensor_reduce(tef[:], tmpi[:], AX.X, ALU.add))
            link(dve.tensor_scalar(te, tef[:], float(NE - 1), None, ALU.min))
            link(dve.tensor_tensor(base[:], c[:], need[:], ALU.subtract))
            link(dve.tensor_scalar(base[:], base[:], float(P), None, ALU.mult))
            link(dve.tensor_tensor(t8[:], src[:], tot[:], ALU.subtract))
            link(dve.tensor_tensor(t8[:], t8[:], pr[:], ALU.add))
            link(dve.tensor_tensor(t8[:], t8[:], base[:].unsqueeze(1).broadcast_to([P, TT, NE]), ALU.add))
            link(dve.tensor_tensor(t8[:], t8[:], onehot[:], ALU.mult))
            link(dve.tensor_reduce(posf[:], t8[:], AX.X, ALU.add))
            dve.tensor_copy(pos, posf[:]).then_inc(s_pos, 1)

        @block.gpsimd
        def _(pool):
            pool.wait_ge(s_pos, 1)
            pool.wait_ge(s_x, 16)
            for t in range(TT):
                pool.indirect_dma_start(
                    out=dram["xs"], out_offset=bass.IndirectOffsetOnAxis(ap=pos[:, t:t + 1], axis=0),
                    in_=x2[:, t, :], in_offset=None).then_inc(s_rows, 16)
            pool.wait_ge(s_rows, 16 * TT)
            pool_share(pool)


def moe_experts(nc, dram, te, pool_share):
    with ExitStack() as ctx:
        def sb(name, shape, dt=F32):
            return ctx.enter_context(nc.sbuf_tensor("e_" + name, shape, dt))

        sem = phase_semaphores(nc, ctx, "e_")
        RING = 3

        ident = sb("ident", [P, P])
        w1 = [sb(f"w1{i}", [P, KT, HID]) for i in range(RING)]
        w2 = [sb(f"w2{i}", [P, HT, D]) for i in range(RING)]
        b1 = [sb(f"b1{i}", [P, HT]) for i in range(RING)]
        b2 = [sb(f"b2{i}", [P, D]) for i in range(RING)]
        xs = [sb(f"xs{i}", [P, D]) for i in range(RING)]
        xsT = [sb(f"xsT{i}", [P, KT, P]) for i in range(2)]
        h = [sb(f"h{i}", [P, HT, P]) for i in range(2)]
        ys = [sb(f"ys{i}", [P, D]) for i in range(2)]
        pt = ctx.enter_context(nc.psum_tensor("e_pt", [P, KT, P], F32))
        ph = [ctx.enter_context(nc.psum_tensor(f"e_ph{i}", [P, HT, P], F32)) for i in range(2)]
        po = [ctx.enter_context(nc.psum_tensor(f"e_po{i}", [P, D], F32)) for i in range(2)]

        s_in = sem("in")
        s_w1 = [sem(f"w1_{i}") for i in range(RING)]
        s_b1 = [sem(f"b1_{i}") for i in range(RING)]
        s_w2 = [sem(f"w2_{i}") for i in range(RING)]
        s_turned = sem("turned")
        s_xsT = sem("xsT")
        s_half = sem("half")
        s_hid = sem("hid")
        s_silu = sem("silu")
        s_out = sem("out")
        s_ys = sem("ys")
        s_sent = [sem(f"sent{i}") for i in range(2)]
        block = ctx.enter_context(nc.Block())

        @block.sync
        def _(sp):
            sp.dma_start(ident[:], dram["ident"]).then_inc(s_in, 16)

            def load(i, r, first):
                e = sp.value_load(te[0:1, bass.ds(i, 1)], min_val=0, max_val=NE - 1)
                if not first:
                    sp.wait_ge(s_hid, i - 2)
                    sp.wait_ge(s_turned, i - 2)
                sp.dma_start(w1[r][:], dram["w1"][bass.ds(e, 1)].rearrange("e p k h -> p (e k) h")).then_inc(s_w1[r], 16)
                sp.dma_start(xs[r][:], dram["xs"][bass.ds(i * P, P), :]).then_inc(s_w1[r], 16)
                if not first:
                    sp.wait_ge(s_silu, i - 2)
                sp.dma_start(b1[r][:], dram["b1"][bass.ds(e, 1)].rearrange("e p h -> p (e h)")).then_inc(s_b1[r], 16)
                if not first:
                    sp.wait_ge(s_ys, i - 2)
                sp.dma_start(w2[r][:], dram["w2"][bass.ds(e, 1)].rearrange("e p k h -> p (e k) h")).then_inc(s_w2[r], 16)
                sp.dma_start(b2[r][:], dram["b2"][bass.ds(e, 1), :].broadcast_to([P, D])).then_inc(s_w2[r], 16)

            for i in range(RING):
                load(i, i, True)
            loads = TILES - RING
            with sp.Fori(0, loads // RING) as t:
                for r in range(RING):
                    load(RING * (t + 1) + r, r, False)
            for i in range(TILES - loads % RING, TILES):
                load(i, i % RING, False)

        @block.gpsimd
        def _(pool):
            pool_share(pool)

            def store(i, p):
                pool.wait_ge(s_ys, i + 1)
                pool.dma_start(dram["ys"][bass.ds(i * P, P), :], ys[p][:]).then_inc(s_sent[p], 16)

            with pool.Fori(0, TILES // 2) as t:
                store(2 * t, 0)
                store(2 * t + 1, 1)
            store(TILES - 1, 0)
            pool.wait_ge(s_sent[0], 16 * (TILES // 2 + 1))
            pool.wait_ge(s_sent[1], 16 * (TILES // 2))

        PASS = 2 * RING
        FULL = (TILES - 1) // PASS
        REST = range(FULL * PASS, TILES)

        @block.tensor
        def _(pe):
            pe.wait_ge(s_in, 16)

            def turn(t, n):
                t, n = (t, n) if n < PASS else (t + 1, n - PASS)
                r = n % RING
                pe.wait_ge(s_w1[r], (2 * t + n // RING) * 32 + 32)
                for k in range(KT):
                    ins = pe.transpose(pt[:, k], xs[r][:, k * P:(k + 1) * P], ident[:])
                ins.then_inc(s_turned, 1)

            def hidden(t, n):
                t, n = (t, n) if n < PASS else (t + 1, n - PASS)
                i, r, p = PASS * t + n, n % RING, n % 2
                pe.wait_ge(s_xsT, i + 1)
                for c in range(HT):
                    for k in range(KT):
                        ins = pe.matmul(ph[p][:, c], w1[r][:, k, c * P:(c + 1) * P], xsT[p][:, k],
                                        start=(k == 0), stop=(k == KT - 1), skip_group_check=True)
                    if c == HT // 2 - 1:
                        ins.then_inc(s_half, 1)
                ins.then_inc(s_hid, 1)

            def outer(t, n):
                i, r, p = PASS * t + n, n % RING, n % 2
                pe.wait_ge(s_silu, i + 1)
                pe.wait_ge(s_w2[r], (2 * t + n // RING) * 32 + 32)
                for c in range(HT):
                    ins = pe.matmul(po[p][:], h[p][:, c], w2[r][:, c], start=(c == 0), stop=(c == HT - 1))
                ins.then_inc(s_out, 1)

            turn(0, 0)
            hidden(0, 0)
            turn(0, 1)
            with pe.Fori(0, FULL) as t:
                for n in range(PASS):
                    hidden(t, n + 1)
                    turn(t, n + 2)
                    outer(t, n)
            for n in range(len(REST)):
                if n + 1 < len(REST):
                    hidden(FULL, n + 1)
                if n + 2 < len(REST):
                    turn(FULL, n + 2)
                pe.wait_ge(s_ys, PASS * FULL + n - 1)
                outer(FULL, n)

        @block.scalar
        def _(act):
            def silu(t, n):
                i, r, p = PASS * t + n, n % RING, n % 2
                act.wait_ge(s_b1[r], (2 * t + n // RING) * 16 + 16)
                for c in range(HT):
                    if c == 0:
                        act.wait_ge(s_half, i + 1)
                    if c == HT // 2:
                        act.wait_ge(s_hid, i + 1)
                    ins = act.activation(h[p][:, c], ph[p][:, c], ACT.Silu, bias=b1[r][:, c:c + 1])
                ins.then_inc(s_silu, 1)

            with act.Fori(0, FULL) as t:
                for n in range(PASS):
                    silu(t, n)
            for n in range(len(REST)):
                silu(FULL, n)

        @block.vector
        def _(dve):
            def turned(i, p):
                dve.wait_ge(s_turned, i + 1)
                dve.tensor_copy(xsT[p][:], pt[:]).then_inc(s_xsT, 1)

            def finish(t, n, first=False):
                i, r, p = PASS * t + n, n % RING, n % 2
                dve.wait_ge(s_out, i + 1)
                if not first:
                    dve.wait_ge(s_sent[p], (RING * t + n // 2) * 16)
                dve.tensor_tensor(ys[p][:], po[p][:], b2[r][:], ALU.add).then_inc(s_ys, 1)

            turned(0, 0)
            turned(1, 1)
            for n in range(PASS):
                turned(n + 2, n % 2)
                finish(0, n, first=n < 2)
            with dve.Fori(1, FULL) as t:
                for n in range(PASS):
                    turned(PASS * t + n + 2, n % 2)
                    finish(t, n)
            for i in REST:
                if i + 2 < TILES:
                    turned(i + 2, i % 2)
                finish(FULL, i - REST[0])


def moe_combine(nc, dram, x2, pos, wtop, pool_share):
    with ExitStack() as ctx:
        def sb(name, shape, dt=F32):
            return ctx.enter_context(nc.sbuf_tensor("m_" + name, shape, dt))

        sem = phase_semaphores(nc, ctx, "m_")

        y = sb("y", [P, TT, D])
        st = sb("st", [P, TT, 6])
        mv = sb("mv", [P, TT, 2])
        lnv = sb("lnv", [P, TT])
        rstd = sb("rstd", [P, TT])
        eps = sb("eps", [P, 1])
        s_y = [sem(f"y{t}") for t in range(TT)]
        s_eps = sem("eps")
        s_dve = sem("dve")
        s_mv = sem("mv")
        s_lnv = sem("lnv")
        s_rstd = sem("rstd")
        s_x3 = sem("x3")
        s_sent = sem("sent")
        block = ctx.enter_context(nc.Block())

        @block.gpsimd
        def _(pool):
            for t in range(TT):
                pool.indirect_dma_start(
                    out=y[:, t, :], out_offset=None, in_=dram["ys"],
                    in_offset=bass.IndirectOffsetOnAxis(ap=pos[:, t:t + 1], axis=0)).then_inc(s_y[t], 16)
            pool_share(pool)

        @block.vector
        def _(dve):
            dve.memset(eps[:], LN_EPS).then_inc(s_eps, 1)
            for t in range(TT):
                dve.wait_ge(s_y[t], 16)
                dve.scalar_tensor_tensor(y[:, t], y[:, t], wtop[:, t:t + 1], x2[:, t], ALU.mult, ALU.add)\
                    .then_inc(s_dve, 1)
                dve.wait_ge(s_dve, 2 * t + 1)
                dve.bn_stats(st[:, t], y[:, t]).then_inc(s_dve, 1)
                dve.wait_ge(s_dve, 2 * t + 2)
                dve.bn_aggr(mv[:, t], st[:, t]).then_inc(s_mv, 1)
            dve.wait_ge(s_mv, TT)
            dve.wait_ge(s_rstd, 1)
            for t in range(TT):
                dve.tensor_scalar(y[:, t], y[:, t], mv[:, t, 0:1], rstd[:, t:t + 1],
                                  ALU.subtract, ALU.mult).then_inc(s_x3, 1)

        @block.scalar
        def _(act):
            act.wait_ge(s_eps, 1)
            act.wait_ge(s_mv, TT)
            act.activation(lnv[:], mv[:, :, 1], ACT.Ln, bias=eps[:]).then_inc(s_lnv, 1)
            act.wait_ge(s_lnv, 1)
            act.activation(rstd[:], lnv[:], ACT.Exp, scale=-0.5).then_inc(s_rstd, 1)

        @block.sync
        def _(sp):
            for q in range(4):
                sp.wait_ge(s_x3, 4 * q + 4)
                sp.dma_start(dram["x3"][2 * q:2 * q + 2].rearrange("b (t p) d -> p (b t) d", p=P),
                             y[:, 4 * q:4 * q + 4]).then_inc(s_sent, 16)
            sp.wait_ge(s_sent, 64)


def layer1_attention(nc, dram, pool_share):
    with ExitStack() as ctx:
        def sb(name, shape, dt=F32):
            return ctx.enter_context(nc.sbuf_tensor("c_" + name, shape, dt))

        def two(name, shape, dt=F32):
            return [sb(f"{name}{i}", shape, dt) for i in range(2)]

        sem = phase_semaphores(nc, ctx, "c_")

        def sems(name):
            return [sem(f"{name}{i}") for i in range(2)]

        ident = sb("ident", [P, P])
        w = sb("w", [P, 3, KT, D])
        wr = sb("wr", [P, 2, KT, D])
        cols = sb("cols", [P, 5, 2])
        br = sb("br", [P, 2, 2])
        bv = sb("bv", [P, D])
        rope = sb("rope", [P, KT, S])
        ropeq = sb("ropeq", [P, KT, S])
        gw = sb("gw", [P, 6, 16])
        gwc = sb("gwc", [P, KT, 16])
        gb = sb("gb", [16, 1])
        eps = sb("eps", [P, 1])
        x = two("x", [P, QT, D])
        xT = two("xT", [P, KT, S])
        cT = two("cT", [P, KT, S])
        qT = two("qT", [P, KT, S])
        kT = two("kT", [P, KT, S])
        v = two("v", [P, QT, D])
        negmax = two("negmax", [P, QT])
        rsum = two("rsum", [P, QT])
        rinv = two("rinv", [P, QT])
        probs = two("probs", [P, QT, S])
        probsT = two("probsT", [P, 4, P])
        y = two("y", [P, QT, D])
        st = two("st", [P, QT, 6])
        mv = two("mv", [P, QT, 2])
        lnv = two("lnv", [P, QT])
        rstd = two("rstd", [P, QT])
        x4 = two("x4", [P, QT, D])
        x4T = two("x4T", [P, KT, S])
        gates = two("gates", [16, S])
        pm = [ctx.enter_context(nc.psum_tensor(f"c_pm{i}", [P, 2, 256], F32)) for i in range(2)]
        ps = [ctx.enter_context(nc.psum_tensor(f"c_ps{i}", [P, 2, 256], F32)) for i in range(2)]
        pt = [ctx.enter_context(nc.psum_tensor(f"c_pt{i}", [P, 4, P], F32)) for i in range(2)]
        po = [ctx.enter_context(nc.psum_tensor(f"c_po{i}", [P, 2, 256], F32)) for i in range(2)]

        s_in = sem("in")
        s_w = sem("w")
        s_x = sems("x")
        s_cT = sems("cT")
        s_step = sems("step")
        s_copied = sems("copied")
        s_scores = sems("scores")
        s_max = sems("max")
        s_exp = sems("exp")
        s_turned = sems("turned")
        s_evac = sems("evac")
        s_pv = sems("pv")
        s_stats = sems("stats")
        s_lnv = sems("lnv")
        s_rstd = sems("rstd")
        s_x4 = sems("x4")
        s_free = sems("free")
        s_sent = sems("sent")
        s_sent_g = sems("sent_g")
        s_dve = sem("dve")
        block = ctx.enter_context(nc.Block())
        STEPS1 = 6
        PASSES = B // 2

        @block.sync
        def _(sp):
            sp.dma_start(ident[:], dram["ident"]).then_inc(s_in, 16)
            sp.dma_start(w[:], dram["w"][:, WQ1:WQ1 + 3]).then_inc(s_in, 16)
            sp.dma_start(cols[:], dram["cols1"]).then_inc(s_in, 16)
            sp.dma_start(bv[:], dram["rows"][:, R_B1V]).then_inc(s_in, 16)
            sp.dma_start(rope[:], dram["rope"][:, 0]).then_inc(s_in, 16)
            sp.dma_start(ropeq[:], dram["rope"][:, 1]).then_inc(s_in, 16)
            sp.dma_start(gw[:], dram["gw"]).then_inc(s_in, 16)
            sp.dma_start(gb[:], dram["gb"]).then_inc(s_in, 16)

            def load_x(b, p):
                sp.dma_start(x[p][:], dram["x3"][bass.ds(b, 1)].rearrange("b (t p) d -> p (b t) d", p=P))\
                    .then_inc(s_x[p], 16)

            def load_c(b, p):
                sp.dma_start(cT[p][:], dram["cT"][bass.ds(b, 1)].rearrange("b p k s -> p (b k) s"))\
                    .then_inc(s_cT[p], 16)

            def store(t, p):
                b = 2 * t + p
                sp.wait_ge(s_x4[p], t + 1)
                sp.dma_start(dram["x4"][bass.ds(b, 1)].rearrange("b (t p) d -> p (b t) d", p=P), x4[p][:])\
                    .then_inc(s_sent[p], 16)
                sp.wait_ge(s_copied[p], t * STEPS1 + 6)
                sp.dma_start(dram["x4T"][bass.ds(b, 1)].rearrange("b p k s -> p (b k) s"), x4T[p][:])\
                    .then_inc(s_sent[p], 16)
                sp.wait_ge(s_copied[p], t * STEPS1 + 7)
                for g, name in enumerate(("gate_i", "gate_f")):
                    sp.dma_start(dram[name][bass.ds(b, 1)].rearrange("b h s -> (b h) s"),
                                 gates[p][8 * g:8 * g + 8, :]).then_inc(s_sent_g[p], 16)

            for p in range(2):
                load_x(p, p)
                load_c(p, p)
            with sp.Fori(0, PASSES - 1) as t:
                for p in range(2):
                    sp.wait_ge(s_stats[p], t + 1)
                    load_x(2 * t + 2 + p, p)
                for p in range(2):
                    store(t, p)
                    sp.wait_ge(s_step[p], t * STEPS1 + 6)
                    load_c(2 * t + 2 + p, p)
                for p in range(2):
                    sp.wait_ge(s_sent[p], 32 * t + 32)
                    sp.wait_ge(s_sent_g[p], 32 * t + 32)
                    sp.sem_inc(s_free[p], 1)
            for p in range(2):
                store(PASSES - 1, p)
            for p in range(2):
                sp.wait_ge(s_sent[p], 32 * PASSES)
                sp.wait_ge(s_sent_g[p], 32 * PASSES)

        @block.gpsimd
        def _(pool):
            pool_share(pool)

        @block.tensor
        def _(pe):
            pe.wait_ge(s_in, 16 * 8)
            pe.wait_ge(s_w, 6)

            def free(t, p, n):
                pe.wait_ge(s_copied[p], t * STEPS1 + n + 1)

            def turn(t, p, n, src):
                free(t, p, n)
                for k in range(KT):
                    for qt in range(QT):
                        ins = pe.transpose(pm[p][:, k, qt * P:(qt + 1) * P], src[p][:, qt, k * P:(k + 1) * P], ident[:])
                ins.then_inc(s_step[p], 1)

            def project_T(t, p, n, wi):
                free(t, p, n)
                for et in range(2):
                    for k in range(KT):
                        ins = pe.matmul(pm[p][:, et], wr[:, wi, k, et * P:(et + 1) * P], xT[p][:, k, :],
                                        start=(k == 0), stop=(k == KT - 1))
                ins.then_inc(s_step[p], 1)

            with pe.Fori(0, PASSES) as t:
                for p in range(2):
                    pe.wait_ge(s_x[p], 16 * t + 16)
                    turn(t, p, 0, x)
                for p in range(2):
                    project_T(t, p, 1, 1)
                for p in range(2):
                    project_T(t, p, 2, 0)
                for p in range(2):
                    free(t, p, 3)
                    for qt in range(QT):
                        for k in range(KT):
                            ins = pe.matmul(pm[p][:, qt], xT[p][:, k, qt * P:(qt + 1) * P], w[:, 2, k, :],
                                            start=(k == 0), stop=(k == KT - 1))
                    ins.then_inc(s_step[p], 1)
                for p in range(2):
                    for qt in range(QT):
                        for k in range(KT):
                            ins = pe.matmul(ps[p][:, qt], qT[p][:, k, qt * P:(qt + 1) * P], kT[p][:, k, :],
                                            start=(k == 0), stop=(k == KT - 1))
                    ins.then_inc(s_scores[p], 1)
                for p in range(2):
                    pe.wait_ge(s_exp[p], t + 1)
                    for qt in range(QT):
                        for c in range(2):
                            ins = pe.transpose(pt[p][:, 2 * qt + c], probs[p][:, qt, c * P:(c + 1) * P], ident[:])
                    ins.then_inc(s_turned[p], 1)
                for p in range(2):
                    free(t, p, 4)
                    pe.wait_ge(s_evac[p], t + 1)
                    for qt in range(QT):
                        for c in range(2):
                            ins = pe.matmul(po[p][:, qt], probsT[p][:, 2 * qt + c], v[p][:, c, :],
                                            start=(c == 0), stop=(c == 1))
                    ins.then_inc(s_pv[p], 1)
                for p in range(2):
                    pe.wait_ge(s_x4[p], t + 1)
                    turn(t, p, 4, x4)
                for p in range(2):
                    free(t, p, 5)
                    pe.wait_ge(s_cT[p], 16 * t + 16)
                    for k in range(KT):
                        pe.matmul(pm[p][0:16, 0], gw[:, k, :], x4T[p][:, k, :], start=(k == 0), stop=False)
                    for k in range(KT):
                        ins = pe.matmul(pm[p][0:16, 0], gwc[:, k, :], cT[p][:, k, :], start=False, stop=(k == KT - 1))
                    ins.then_inc(s_step[p], 1)

        @block.scalar
        def _(act):
            act.wait_ge(s_in, 16 * 8)
            with act.Fori(0, PASSES) as t:
                for p in range(2):
                    act.wait_ge(s_step[p], t * STEPS1 + 1)
                    act.copy(xT[p][:], pm[p][:]).then_inc(s_copied[p], 1)
                for p in range(2):
                    act.wait_ge(s_step[p], t * STEPS1 + 4)
                    act.copy(v[p][:], pm[p][:]).then_inc(s_copied[p], 1)
                for p in range(2):
                    act.wait_ge(s_max[p], t + 1)
                    for qt in range(QT):
                        ins = act.activation(probs[p][:, qt], ps[p][:, qt], ACT.Exp, bias=negmax[p][:, qt:qt + 1],
                                             accum_out=rsum[p][:, qt:qt + 1])
                    ins.then_inc(s_exp[p], 1)
                for p in range(2):
                    act.wait_ge(s_turned[p], t + 1)
                    act.copy(probsT[p][:], pt[p][:]).then_inc(s_evac[p], 1)
                for p in range(2):
                    act.wait_ge(s_stats[p], t + 1)
                    act.activation(lnv[p][:], mv[p][:, :, 1], ACT.Ln, bias=eps[:]).then_inc(s_lnv[p], 1)
                    act.wait_ge(s_lnv[p], t + 1)
                    act.activation(rstd[p][:], lnv[p][:], ACT.Exp, scale=-0.5).then_inc(s_rstd[p], 1)
                for p in range(2):
                    act.wait_ge(s_free[p], t + 1)
                    act.wait_ge(s_step[p], t * STEPS1 + 5)
                    act.copy(x4T[p][:], pm[p][:]).then_inc(s_copied[p], 1)
                for p in range(2):
                    act.wait_ge(s_step[p], t * STEPS1 + 6)
                    act.activation(gates[p][:], pm[p][0:16, 0], ACT.Identity, bias=gb[:]).then_inc(s_copied[p], 1)

        @block.vector
        def _(dve):
            dve.memset(eps[:], LN_EPS).then_inc(s_w, 1)
            for p in range(2):
                dve.sem_inc(s_copied[p], 1)
                dve.sem_inc(s_free[p], 1)
            dve.wait_ge(s_in, 16 * 8)
            src = w[:, 0:2].rearrange("p w k (i two) -> p (w k i) two", two=2)
            dst = wr[:].rearrange("p w k (i two) -> p (w k i) two", two=2)
            dve.tensor_tensor(dst[:, :, 0], src[:, :, 0], src[:, :, 1], ALU.subtract).then_inc(s_w, 1)
            dve.tensor_tensor(dst[:, :, 1], src[:, :, 1], src[:, :, 0], ALU.add).then_inc(s_w, 1)
            for i in range(2):
                dve.scalar_tensor_tensor(br[:, i], cols[:, 2 + i], cols[:, 4, 0:1], cols[:, i], ALU.mult, ALU.add)\
                    .then_inc(s_w, 1)
            dve.tensor_tensor(gwc[:], gw[:, 2:4], gw[:, 4:6], ALU.add).then_inc(s_w, 1)
            dve.wait_ge(s_w, 6)
            with dve.Fori(0, PASSES) as t:
                chain = Count(dve, s_dve, 6, t * 6)
                for p in range(2):
                    dve.wait_ge(s_step[p], t * STEPS1 + 2)
                    for et in range(2):
                        ins = dve.scalar_tensor_tensor(kT[p][:, et], pm[p][:, et], br[:, 1, et:et + 1], rope[:, et],
                                                       ALU.add, ALU.mult)
                    ins.then_inc(s_copied[p], 1)
                for p in range(2):
                    dve.wait_ge(s_step[p], t * STEPS1 + 3)
                    for et in range(2):
                        ins = dve.scalar_tensor_tensor(qT[p][:, et], pm[p][:, et], br[:, 0, et:et + 1], ropeq[:, et],
                                                       ALU.add, ALU.mult)
                    ins.then_inc(s_copied[p], 1)
                for p in range(2):
                    dve.wait_ge(s_scores[p], t + 1)
                    dve.tensor_reduce(negmax[p][:], ps[p][:], AX.X, ALU.max, negate=True).then_inc(s_max[p], 1)
                for p in range(2):
                    dve.wait_ge(s_x[p], 16 * t + 16)
                    dve.tensor_tensor(y[p][:], x[p][:], bv[:].unsqueeze(1).broadcast_to([P, QT, D]), ALU.add)
                    dve.wait_ge(s_exp[p], t + 1)
                    chain.link(dve.reciprocal(rinv[p][:], rsum[p][:]))
                for p in range(2):
                    dve.wait_ge(s_pv[p], t + 1)
                    for qt in range(QT):
                        ins = dve.scalar_tensor_tensor(y[p][:, qt], po[p][:, qt], rinv[p][:, qt:qt + 1], y[p][:, qt],
                                                       ALU.mult, ALU.add)
                    chain.link(ins)
                    dve.bn_stats(st[p][:, 0], y[p][:, 0])
                    chain.link(dve.bn_stats(st[p][:, 1], y[p][:, 1]))
                    dve.nop(nofuse=True)
                    dve.bn_aggr(mv[p][:, 0], st[p][:, 0])
                    dve.bn_aggr(mv[p][:, 1], st[p][:, 1]).then_inc(s_stats[p], 1)
                for p in range(2):
                    dve.wait_ge(s_free[p], t + 1)
                    dve.wait_ge(s_rstd[p], t + 1)
                    dve.wait_ge(s_stats[p], t + 1)
                    for qt in range(QT):
                        ins = dve.tensor_scalar(x4[p][:, qt], y[p][:, qt], mv[p][:, qt, 0:1], rstd[p][:, qt:qt + 1],
                                                ALU.subtract, ALU.mult)
                    ins.then_inc(s_x4[p], 1)
                chain.end()


H1 = 8
HW = D // H1
BH = B * H1
SCALE1 = float(1.0 / np.sqrt(np.float32(HW)))


def mlstm_gates(nc, dram, aT, eT, pool_share):
    with ExitStack() as ctx:
        def sb(name, shape, dt=F32):
            return ctx.enter_context(nc.sbuf_tensor("g_" + name, shape, dt))

        sem = phase_semaphores(nc, ctx, "g_")

        ident = sb("ident", [P, P])
        gi = sb("gi", [BH, S])
        gf = sb("gf", [BH, S])
        ab = sb("ab", [BH, S])
        ex = sb("ex", [BH, S])
        l1 = sb("l1", [BH, S])
        ls = sb("ls", [BH, S])
        ones = sb("ones", [BH, S])
        one = sb("one", [BH, 1])
        cs = sb("cs", [BH, S])
        a = sb("a", [BH, S])
        m = sb("m", [BH, S])
        en = sb("en", [BH, S])
        pt = ctx.enter_context(nc.psum_tensor("g_pt", [P, 2, 2, BH], F32))
        s_in = sem("in")
        s_ones = sem("ones")
        s_abs = sem("abs")
        s_ex = sem("ex")
        s_l1 = sem("l1")
        s_a = sem("a")
        s_m = sem("m")
        s_mld = sem("mld")
        s_en = sem("en")
        s_turned = sem("turned")
        s_done = sem("done")
        s_sent = sem("sent")
        s_dve = sem("dve")
        block = ctx.enter_context(nc.Block())

        @block.sync
        def _(sp):
            sp.dma_start(gf[:], dram["gate_f"].rearrange("b h s -> (b h) s")).then_inc(s_in, 16)
            sp.dma_start(gi[:], dram["gate_i"].rearrange("b h s -> (b h) s")).then_inc(s_in, 16)
            sp.dma_start(ident[:], dram["ident"]).then_inc(s_in, 16)
            sp.wait_ge(s_m, 1)
            sp.dma_start(dram["runmax"], m[:]).then_inc(s_sent, 16)
            sp.wait_ge(s_sent, 16)

        @block.gpsimd
        def _(pool):
            pool_share(pool)

        @block.scalar
        def _(act):
            act.wait_ge(s_abs, 1)
            act.activation(ex[:], ab[:], ACT.Exp, scale=-1.0).then_inc(s_ex, 1)
            act.wait_ge(s_ex, 1)
            act.activation(l1[:], ex[:], ACT.Ln, bias=one[:]).then_inc(s_l1, 1)
            act.wait_ge(s_mld, 1)
            act.activation(en[:], ab[:], ACT.Exp, scale=-1.0).then_inc(s_en, 1)

        @block.vector
        def _(dve):
            n = [0]

            def link(ins):
                ins.then_inc(s_dve, 1)
                n[0] += 1
                dve.wait_ge(s_dve, n[0])

            dve.memset(ones[:], 1.0)
            link(dve.memset(one[:], 1.0))
            dve.wait_ge(s_in, 48)
            dve.scalar_tensor_tensor(ab[:], gf[:], -1.0, gf[:], ALU.mult, ALU.max).then_inc(s_abs, 1)
            link(dve.tensor_scalar(ls[:], gf[:], 0.0, None, ALU.min))
            dve.wait_ge(s_l1, 1)
            link(dve.tensor_tensor(ls[:], ls[:], l1[:], ALU.subtract))
            link(dve.tensor_tensor_scan(cs[:], ones[:], ls[:], 0.0, ALU.mult, ALU.add))
            dve.tensor_tensor(a[:], gi[:], cs[:], ALU.subtract).then_inc(s_a, 1)
            dve.wait_ge(s_a, 1)
            dve.tensor_tensor_scan(m[:], a[:], a[:], -3.0e38, ALU.max, ALU.max).then_inc(s_m, 1)
            dve.wait_ge(s_m, 1)
            dve.wait_ge(s_ex, 1)
            dve.tensor_tensor(ab[:], cs[:], m[:], ALU.add).then_inc(s_mld, 1)
            dve.wait_ge(s_turned, 1)
            dve.tensor_copy(aT[:], pt[:, 0])
            dve.tensor_copy(eT[:], pt[:, 1]).then_inc(s_done, 1)

        @block.tensor
        def _(pe):
            pe.wait_ge(s_in, 48)
            pe.wait_ge(s_a, 1)
            pe.wait_ge(s_en, 1)
            for i, src in enumerate((a, en)):
                for t in range(2):
                    ins = pe.transpose(pt[:, i, t], src[:, t * P:(t + 1) * P], ident[0:BH, 0:BH])
            ins.then_inc(s_turned, 1)


def query_blocks(nc, dram, vt, qblk, pool_share):
    with ExitStack() as ctx:
        xq = ctx.enter_context(nc.sbuf_tensor(f"q{vt}_xq", [P, B, KT, P], F32))
        sem = phase_semaphores(nc, ctx, f"q{vt}_")
        s_xq = sem("xq_in")
        s_zero = sem("zero")
        block = ctx.enter_context(nc.Block())

        @block.sync
        def _(sp):
            for b in range(B):
                sp.dma_start(xq[:, b], dram["x4T"][b, :, :, vt * P:(vt + 1) * P]).then_inc(s_xq, 16)

        def fill(eng, copy, hp):
            src = xq[32 * hp:32 * hp + 32].rearrange("p b k v -> p (k v) b")
            dst = qblk[32 * hp:32 * hp + 32].rearrange("p k v n -> p (k v) n")[:, :, 8 * hp:8 * hp + 8]
            copy(dst, src)

        @block.gpsimd
        def _(pool):
            if vt == 0:
                pool.memset(qblk[:, 1], 0.0).then_inc(s_zero, 1)
            pool_share(pool)

        @block.vector
        def _(dve):
            if vt == 0:
                dve.memset(qblk[:, 0], 0.0).then_inc(s_zero, 1)
                dve.wait_ge(s_zero, 2)
            dve.wait_ge(s_xq, 16 * B)
            for hp in range(2):
                fill(dve, dve.tensor_copy, hp)

        @block.scalar
        def _(act):
            if vt == 0:
                act.wait_ge(s_zero, 2)
            act.wait_ge(s_xq, 16 * B)
            for hp in range(2, 4):
                fill(act, act.copy, hp)


def hop_scores(nc, dram, vt, qblk, kh, pool_share):
    first = 0 if vt == 0 else P // GROUP
    groups = P * (vt + 1) // GROUP
    queries = GROUP // (vt + 1)
    ring = 4
    passes = groups // ring
    N = BH // KT
    with ExitStack() as ctx:
        sem = phase_semaphores(nc, ctx, f"h{vt}_")

        ident = ctx.enter_context(nc.sbuf_tensor(f"h{vt}_ident", [P, P], F32))
        rows = [ctx.enter_context(nc.sbuf_tensor(f"h{vt}_rows{i}", [P, GROUP, D], F32)) for i in range(ring)]
        rT = [ctx.enter_context(nc.sbuf_tensor(f"h{vt}_rT{i}", [P, KT, GROUP, P], F32)) for i in range(2)]
        qs = [ctx.enter_context(nc.sbuf_tensor(f"h{vt}_qs{i}", [P, KT, queries, N], F32)) for i in range(2)]
        sc = [ctx.enter_context(nc.sbuf_tensor(f"h{vt}_sc{i}", [P, KT, P], F32)) for i in range(2)]
        pt = [[ctx.enter_context(nc.psum_tensor(f"h{vt}_pt{i}{k}", [P, GROUP, P], F32)) for k in range(KT)]
              for i in range(2)]
        pc = [ctx.enter_context(nc.psum_tensor(f"h{vt}_pc{i}", [P, KT, P], F32)) for i in range(2)]
        po = [ctx.enter_context(nc.psum_tensor(f"h{vt}_po{i}", [P, KT, GROUP, N], F32)) for i in range(2)]
        s_in = sem("in")
        s_rows = [sem(f"rows{i}") for i in range(ring)]
        s_turned = sem("turned")
        s_rT = [sem("rT_act"), sem("rT_dve")]
        s_qs = sem("queries")
        s_prod = sem("prod")
        s_sc = [sem("sc_act"), sem("sc_dve")]
        s_back = sem("back")
        s_kh = [sem("kh_act"), sem("kh_dve")]
        block = ctx.enter_context(nc.Block())

        @block.sync
        def _(sp):
            sp.dma_start(ident[:], dram["ident"]).then_inc(s_in, 16)

            def load(n, i):
                sp.dma_start(rows[i][:].rearrange("p j d -> p (j d)"),
                             dram["pos_rows"][bass.ds(first + n, 1)].rearrange("g p n -> p (g n)"))\
                    .then_inc(s_rows[i], 16)

            for i in range(ring):
                load(i, i)
            with sp.Fori(0, passes - 1) as t:
                for i in range(ring):
                    sp.wait_ge(s_turned, 4 * t + i + 1)
                    load(4 * t + ring + i, i)

        @block.gpsimd
        def _(pool):
            pool.sem_inc(s_prod, 2)
            pool.sem_inc(s_back, 2)
            pool_share(pool)
            with pool.Fori(0, passes) as t:
                for i in range(ring):
                    n = 4 * t + i
                    pool.wait_ge(s_prod, n + 1)
                    pool.tensor_copy(qs[i % 2][:], qblk[:, :, bass.ds(n * queries, queries)]).then_inc(s_qs, 1)

        @block.tensor
        def _(pe):
            pe.wait_ge(s_in, 16)

            def turn(t, i):
                pe.wait_ge(s_rows[i], 16 * t + 16)
                for k in range(KT):
                    for j in range(GROUP):
                        ins = pe.transpose(pt[i % 2][k][:, j], rows[i][:, j, k * P:(k + 1) * P], ident[:])
                ins.then_inc(s_turned, 1)

            def product(t, i):
                n = 4 * t + i
                pe.wait_ge(s_qs, n + 1)
                pe.wait_ge(s_rT[0], n + 1)
                pe.wait_ge(s_rT[1], n + 1)
                for k in range(KT):
                    for j in range(GROUP):
                        ins = pe.matmul(pc[i % 2][N * j:N * j + N, k], qs[i % 2][:, k, j // (vt + 1)],
                                        rT[i % 2][:, k, j], start=True, stop=True, skip_group_check=True)
                ins.then_inc(s_prod, 1)

            def back(t, i):
                pe.wait_ge(s_sc[i % 2], 2 * t + i // 2 + 1)
                pe.wait_ge(s_kh[i % 2], 2 * t + i // 2 + 1)
                for k in range(KT):
                    ins = pe.transpose(po[i % 2][:, k].rearrange("p j n -> p (j n)"), sc[i % 2][:, k], ident[:])
                ins.then_inc(s_back, 1)

            def group(t, i, start=False, end=False):
                if i < ring - 1:
                    turn(t, i + 1)
                elif not end:
                    turn(t + 1, 0)
                product(t, i)
                if i > 0:
                    back(t, i - 1)
                elif not start:
                    back(t - 1, ring - 1)

            turn(0, 0)
            for i in range(ring):
                group(0, i, start=True)
            with pe.Fori(1, passes - 1) as t:
                for i in range(ring):
                    group(t, i)
            for i in range(ring):
                group(passes - 1, i, end=True)
            back(passes - 1, ring - 1)

        def evacuate(eng, copy, which):
            eng.sem_inc(s_kh[which], 1)

            def rows_of(t, i):
                n = 4 * t + i
                eng.wait_ge(s_prod, n + 1)
                eng.wait_ge(s_turned, n + 1)
                copy(rT[i % 2][:, which], pt[i % 2][which][:]).then_inc(s_rT[which], 1)

            def scores_of(t, i):
                n = 4 * t + i
                eng.wait_ge(s_prod, n + 3)
                eng.wait_ge(s_back, n + 1)
                copy(sc[i % 2][:], pc[i % 2][:]).then_inc(s_sc[which], 1)

            def keep(t, i):
                n = 4 * t + i
                eng.wait_ge(s_back, n + 3)
                if vt == 0:
                    dst = kh[:, bass.ds(n * GROUP, GROUP), 0].rearrange("p v (k n) -> p k v n", k=KT)
                else:
                    dst = kh[:, bass.ds(n * queries, queries)].rearrange("p v t (k n) -> p k (v t) n", k=KT)
                copy(dst, po[i % 2][:]).then_inc(s_kh[which], 1)

            def group(t, i, start=False, end=False):
                if i < ring - 1:
                    rows_of(t, i + 1)
                elif not end:
                    rows_of(t + 1, 0)
                if i % 2 == which:
                    scores_of(t, i)
                elif i > 0:
                    keep(t, i - 1)
                elif not start:
                    keep(t - 1, ring - 1)

            rows_of(0, 0)
            for i in range(ring):
                group(0, i, start=True)
            with eng.Fori(1, passes - 1) as t:
                for i in range(ring):
                    group(t, i)
            for i in range(ring):
                group(passes - 1, i, end=True)
            if which == 1:
                keep(passes - 1, ring - 1)

        @block.scalar
        def _(act):
            evacuate(act, act.copy, 0)

        @block.vector
        def _(dve):
            evacuate(dve, dve.tensor_copy, 1)


def mlstm_heads(nc, dram, vt, qblk, kh, aT, eT):
    mts = range(vt + 1)
    nm = len(mts)
    with ExitStack() as ctx:
        def sb(name, shape, dt=F32):
            return ctx.enter_context(nc.sbuf_tensor(f"l{vt}_" + name, shape, dt))

        def two(name, shape, dt=F32):
            return [sb(f"{name}{i}", shape, dt) for i in range(2)]

        sem = phase_semaphores(nc, ctx, f"l{vt}_")

        def sems(name):
            return [sem(f"{name}{i}") for i in range(2)]

        lnw = sb("lnw", [P, D])
        lnb = sb("lnb", [P, D])
        eps = sb("eps", [P, 1])
        cT = two("cT", [P, KT, S])
        va = two("va", [P, 2, H1 * (HW + 1)])
        x4 = two("x4", [P, D])
        mb = two("mb", [P, H1, P])
        dm = two("dm", [P, nm, H1, P])
        cm = two("cm", [P, nm, H1, P])
        den = sb("den", [P, H1])
        rn = sb("rn", [P, H1])
        hh = sb("hh", [P, H1, HW])
        sq = sb("sq", [P, H1, HW])
        mu = sb("mu", [P, H1])
        var = sb("var", [P, H1])
        lnv8 = sb("lnv8", [P, H1])
        r8 = sb("r8", [P, H1])
        y = two("y", [P, D])
        st = sb("st", [P, 6])
        mv = two("mv", [P, 2])
        lnv = sb("lnv", [P, 1])
        rstd = two("rstd", [P, 1])
        x5 = two("x5", [P, D])
        pq = [[ctx.enter_context(nc.psum_tensor(f"l{vt}_pq{m}{i}", [P, H1, P], F32)) for i in range(2 - m)]
              for m in mts]
        pv = [ctx.enter_context(nc.psum_tensor(f"l{vt}_pv{i}", [P, H1, HW + 1], F32)) for i in range(2)]

        s_in = sem("in")
        s_w = sem("w")
        s_q = sems("q")
        s_va = sems("va")
        s_x4 = sems("x4")
        s_mb = sems("mb")
        s_pool = sem("pool")
        s_arg = sem("arg")
        s_dm = sem("dm")
        s_dm_free = sem("dm_free")
        s_qk = [sem(f"qk{m}") for m in mts]
        s_qk_read = [sem(f"qk_read{m}") for m in mts]
        s_c = [sem(f"c{m}") for m in mts]
        s_pv = sem("pv")
        s_var = sem("var")
        s_ln8 = sem("ln8")
        s_r8 = sem("r8")
        s_xb = sem("xb")
        s_y = sem("y")
        s_mv = sem("mv")
        s_lnv = sem("lnv")
        s_rstd = sem("rstd")
        s_x5 = sem("x5")
        s_sent = sems("sent")
        s_dve = sem("dve")
        block = ctx.enter_context(nc.Block())
        PASSES = B // 2

        @block.sync
        def _(sp):
            sp.dma_start(lnw[:], dram["rows"][:, R_LNW]).then_inc(s_in, 16)
            sp.dma_start(lnb[:], dram["rows"][:, R_LNB]).then_inc(s_in, 16)

            def load(b, p, first):
                if not first:
                    sp.wait_ge(s_qk[-1], b - 1)
                one = bass.ds(b, 1)
                sp.dma_start(cT[p][:], dram["cT"][one].rearrange("b p k s -> p (b k) s")).then_inc(s_q[p], 16)
                if not first:
                    sp.wait_ge(s_arg, b - 1)
                sp.dma_start(mb[p][:], dram["runmax"].rearrange("(b h) s -> b h s", h=H1)[
                    one, :, vt * P:(vt + 1) * P].broadcast_to([P, H1, P])).then_inc(s_mb[p], 16)
                if not first:
                    sp.wait_ge(s_pv, b - 1)
                sp.dma_start(va[p][:], dram["ctx_ones"][one].rearrange("b p m n -> p (b m) n")).then_inc(s_va[p], 16)
                if not first:
                    sp.wait_ge(s_y, b - 1)
                sp.dma_start(x4[p][:], dram["x4"][one, vt * P:(vt + 1) * P].rearrange("b p d -> p (b d)"))\
                    .then_inc(s_x4[p], 16)

            load(0, 0, True)
            load(1, 1, True)
            with sp.Fori(0, PASSES - 1) as t:
                for p in range(2):
                    load(2 * t + 2 + p, p, False)
            for p in range(2):
                sp.wait_ge(s_sent[p], 16 * PASSES)

        @block.gpsimd
        def _(pool):
            pool.wait_ge(s_w, 2)

            def args(t, p):
                b = 2 * t + p
                pool.wait_ge(s_mb[p], 16 * t + 16)
                pool.wait_ge(s_dm_free, b + 1)
                pool.nop(nofuse=True)
                pool.nop(nofuse=True)
                for m in mts:
                    ins = pool.tensor_tensor(
                        dm[p][:, m], aT[:, m, bass.ds(H1 * b, H1)].unsqueeze(2).broadcast_to([P, H1, P]), mb[p][:],
                        ALU.subtract)
                ins.then_inc(s_pool, 1)
                pool.wait_ge(s_pool, b + 1)
                pool.nop(nofuse=True)
                pool.affine_select(out=dm[p][:, vt], in_=dm[p][:, vt], compare_op=ALU.is_ge, fill=NEG, base=0,
                                   pattern=[[0, H1], [1, P]], channel_multiplier=-1).then_inc(s_arg, 1)

            def bias(t, p):
                pool.wait_ge(s_x4[p], 16 * t + 16)
                pool.tensor_tensor(x4[p][:], x4[p][:], lnb[:], ALU.add).then_inc(s_xb, 1)

            def product(t, p):
                b = 2 * t + p
                pool.wait_ge(s_qk_read[0], b + 3)
                pool.wait_ge(s_dm, b + 1)
                pool.tensor_tensor(cm[p][:, 0], cm[p][:, 0], dm[p][:, 0], ALU.mult).then_inc(s_c[0], 1)
                pool.wait_ge(s_c[0], b + 1)

            args(0, 0)
            args(0, 1)
            with pool.Fori(0, PASSES - 1) as t:
                for p in range(2):
                    if nm == 2:
                        product(t, p)
                    args(t + 1, p)
                    bias(t, p)
            for p in range(2):
                if nm == 2:
                    product(PASSES - 1, p)
                bias(PASSES - 1, p)

        @block.tensor
        def _(pe):
            def qk(t, p):
                b = 2 * t + p
                pe.wait_ge(s_q[p], 16 * t + 16)
                for m in mts:
                    pe.wait_ge(s_qk_read[m], b + 1)
                    for k in range(KT):
                        q = qblk[:, k].rearrange("p v (h b) -> p h v b", b=B)[:, :, :, bass.ds(b, 1)]\
                            .rearrange("p h v b -> p h (v b)")
                        ins = pe.matmul(pq[m][p * (1 - m)][:, 4 * k:4 * k + 4], cT[p][:, k, m * P:(m + 1) * P], q,
                                        start=True, stop=True, skip_group_check=True)
                    ins.then_inc(s_qk[m], 1)

            def values(t, p):
                b = 2 * t + p
                pe.wait_ge(s_va[p], 16 * t + 16)
                for m in mts:
                    pe.wait_ge(s_c[m], b + 1)
                for h in range(H1):
                    for m in mts:
                        ins = pe.matmul(pv[p][:, h], cm[p][:, m, h], va[p][:, m, h * (HW + 1):(h + 1) * (HW + 1)],
                                        start=(m == 0), stop=(m == nm - 1), skip_group_check=True)
                ins.then_inc(s_pv, 1)

            qk(0, 0)
            with pe.Fori(0, PASSES - 1) as t:
                qk(t, 1)
                values(t, 0)
                qk(t + 1, 0)
                values(t, 1)
            qk(PASSES - 1, 1)
            values(PASSES - 1, 0)
            values(PASSES - 1, 1)

        @block.scalar
        def _(act):
            act.preload_act_table_set("natural_log_exp_and_others")
            act.wait_ge(s_w, 2)

            def decay(t, p):
                b = 2 * t + p
                act.wait_ge(s_arg, b + 1)
                act.activation(dm[p][:], dm[p][:], ACT.Exp).then_inc(s_dm, 1)

            def roots8(t, p):
                b = 2 * t + p
                act.wait_ge(s_var, b + 1)
                act.activation(lnv8[:], var[:], ACT.Ln, bias=eps[:], scale=1.0 / HW).then_inc(s_ln8, 1)
                act.wait_ge(s_ln8, b + 1)
                act.activation(r8[:], lnv8[:], ACT.Exp, scale=-0.5).then_inc(s_r8, 1)

            def roots(t, p):
                b = 2 * t + p
                act.wait_ge(s_mv, b + 1)
                act.activation(lnv[:], mv[p][:, 1:2], ACT.Ln, bias=eps[:]).then_inc(s_lnv, 1)
                act.wait_ge(s_lnv, b + 1)
                act.activation(rstd[p][:], lnv[:], ACT.Exp, scale=-0.5).then_inc(s_rstd, 1)

            def store(t, p):
                b = 2 * t + p
                act.wait_ge(s_x5, b + 1)
                act.dma_start(dram["x5"][bass.ds(b, 1), vt * P:(vt + 1) * P].rearrange("b p d -> p (b d)"), x5[p][:])\
                    .then_inc(s_sent[p], 16)

            def batch(t, p, first=False, last=False):
                if not last:
                    decay(t + p, 1 - p)
                roots8(t, p)
                if not first:
                    store(t + p - 1, 1 - p)
                roots(t, p)

            decay(0, 0)
            batch(0, 0, first=True)
            batch(0, 1)
            with act.Fori(1, PASSES - 1) as t:
                batch(t, 0)
                batch(t, 1)
            batch(PASSES - 1, 0)
            batch(PASSES - 1, 1, last=True)
            store(PASSES - 1, 1)

        @block.vector
        def _(dve):
            dve.memset(eps[:], LN_EPS).then_inc(s_w, 1)
            for m in mts:
                dve.sem_inc(s_qk_read[m], 2 - m)
            dve.sem_inc(s_dm_free, 2)
            dve.wait_ge(s_in, 32)
            dve.tensor_scalar(lnw[:], lnw[:], 1.0, None, ALU.add).then_inc(s_w, 1)
            dve.wait_ge(s_w, 2)
            wide = [P, H1, HW]

            def front(t, p):
                b = 2 * t + p
                for m in mts:
                    hop = kh[:, :, m, :].rearrange("p v (h b) -> p h v b", b=B)[:, :, :, bass.ds(b, 1)]\
                        .rearrange("p h v b -> p h (v b)")
                    dve.wait_ge(s_qk[m], b + 1)
                    dve.scalar_tensor_tensor(cm[p][:, m], pq[m][p * (1 - m)][:], SCALE1, hop, ALU.mult, ALU.add)\
                        .then_inc(s_qk_read[m], 1)
                m = mts[-1]
                dve.wait_ge(s_qk_read[m], b + 3 - m)
                dve.wait_ge(s_dm, b + 1)
                dve.tensor_tensor(cm[p][:, m], cm[p][:, m], dm[p][:, m], ALU.mult).then_inc(s_c[m], 1)
                dve.wait_ge(s_c[m], b + 1)
                dve.sem_inc(s_dm_free, 1)

            LINKS = 12

            def heads(t, p):
                b = 2 * t + p
                chain = Count(dve, s_dve, 9, LINKS * b)
                dve.wait_ge(s_pv, b + 1)
                chain.link(dve.scalar_tensor_tensor(den[:], pv[p][:, :, HW], -1.0, eT[:, vt, bass.ds(H1 * b, H1)],
                                                    ALU.mult, ALU.max))
                chain.link(dve.tensor_tensor(den[:], pv[p][:, :, HW], den[:], ALU.max))
                chain.link(dve.tensor_scalar(den[:], den[:], 1.0e-6, None, ALU.add))
                chain.link(dve.reciprocal(rn[:], den[:]))
                chain.link(dve.tensor_tensor(hh[:], pv[p][:, :, 0:HW], rn[:].unsqueeze(2).broadcast_to(wide), ALU.mult))
                chain.link(dve.tensor_reduce(mu[:], hh[:], AX.X, ALU.add))
                chain.link(dve.tensor_scalar(mu[:], mu[:], -1.0 / HW, None, ALU.mult))
                chain.link(dve.tensor_tensor(hh[:], hh[:], mu[:].unsqueeze(2).broadcast_to(wide), ALU.add))
                chain.link(dve.tensor_tensor(sq[:], hh[:], hh[:], ALU.mult))
                dve.tensor_reduce(var[:], sq[:], AX.X, ALU.add).then_inc(s_var, 1)
                chain.end()

            def residual(t, p, before):
                b = 2 * t + p
                chain = Count(dve, s_dve, 3, LINKS * b + 9)
                dve.wait_ge(s_r8, b + 1)
                chain.link(dve.tensor_tensor(hh[:], hh[:], r8[:].unsqueeze(2).broadcast_to(wide), ALU.mult))
                if before:
                    dve.wait_ge(s_x5, b - 1)
                chain.link(dve.tensor_tensor(y[p][:], hh[:].rearrange("p h c -> p (h c)"), lnw[:], ALU.mult))
                dve.wait_ge(s_xb, b + 1)
                dve.tensor_tensor(y[p][:], y[p][:], x4[p][:], ALU.add).then_inc(s_y, 1)
                dve.wait_ge(s_y, b + 1)
                chain.link(dve.bn_stats(st[:], y[p][:]))
                dve.nop(nofuse=True)
                dve.bn_aggr(mv[p][:], st[:]).then_inc(s_mv, 1)
                chain.end()

            def norm(t, p, before=True):
                b = 2 * t + p
                if before:
                    dve.wait_ge(s_sent[p], 16 * t)
                dve.wait_ge(s_mv, b + 1)
                dve.wait_ge(s_rstd, b + 1)
                dve.tensor_scalar(x5[p][:], y[p][:], mv[p][:, 0:1], rstd[p][:], ALU.subtract, ALU.mult)\
                    .then_inc(s_x5, 1)

            front(0, 0)
            front(0, 1)
            heads(0, 0)
            residual(0, 0, False)
            front(1, 0)
            heads(0, 1)
            norm(0, 0, False)
            residual(0, 1, False)
            front(1, 1)
            heads(1, 0)
            norm(0, 1, False)
            residual(1, 0, True)
            with dve.Fori(1, PASSES - 1) as t:
                front(t + 1, 0)
                heads(t, 1)
                norm(t, 0)
                residual(t, 1, True)
                front(t + 1, 1)
                heads(t + 1, 0)
                norm(t, 1)
                residual(t + 1, 0, True)
            heads(PASSES - 1, 1)
            norm(PASSES - 1, 0)
            residual(PASSES - 1, 1, True)
            norm(PASSES - 1, 1)


HID1 = P
SHARED = NE


class ExpertWeights:

    def __init__(self, nc, ctx, dram):
        self.dram = dram

        def sb(name, shape):
            return ctx.enter_context(nc.sbuf_tensor("fw_" + name, shape, F32))

        self.tiles = {
            "ident": sb("ident", [P, P]),
            "gate1": sb("gate1", [P, KT, P]),
            "rscale": sb("rscale", [P, 1]),
            "iota8m": sb("iota8m", [P, QT, NE]),
            "f_w1": sb("w1", [P, KT, NE + 1, HID1]),
            "f_b1": sb("b1", [P, NE + 1]),
            "f_w2": sb("w2", [P, NE + 1, D]),
            "f_b2": sb("b2", [P, D]),
            "bs2": sb("bs2", [P, D]),
        }
        self.s_loaded = ctx.enter_context(nc.semaphore("f_weights_loaded"))

    def load(self, pool):
        for name, tile in self.tiles.items():
            src = self.dram["rows"][:, R_BS2] if name == "bs2" else self.dram[name]
            pool.dma_start(tile[:], src).then_inc(self.s_loaded, 16)

    def wait(self, eng):
        eng.wait_ge(self.s_loaded, 16 * len(self.tiles))


def experts_top2(nc, dram, weights):
    with ExitStack() as ctx:
        def sb(name, shape, dt=F32):
            return ctx.enter_context(nc.sbuf_tensor("f_" + name, shape, dt))

        def ring(n, name, shape, dt=F32):
            return [sb(f"{name}{i}", shape, dt) for i in range(n)]

        sem = phase_semaphores(nc, ctx, "f_")

        def sems(name):
            return [sem(f"{name}{i}") for i in range(2)]

        ident, gw, rscale, iota8m, w1, b1, w2, b2, bs2 = (
            weights.tiles[n] for n in ("ident", "gate1", "rscale", "iota8m", "f_w1", "f_b1", "f_w2", "f_b2", "bs2"))
        x = ring(2, "x", [P, QT, D])
        xT = ring(2, "xT", [P, KT, S])
        e = sb("e", [P, QT, NE])
        s1 = sb("s1", [P, QT, NE])
        s2 = sb("s2", [P, QT, NE])
        t8 = sb("t8", [P, QT, NE])
        one1 = sb("one1", [P, QT, NE])
        one2 = sb("one2", [P, QT, NE])
        m1 = sb("m1", [P, QT])
        m2 = sb("m2", [P, QT])
        low = sb("low", [P, QT])
        gate = ring(2, "gate", [P, QT, P])
        gT = ring(2, "gT", [P, QT, P])
        h = ring(3, "h", [P, S])
        acc = ring(2, "acc", [P, QT, D])
        st = sb("st", [P, QT, 6])
        mv = sb("mv", [P, QT, 2])
        eps = sb("eps", [P, 1])
        lnv = sb("lnv", [P, QT])
        rstd = sb("rstd", [P, QT])
        y = ring(2, "y", [P, QT, D])
        pm = ctx.enter_context(nc.psum_tensor("f_pm", [P, KT, S], F32))
        pg = ctx.enter_context(nc.psum_tensor("f_pg", [P, QT, P], F32))
        pgT = ctx.enter_context(nc.psum_tensor("f_pgT", [P, QT, P], F32))
        ph = [ctx.enter_context(nc.psum_tensor(f"f_ph{i}", [P, S], F32)) for i in range(3)]
        po = [ctx.enter_context(nc.psum_tensor(f"f_po{i}", [P, QT, D], F32)) for i in range(2)]

        s_x = sems("x")
        s_turned = sem("turned")
        s_xT = sem("xT")
        s_xb = sem("xb")
        s_logits = sem("logits")
        s_e = sem("e")
        s_zero = sem("zero")
        s_gate = sem("gate")
        s_gT = sem("gT")
        s_gT_copied = sem("gT_copied")
        s_h = sem("h")
        s_gelu = sem("gelu")
        s_o = sem("o")
        s_acc = sem("acc")
        s_st = sem("st")
        s_mv = sem("mv")
        s_lnv = sem("lnv")
        s_rstd = sem("rstd")
        s_y = sem("y")
        s_free = sems("free")
        s_sent = sems("sent")
        s_dve = sem("dve")
        block = ctx.enter_context(nc.Block())
        PASSES = B // 2
        N = NE + 1
        ORDER = [SHARED] + list(range(NE))

        @block.sync
        def _(sp):
            def load(b, p):
                sp.dma_start(x[p][:], dram["x5"][bass.ds(b, 1)].rearrange("b (t p) d -> p (b t) d", p=P))\
                    .then_inc(s_x[p], 16)

            def store(b, p):
                sp.wait_ge(s_y, b + 1)
                sp.dma_start(dram["out"][bass.ds(b, 1)].rearrange("b (t p) d -> p (b t) d", p=P), y[p][:])\
                    .then_inc(s_sent[p], 16)

            load(0, 0)
            load(1, 1)
            def reload(b, p):
                sp.wait_ge(s_acc, (b - 2) * N + 1)
                load(b, p)

            def store_and_free(t, p):
                store(2 * t + p, p)
                sp.wait_ge(s_sent[p], 16 * t + 16)
                sp.sem_inc(s_free[p], 1)

            reload(2, 0)
            with sp.Fori(0, PASSES - 2) as t:
                reload(2 * t + 3, 1)
                store_and_free(t, 0)
                reload(2 * t + 4, 0)
                store_and_free(t, 1)
            reload(B - 1, 1)
            store_and_free(PASSES - 2, 0)
            store_and_free(PASSES - 2, 1)
            for p in range(2):
                store(B - 2 + p, p)
            for p in range(2):
                sp.wait_ge(s_sent[p], 16 * PASSES)

        @block.gpsimd
        def _(pool):
            for p in range(2):
                pool.memset(gate[p][:], 0.0).then_inc(s_zero, 1)
            weights.wait(pool)

            def bias(t, p):
                pool.wait_ge(s_x[p], 16 * t + 16)
                pool.wait_ge(s_turned, 2 * t + p + 1)
                pool.tensor_tensor(x[p][:], x[p][:], bs2[:].unsqueeze(1).broadcast_to([P, QT, D]), ALU.add)\
                    .then_inc(s_xb, 1)

            with pool.Fori(0, PASSES) as t:
                for p in range(2):
                    bias(t, p)

        @block.tensor
        def _(pe):
            weights.wait(pe)

            def turn(t, p):
                pe.wait_ge(s_x[p], 16 * t + 16)
                for k in range(KT):
                    for qt in range(QT):
                        ins = pe.transpose(pm[:, k, qt * P:(qt + 1) * P], x[p][:, qt, k * P:(k + 1) * P], ident[:])
                ins.then_inc(s_turned, 1)

            def logits(t, p):
                pe.wait_ge(s_xT, 2 * t + p + 1)
                for qt in range(QT):
                    for k in range(KT):
                        ins = pe.matmul(pg[:, qt], xT[p][:, k, qt * P:(qt + 1) * P], gw[:, k],
                                        start=(k == 0), stop=(k == KT - 1))
                ins.then_inc(s_logits, 1)

            def turn_gates(t, p):
                pe.wait_ge(s_gate, 2 * t + p + 1)
                for qt in range(QT):
                    ins = pe.transpose(pgT[:, qt], gate[p][:, qt], ident[:])
                ins.then_inc(s_gT, 1)

            def hidden(b, p, i, emptied=True):
                if emptied:
                    pe.wait_ge(s_gelu, b * N + i - 2)
                for k in range(KT):
                    ins = pe.matmul(ph[i % 3][:], w1[:, k, ORDER[i]], xT[p][:, k], start=(k == 0), stop=(k == KT - 1))
                ins.then_inc(s_h, 1)

            def outer(b, p, i, emptied):
                pe.wait_ge(s_gelu, b * N + i + 1)
                if emptied:
                    pe.wait_ge(s_acc, b * N + i - 1)
                for qt in range(QT):
                    if i == 0:
                        pe.matmul(po[p][:, qt], gT[p][:, qt], b2[:], start=True, stop=False)
                    ins = pe.matmul(po[(p + i) % 2][:, qt], h[i % 3][:, qt * P:(qt + 1) * P], w2[:, ORDER[i]],
                                    start=(i != 0), stop=True)
                ins.then_inc(s_o, 1)

            def batch(t, p, first, last):
                b = 2 * t + p
                for i in range(N):
                    if i + 2 < N:
                        hidden(b, p, i + 2, not (first and i == 0))
                    elif not last:
                        hidden(b + 1, 1 - p, i + 2 - N)
                    if i == 0:
                        pe.wait_ge(s_gT_copied, b + 1)
                    outer(b, p, i, not (first and i < 2))
                    if not last:
                        following = (t + p, 1 - p)
                        if i == 0:
                            turn(*following)
                        elif i == 2:
                            logits(*following)
                        elif i == 8:
                            turn_gates(*following)

            turn(0, 0)
            logits(0, 0)
            hidden(0, 0, 0, False)
            hidden(0, 0, 1, False)
            turn_gates(0, 0)
            batch(0, 0, True, False)
            batch(0, 1, False, False)
            with pe.Fori(1, PASSES - 1) as t:
                batch(t, 0, False, False)
                batch(t, 1, False, False)
            batch(PASSES - 1, 0, False, False)
            batch(PASSES - 1, 1, False, True)

        @block.scalar
        def _(act):
            weights.wait(act)
            act.wait_ge(s_zero, 3)

            def rows(b, p):
                act.wait_ge(s_turned, b + 1)
                act.copy(xT[p][:], pm[:]).then_inc(s_xT, 1)

            def exps(b):
                act.wait_ge(s_logits, b + 1)
                act.activation(e[:], pg[:, :, 0:NE], ACT.Exp, scale=-1.0).then_inc(s_e, 1)

            def root(b):
                act.wait_ge(s_mv, b + 1)
                act.activation(lnv[:], mv[:, :, 1], ACT.Ln, bias=eps[:]).then_inc(s_lnv, 1)
                act.wait_ge(s_lnv, b + 1)
                act.activation(rstd[:], lnv[:], ACT.Exp, scale=-0.5).then_inc(s_rstd, 1)

            def batch(t, p, first, last):
                b = 2 * t + p
                for i in range(N):
                    act.wait_ge(s_h, b * N + i + 1)
                    if not (first and i < 3):
                        act.wait_ge(s_o, b * N + i - 2)
                    act.activation(h[i % 3][:], ph[i % 3][:], ACT.Gelu, bias=b1[:, ORDER[i]:ORDER[i] + 1])\
                        .then_inc(s_gelu, 1)
                    if i == 0:
                        act.wait_ge(s_gT, b + 1)
                        act.copy(gT[p][:], pgT[:]).then_inc(s_gT_copied, 1)
                    if not last:
                        if i == 2:
                            rows(b + 1, 1 - p)
                        elif i == 4:
                            exps(b + 1)
                    if i == 7 and not first:
                        root(b - 1)

            rows(0, 0)
            exps(0)
            batch(0, 0, True, False)
            batch(0, 1, False, False)
            with act.Fori(1, PASSES - 1) as t:
                batch(t, 0, False, False)
                batch(t, 1, False, False)
            batch(PASSES - 1, 0, False, False)
            batch(PASSES - 1, 1, False, True)
            root(B - 1)

        @block.vector
        def _(dve):
            dve.memset(eps[:], LN_EPS).then_inc(s_zero, 1)
            for p in range(2):
                dve.sem_inc(s_free[p], 1)
            weights.wait(dve)
            dve.wait_ge(s_zero, 2)
            shape = [P, QT, NE]
            LINKS = 16

            def largest(chain, src, m, onehot):
                chain.link(dve.tensor_reduce(m[:], src[:], AX.X, ALU.max))
                chain.link(dve.tensor_tensor(t8[:], src[:], m[:].unsqueeze(2).broadcast_to(shape), ALU.is_equal))
                chain.link(dve.tensor_tensor(t8[:], t8[:], iota8m[:], ALU.mult))
                chain.link(dve.tensor_reduce(low[:], t8[:], AX.X, ALU.min))
                chain.link(dve.tensor_tensor(onehot[:], iota8m[:], low[:].unsqueeze(2).broadcast_to(shape),
                                             ALU.is_equal))

            def gating(t, p, chain, part):
                if part == 0:
                    dve.wait_ge(s_e, 2 * t + p + 1)
                    chain.link(dve.tensor_scalar(s1[:], e[:], 1.0, None, ALU.add))
                    chain.link(dve.reciprocal(s2[:], s1[:]))
                    chain.link(dve.tensor_scalar(s1[:], s2[:], rscale[:, 0:1], None, ALU.mult))
                elif part == 1:
                    largest(chain, s1, m1, one1)
                elif part == 2:
                    chain.link(dve.scalar_tensor_tensor(s2[:], one1[:], NEG, s1[:], ALU.mult, ALU.add))
                    largest(chain, s2, m2, one2)
                else:
                    dve.tensor_tensor(m1[:], m1[:], m2[:], ALU.add)
                    chain.link(dve.tensor_tensor(one1[:], one1[:], one2[:], ALU.add))
                    dve.reciprocal(m2[:], m1[:])
                    chain.link(dve.tensor_tensor(s1[:], s1[:], one1[:], ALU.mult))
                    dve.tensor_tensor(gate[p][:, :, 0:NE], s1[:], m2[:].unsqueeze(2).broadcast_to(shape), ALU.mult)\
                        .then_inc(s_gate, 1)

            def norm(t, p, part):
                b = 2 * t + p
                if part == 0:
                    dve.wait_ge(s_acc, b * N + N)
                    dve.bn_stats(st[:, 0], acc[p][:, 0])
                    dve.bn_stats(st[:, 1], acc[p][:, 1]).then_inc(s_st, 1)
                elif part == 1:
                    dve.wait_ge(s_st, b + 1)
                    dve.nop(nofuse=True)
                    dve.bn_aggr(mv[:, 0], st[:, 0])
                    dve.bn_aggr(mv[:, 1], st[:, 1]).then_inc(s_mv, 1)
                else:
                    dve.wait_ge(s_free[p], t + 1)
                    dve.wait_ge(s_rstd, b + 1)
                    for qt in range(QT):
                        ins = dve.tensor_scalar(y[p][:, qt], acc[p][:, qt], mv[:, qt, 0:1], rstd[:, qt:qt + 1],
                                                ALU.subtract, ALU.mult)
                    ins.then_inc(s_y, 1)

            def batch(t, p, before, last):
                b = 2 * t + p
                chain = Count(dve, s_dve, LINKS, (b + 1) * LINKS)
                for i in range(N):
                    dve.wait_ge(s_o, b * N + i + 1)
                    if i == 0:
                        dve.wait_ge(s_xb, b + 1)
                        if before == 2:
                            dve.wait_ge(s_y, b - 1)
                        ins = dve.tensor_tensor(acc[p][:], po[p][:], x[p][:], ALU.add)
                    else:
                        dve.wait_ge(s_acc, b * N + i)
                        for qt in range(QT):
                            ins = dve.scalar_tensor_tensor(
                                acc[p][:, qt], po[(p + i) % 2][:, qt], gate[p][:, qt, ORDER[i]:ORDER[i] + 1],
                                acc[p][:, qt], ALU.mult, ALU.add)
                    ins.then_inc(s_acc, 1)
                    if i in (0, 1, 8) and before > 0:
                        norm(t + p - 1, 1 - p, min(i, 2))
                    if i in (4, 5, 6, 7) and not last:
                        gating(t + p, 1 - p, chain, i - 4)
                if not last:
                    chain.end()

            chain = Count(dve, s_dve, LINKS, 0)
            for part in range(4):
                gating(0, 0, chain, part)
            chain.end()
            batch(0, 0, 0, False)
            batch(0, 1, 1, False)
            with dve.Fori(1, PASSES - 1) as t:
                batch(t, 0, 2, False)
                batch(t, 1, 2, False)
            batch(PASSES - 1, 0, 2, False)
            batch(PASSES - 1, 1, 2, True)
            for part in range(3):
                norm(PASSES - 1, 1, part)


def build(nc, dram, phases):
    with ExitStack() as ctx:
        rows = TableRows(nc, ctx, dram)
        layer0_attention(nc, dram, rows.share(0, GATHERED_FIRST))
        if phases < 2:
            return
        with ExitStack() as own:
            x2 = own.enter_context(nc.sbuf_tensor("x2_tok", [P, TT, D], F32))
            pos = own.enter_context(nc.sbuf_tensor("pos", [P, TT], I32))
            te = own.enter_context(nc.sbuf_tensor("tile_expert", [P, TILES], I32))
            wtop = own.enter_context(nc.sbuf_tensor("wtop", [P, TT], F32))
            moe_route(nc, dram, x2, pos[:], te[:], wtop[:], lambda pool: None)
            moe_experts(nc, dram, te[:], lambda pool: None)
            moe_combine(nc, dram, x2, pos[:], wtop[:], lambda pool: None)
        if phases < 3:
            return
        layer1_attention(nc, dram, rows.share(GATHERED_FIRST, GROUPS // 2))
        if phases < 4:
            return
        weights = ExpertWeights(nc, ctx, dram)
        with ExitStack() as own:
            aT = own.enter_context(nc.sbuf_tensor("aT", [P, 2, BH], F32))
            eT = own.enter_context(nc.sbuf_tensor("eT", [P, 2, BH], F32))
            qblk = own.enter_context(nc.sbuf_tensor("qblk", [P, KT, P, 32], F32))
            kh = own.enter_context(nc.sbuf_tensor("kh", [P, P, 2, BH], F32))
            mlstm_gates(nc, dram, aT, eT, lambda pool: None)
            for vt in range(QT):
                query_blocks(nc, dram, vt, qblk, lambda pool: None)
                hop_scores(nc, dram, vt, qblk, kh, lambda pool: weights.load(pool) if vt == 0 else None)
                mlstm_heads(nc, dram, vt, qblk, kh, aT, eT)
        if phases < 5:
            return
        experts_top2(nc, dram, weights)


def kernel(phases=9, **a):
    import concourse.bacc as _bacc
    from concourse.bass_utils import run_bass_kernel_spmd as _run

    a = {k: np.asarray(v) for k, v in a.items()}

    def kmajor(m):
        return m.reshape(KT, P, -1).transpose(1, 0, 2)

    def tokens_T(m):
        return m.transpose(0, 2, 1).reshape(B, KT, P, S).transpose(0, 2, 1, 3)

    arrays = {
        "x": a["x"], "xT": tokens_T(a["x"]), "cT": tokens_T(a["ctx_1024"]), "ctx": a["ctx_1024"],
        "w": np.stack([kmajor(m) for m in (
            a["L0_attn_Wq"].T, a["L0_attn_Wk"].T, a["L0_attn_Wv"].T, a["L0_attn_Wo"].T,
            a["L0_xattn_Wq"], a["L0_xattn_Wk"], a["L0_xattn_Wv"], a["L0_xattn_Wp"],
            a["L1_attn_Wq"].T, a["L1_attn_Wk"].T, a["L1_attn_Wv"].T)], axis=1),
        "cols": np.stack([m.reshape(2, P).T for m in (
            a["L0_xattn_bq"], a["L0_xattn_bk"], a["L1_attn_bq"], a["L1_attn_bk"])], axis=1),
        "rows": np.broadcast_to(np.stack([
            a["L0_xattn_bv"], a["L0_xattn_bp"], a["L1_attn_bv"], a["L1_xattn_ln_w"], a["L1_xattn_ln_b"],
            a["L1_ffn_bs2"]]), (P, 6, D)),
        "hopsT": hop_units(a["itok_SxS2_0_2016"]), "rpe": a["L1_xattn_rpe"],
        "wg": kmajor(a["L0_ffn_Wg"]), "before": np.triu(np.ones((P, P), np.float32), 1),
        "route": routing_constants(a["L0_ffn_bg"]),
        "w1": a["L0_ffn_W1"].reshape(NE, KT, P, HID).transpose(0, 2, 1, 3),
        "w2": a["L0_ffn_W2"].reshape(NE, HT, P, D).transpose(0, 2, 1, 3),
        "b1": a["L0_ffn_b1"].reshape(NE, HT, P).transpose(0, 2, 1), "b2": a["L0_ffn_b2"],
        "cols1": np.stack([m.reshape(2, P).T for m in (
            a["L1_attn_bq"], a["L1_attn_bk"], pair_swapped(a["L1_attn_bq"]), pair_swapped(a["L1_attn_bk"]),
            pair_signs())], axis=1),
        "rope": rope_tables(),
        "gw": np.concatenate([a["L1_xattn_igate_w"], a["L1_xattn_fgate_w"]]).T.reshape(6, P, 16).transpose(1, 0, 2),
        "gb": np.concatenate([a["L1_xattn_igate_b"], a["L1_xattn_fgate_b"]])[:, None],
        "ctx_ones": values_with_ones(a["ctx_1024"]),
        "gate1": padded(kmajor(a["L1_ffn_gate_W"]), 2), "rscale": np.broadcast_to(a["L1_ffn_route_scale"].reshape(1, 1), (P, 1)),
        "iota8m": np.broadcast_to((np.arange(NE) - NE).astype(np.float32), (P, QT, NE)),
        "f_w1": np.concatenate([a["L1_ffn_W1"], a["L1_ffn_Ws1"][None]]).reshape(NE + 1, KT, P, HID1)
        .transpose(2, 1, 0, 3),
        "f_w2": np.concatenate([a["L1_ffn_W2"], a["L1_ffn_Ws2"][None]]).transpose(1, 0, 2),
        "f_b1": np.concatenate([a["L1_ffn_b1"], a["L1_ffn_bs1"][None]]).T, "f_b2": padded(a["L1_ffn_b2"], 0),
        "masks8": head_masks(), "masks": window_masks(), "ident": np.eye(P, dtype=np.float32),
    }
    nc = _bacc.Bacc("TRN2", target_bir_lowering=False, num_devices=1)
    dram, given = {}, {}
    for name, m in arrays.items():
        m = np.ascontiguousarray(m)
        given["in_" + name] = m
        dram[name] = nc.dram_tensor("in_" + name, m.shape, mybir.dt.from_np(m.dtype), kind="ExternalInput").ap()
    dram["out"] = nc.dram_tensor("out", (B, S, D), F32, kind="ExternalOutput").ap()
    for name, shape in (("x2", (B, S, D)), ("x3", (B, S, D)), ("xs", (TILES * P, D)), ("ys", (TILES * P, D)),
                        ("x4", (B, S, D)), ("x4T", (B, P, KT, S)), ("gate_i", (B, 8, S)), ("gate_f", (B, 8, S)), ("x5", (B, S, D)),
                        ("runmax", (BH, S))):
        dram[name] = nc.dram_tensor(name, shape, F32, kind="Internal").ap()
    dram[{1: "x2", 2: "x3", 3: "x4", 4: "x5"}.get(phases, "nothing")] = dram["out"]
    dram["pos_rows"] = nc.dram_tensor("pos_rows", (GROUPS, P, GROUP * D), F32, kind="Internal").ap()
    build(nc, dram, phases)
    r = _run(nc, [given], core_ids=[0])
    return r.results[0]["out"]


def padded(m, axis):
    return np.pad(m, [(0, P - n if i == axis else 0) for i, n in enumerate(m.shape)])


def head_masks():
    head = np.arange(P)[:, None] // HD
    return ((head == np.arange(8)) / np.sqrt(HD)).astype(np.float32)


def window_masks():
    q, k = np.arange(P)[:, None], np.arange(P)[None, :]
    first = np.where((k <= q) & (k > q - WINDOW), 0.0, NEG)
    q, k = q + P, np.arange(64, 256)[None, :]
    second = np.where((k <= q) & (k > q - WINDOW), 0.0, NEG)
    return np.concatenate([first] * 4 + [second] * 2, axis=1).astype(np.float32)


def hop_units(hops):
    t = hops.T.reshape(2, P, S)
    late = t[:, :, P:].transpose(1, 2, 0).reshape(P, 2 * P)
    return np.concatenate([t[0, :, :P], late], axis=1)


def routing_constants(bg):
    row = np.concatenate([
        np.tile(np.arange(NE) - NE, TT), np.tile(bg, TT), np.tile(np.arange(TT) * P, NE),
        np.repeat(np.arange(TILES), NE)]).astype(np.float32)
    return np.broadcast_to(row, (P, row.size))


def pair_swapped(v):
    return v.reshape(-1, 2)[:, ::-1].reshape(-1)


def pair_signs():
    return np.tile(np.array([-1.0, 1.0], np.float32), D // 2)


def rope_tables():
    head = 128
    pos = np.arange(S, dtype=np.float32)
    inv = np.power(np.float32(10000.0), np.arange(0, head, 2, dtype=np.float32) / np.float32(head))
    rad = pos[:, None] / inv
    t = np.repeat(np.stack((np.sin(rad), np.cos(rad)), axis=-1).reshape(S, -1), 2, axis=-1)
    t = t.T.reshape(KT, P, S).transpose(1, 0, 2)
    return np.stack([t, t / np.float32(np.sqrt(head))], axis=1).astype(np.float32)


def values_with_ones(ctx):
    v = ctx.reshape(B, 2, P, H1, HW).transpose(0, 2, 1, 3, 4)
    return np.concatenate([v, np.ones(v.shape[:-1] + (1,), v.dtype)], axis=-1).reshape(B, P, 2, H1 * (HW + 1))
```
